# Optimizing a Trainium2 kernel written in Bass

```python
import numpy as np
import jax
import jax.numpy as jnp

def _softmax(x, axis=-1):
    return jax.nn.softmax(x, axis=axis)

def _gelu(x):
    return jax.nn.gelu(x, approximate=True)

def _silu(x):
    return jax.nn.silu(x)

def _sigmoid(x):
    return jax.nn.sigmoid(x)

def _layernorm(x, axis=-1, eps=1e-05):
    m = jnp.mean(x, axis=axis, keepdims=True)
    v = jnp.var(x, axis=axis, keepdims=True)
    return (x - m) / jnp.sqrt(v + eps)

def _scatter_add(tgt, idx, src, axis=0):
    return tgt.at[idx].add(src)

def _segment_sum(src, seg, n):
    return jax.ops.segment_sum(src, seg, n)
kernel_name = 'mk_gnn_ffn_d1_gnn_r8_9da367'

def setup_inputs(seed: int=0):
    np.random.seed(seed)
    _w = jnp.asarray

    def _rec_inputs():
        import jax
        import jax.numpy as jnp
        _gk = jax.random.key(seed)
        x = -0.0003713 + 1 * jax.random.normal(jax.random.fold_in(_gk, 1), (6250, 256), jnp.float32)
        _s = jax.random.randint(jax.random.fold_in(_gk, 2), (50000,), 0, 6250, jnp.int32)
        _d = jax.random.randint(jax.random.fold_in(_gk, 3), (50000,), 0, 6250, jnp.int32)
        _loop = jnp.arange(6250, dtype=jnp.int32)
        src = jnp.concatenate([_s, _d, _loop])
        dst = jnp.concatenate([_d, _s, _loop])
        _o = jnp.argsort(dst, stable=True)
        src = src[_o]
        dst = dst[_o]
        return (x, src, dst)
    x, src, dst = _rec_inputs()

    def _L0_gnn_setup():
        import jax, jax.numpy as jnp
        import numpy as np
        N, E = (6250, 200000)
        IN, HID = (256, 64)
        H0, H1 = (4, 4)
        NEG_SLOPE = 0.2

        def _gat_layer(h, W, al, ar, b, src, dst, n_nodes, n_heads, d, residual):
            feat = (h @ W).reshape(n_nodes, n_heads, d)
            el = jnp.einsum('nhd,hd->nh', feat, al)
            er = jnp.einsum('nhd,hd->nh', feat, ar)
            e = el[src] + er[dst]
            e = jnp.where(e > 0, e, NEG_SLOPE * e)
            emax = jax.ops.segment_max(e, dst, num_segments=n_nodes)
            ex = jnp.exp(e - emax[dst])
            denom = jax.ops.segment_sum(ex, dst, num_segments=n_nodes)
            alpha = ex / jnp.where(denom[dst] > 0, denom[dst], 1.0)
            msg = alpha[:, :, None] * feat[src]
            rst = jax.ops.segment_sum(msg, dst, num_segments=n_nodes)
            if residual:
                rst = rst + h.reshape(n_nodes, n_heads, d)
            rst = rst + b.reshape(1, n_heads, d)
            rst = jax.nn.elu(rst)
            return rst.reshape(n_nodes, n_heads * d)
        key = jax.random.key(seed)
        ks = jax.random.split(key, 12)
        s = 0.1
        return {'inputs': jax.random.normal(ks[0], (N, IN), dtype=jnp.float32), 'src': jax.random.randint(ks[1], (E,), 0, N, dtype=jnp.int32), 'dst': jax.random.randint(ks[2], (E,), 0, N, dtype=jnp.int32), 'W1': jax.random.normal(ks[3], (IN, H0 * HID), dtype=jnp.float32) * s, 'al1': jax.random.normal(ks[4], (H0, HID), dtype=jnp.float32) * s, 'ar1': jax.random.normal(ks[5], (H0, HID), dtype=jnp.float32) * s, 'b1': jnp.zeros((H0 * HID,), dtype=jnp.float32), 'W2': jax.random.normal(ks[6], (H0 * HID, H1 * HID), dtype=jnp.float32) * s, 'al2': jax.random.normal(ks[7], (H1, HID), dtype=jnp.float32) * s, 'ar2': jax.random.normal(ks[8], (H1, HID), dtype=jnp.float32) * s, 'b2': jnp.zeros((H1 * HID,), dtype=jnp.float32)}
    _L0_gnn_all = _L0_gnn_setup()
    _L0_gnn_in = {k: v for k, v in _L0_gnn_all.items() if k in ('W1', 'al1', 'ar1', 'b1', 'W2', 'al2', 'ar2', 'b2')}
    del _L0_gnn_all

    def _L0_ffn_setup():
        import jax, jax.numpy as jnp
        import numpy as np
        B, N, D = (16, 512, 256)
        NUM_EXPERTS, TOP_K, HEADS = (4, 2, 4)
        N_EDGES = 131072
        LN_EPS = 1e-05

        def _layernorm(x, g, b):
            mu = x.mean(-1, keepdims=True)
            var = ((x - mu) ** 2).mean(-1, keepdims=True)
            return (x - mu) * jax.lax.rsqrt(var + LN_EPS) * g + b

        def _forward(x, edge_index, W_gat, att_src, att_dst, b_gat, ln_gamma, ln_beta, W1, b1, W2, b2):
            Bc, Nc, Dc = x.shape
            M = Bc * Nc
            x_flat = x.reshape(M, Dc)
            h = (x_flat @ W_gat).reshape(M, HEADS, NUM_EXPERTS)
            loops = jnp.arange(M, dtype=edge_index.dtype)
            src = jnp.concatenate([edge_index[0], loops])
            dst = jnp.concatenate([edge_index[1], loops])
            a_src = (h * att_src).sum(-1)
            a_dst = (h * att_dst).sum(-1)
            e = jax.nn.leaky_relu(a_src[src] + a_dst[dst], negative_slope=0.2)
            e_max = jax.ops.segment_max(e, dst, num_segments=M)
            ee = jnp.exp(e - e_max[dst])
            denom = jax.ops.segment_sum(ee, dst, num_segments=M)
            alpha = ee / (denom[dst] + 1e-16)
            msg = h[src] * alpha[:, :, None]
            agg = jax.ops.segment_sum(msg, dst, num_segments=M).reshape(M, HEADS * NUM_EXPERTS) + b_gat
            scores = _layernorm(agg, ln_gamma, ln_beta).reshape(M, HEADS, NUM_EXPERTS).mean(1)
            scores = scores.reshape(Bc, Nc, NUM_EXPERTS)
            topk_s, topk_i = jax.lax.top_k(scores, TOP_K)
            w = jax.nn.softmax(topk_s, axis=-1)
            out = jnp.zeros_like(x)
            for ei in range(NUM_EXPERTS):
                g = jnp.where(topk_i == ei, w, 0.0).sum(-1)
                hh = jax.nn.gelu(x @ W1[ei] + b1[ei], approximate=False)
                out = out + g[..., None] * (hh @ W2[ei] + b2[ei])
            return out
        key = jax.random.key(seed)
        ks = jax.random.split(key, 8)
        s = 0.05
        return {'x': jax.random.normal(ks[0], (B, N, D), jnp.float32), 'W_gat': jax.random.normal(ks[1], (D, HEADS * NUM_EXPERTS), jnp.float32) * s, 'att_src': jax.random.normal(ks[2], (HEADS, NUM_EXPERTS), jnp.float32) * s, 'att_dst': jax.random.normal(ks[3], (HEADS, NUM_EXPERTS), jnp.float32) * s, 'b_gat': jnp.zeros((HEADS * NUM_EXPERTS,), jnp.float32), 'ln_gamma': jnp.ones((HEADS * NUM_EXPERTS,), jnp.float32), 'ln_beta': jnp.zeros((HEADS * NUM_EXPERTS,), jnp.float32), 'W1': jax.random.normal(ks[4], (NUM_EXPERTS, D, 2 * D), jnp.float32) * s, 'b1': jnp.zeros((NUM_EXPERTS, 2 * D), jnp.float32), 'W2': jax.random.normal(ks[5], (NUM_EXPERTS, 2 * D, D), jnp.float32) * s, 'b2': jnp.zeros((NUM_EXPERTS, D), jnp.float32), 'edge_index': jax.random.randint(ks[6], (2, N_EDGES), 0, B * N, jnp.int32)}
    _L0_ffn_all = _L0_ffn_setup()
    _L0_ffn_in = {k: v for k, v in _L0_ffn_all.items() if k in ('W_gat', 'att_src', 'att_dst', 'b_gat', 'ln_gamma', 'ln_beta', 'W1', 'b1', 'W2', 'b2', 'edge_index')}
    del _L0_ffn_all
    return {'x': x, 'src': src, 'dst': dst, 'L0_gnn_W1': _L0_gnn_in['W1'], 'L0_gnn_al1': _L0_gnn_in['al1'], 'L0_gnn_ar1': _L0_gnn_in['ar1'], 'L0_gnn_b1': _L0_gnn_in['b1'], 'L0_gnn_W2': _L0_gnn_in['W2'], 'L0_gnn_al2': _L0_gnn_in['al2'], 'L0_gnn_ar2': _L0_gnn_in['ar2'], 'L0_gnn_b2': _L0_gnn_in['b2'], 'L0_ffn_W_gat': _L0_ffn_in['W_gat'], 'L0_ffn_att_src': _L0_ffn_in['att_src'], 'L0_ffn_att_dst': _L0_ffn_in['att_dst'], 'L0_ffn_b_gat': _L0_ffn_in['b_gat'], 'L0_ffn_ln_gamma': _L0_ffn_in['ln_gamma'], 'L0_ffn_ln_beta': _L0_ffn_in['ln_beta'], 'L0_ffn_W1': _L0_ffn_in['W1'], 'L0_ffn_b1': _L0_ffn_in['b1'], 'L0_ffn_W2': _L0_ffn_in['W2'], 'L0_ffn_b2': _L0_ffn_in['b2'], 'L0_ffn_edge_index': _L0_ffn_in['edge_index']}

def reference(x, src, dst, L0_gnn_W1, L0_gnn_al1, L0_gnn_ar1, L0_gnn_b1, L0_gnn_W2, L0_gnn_al2, L0_gnn_ar2, L0_gnn_b2, L0_ffn_W_gat, L0_ffn_att_src, L0_ffn_att_dst, L0_ffn_b_gat, L0_ffn_ln_gamma, L0_ffn_ln_beta, L0_ffn_W1, L0_ffn_b1, L0_ffn_W2, L0_ffn_b2, L0_ffn_edge_index):
    import jax
    import jax.numpy as jnp

    def _L0_gnn_ref(inputs, src, dst, W1, al1, ar1, b1, W2, al2, ar2, b2):
        import jax, jax.numpy as jnp
        import numpy as np
        N, E = (6250, 200000)
        IN, HID = (256, 64)
        H0, H1 = (4, 4)
        NEG_SLOPE = 0.2

        def _gat_layer(h, W, al, ar, b, src, dst, n_nodes, n_heads, d, residual):
            feat = (h @ W).reshape(n_nodes, n_heads, d)
            el = jnp.einsum('nhd,hd->nh', feat, al)
            er = jnp.einsum('nhd,hd->nh', feat, ar)
            e = el[src] + er[dst]
            e = jnp.where(e > 0, e, NEG_SLOPE * e)
            emax = jax.ops.segment_max(e, dst, num_segments=n_nodes)
            ex = jnp.exp(e - emax[dst])
            denom = jax.ops.segment_sum(ex, dst, num_segments=n_nodes)
            alpha = ex / jnp.where(denom[dst] > 0, denom[dst], 1.0)
            msg = alpha[:, :, None] * feat[src]
            rst = jax.ops.segment_sum(msg, dst, num_segments=n_nodes)
            if residual:
                rst = rst + h.reshape(n_nodes, n_heads, d)
            rst = rst + b.reshape(1, n_heads, d)
            rst = jax.nn.elu(rst)
            return rst.reshape(n_nodes, n_heads * d)
        h = _gat_layer(inputs, W1, al1, ar1, b1, src, dst, N, H0, HID, residual=False)
        h = _gat_layer(h, W2, al2, ar2, b2, src, dst, N, H1, HID, residual=True)
        return h

    def _L0_ffn_ref(x, W_gat, att_src, att_dst, b_gat, ln_gamma, ln_beta, W1, b1, W2, b2, edge_index):
        import jax, jax.numpy as jnp
        import numpy as np
        B, N, D = (16, 512, 256)
        NUM_EXPERTS, TOP_K, HEADS = (4, 2, 4)
        N_EDGES = 131072
        LN_EPS = 1e-05

        def _layernorm(x, g, b):
            mu = x.mean(-1, keepdims=True)
            var = ((x - mu) ** 2).mean(-1, keepdims=True)
            return (x - mu) * jax.lax.rsqrt(var + LN_EPS) * g + b

        def _forward(x, edge_index, W_gat, att_src, att_dst, b_gat, ln_gamma, ln_beta, W1, b1, W2, b2):
            Bc, Nc, Dc = x.shape
            M = Bc * Nc
            x_flat = x.reshape(M, Dc)
            h = (x_flat @ W_gat).reshape(M, HEADS, NUM_EXPERTS)
            loops = jnp.arange(M, dtype=edge_index.dtype)
            src = jnp.concatenate([edge_index[0], loops])
            dst = jnp.concatenate([edge_index[1], loops])
            a_src = (h * att_src).sum(-1)
            a_dst = (h * att_dst).sum(-1)
            e = jax.nn.leaky_relu(a_src[src] + a_dst[dst], negative_slope=0.2)
            e_max = jax.ops.segment_max(e, dst, num_segments=M)
            ee = jnp.exp(e - e_max[dst])
            denom = jax.ops.segment_sum(ee, dst, num_segments=M)
            alpha = ee / (denom[dst] + 1e-16)
            msg = h[src] * alpha[:, :, None]
            agg = jax.ops.segment_sum(msg, dst, num_segments=M).reshape(M, HEADS * NUM_EXPERTS) + b_gat
            scores = _layernorm(agg, ln_gamma, ln_beta).reshape(M, HEADS, NUM_EXPERTS).mean(1)
            scores = scores.reshape(Bc, Nc, NUM_EXPERTS)
            topk_s, topk_i = jax.lax.top_k(scores, TOP_K)
            w = jax.nn.softmax(topk_s, axis=-1)
            out = jnp.zeros_like(x)
            for ei in range(NUM_EXPERTS):
                g = jnp.where(topk_i == ei, w, 0.0).sum(-1)
                hh = jax.nn.gelu(x @ W1[ei] + b1[ei], approximate=False)
                out = out + g[..., None] * (hh @ W2[ei] + b2[ei])
            return out
        return _forward(x, edge_index, W_gat, att_src, att_dst, b_gat, ln_gamma, ln_beta, W1, b1, W2, b2)
    x = x + _L0_gnn_ref(_layernorm(x, axis=-1), src, dst, L0_gnn_W1, L0_gnn_al1, L0_gnn_ar1, L0_gnn_b1, L0_gnn_W2, L0_gnn_al2, L0_gnn_ar2, L0_gnn_b2)
    x = x + _L0_ffn_ref(_layernorm(x, axis=-1)[None], L0_ffn_W_gat, L0_ffn_att_src, L0_ffn_att_dst, L0_ffn_b_gat, L0_ffn_ln_gamma, L0_ffn_ln_beta, L0_ffn_W1, L0_ffn_b1, L0_ffn_W2, L0_ffn_b2, L0_ffn_edge_index)[0]
    return x

_drawn_inputs = setup_inputs


def setup_inputs(seed=0):
    import zlib

    import numpy as np

    out = dict(_drawn_inputs(seed))
    spreads = {'L0_gnn_b1': (0.0, 0.1),
     'L0_gnn_b2': (0.0, 0.1),
     'L0_ffn_b_gat': (0.0, 0.1),
     'L0_ffn_ln_gamma': (1.0, 0.2),
     'L0_ffn_ln_beta': (0.0, 0.1),
     'L0_ffn_b1': (0.0, 0.1),
     'L0_ffn_b2': (0.0, 0.1)}
    factors = {'L0_ffn_att_dst': 3.041}
    for name, (base, spread) in spreads.items():
        noise = np.random.default_rng([zlib.crc32(name.encode()), seed]).standard_normal(out[name].shape)
        drawn = base * np.exp(spread * noise) if base else spread * noise
        out[name] = jnp.asarray(drawn.astype(out[name].dtype))
    for name, factor in factors.items():
        out[name] = (out[name] * factor).astype(out[name].dtype)
    return out
```

```python
import concourse.bass as bass
from concourse import mybir
from contextlib import ExitStack

FP = mybir.dt.float32
BF = mybir.dt.bfloat16
I32 = mybir.dt.int32
U32 = mybir.dt.uint32
ALU = mybir.AluOpType
ACT = mybir.ActivationFunctionType
X = mybir.AxisListType.X

P = 128
NODES = 6250
TILES = 50
PAIRS = TILES // 2
SLOTS = TILES * P
DUMMY = SLOTS
HEADS = 4
DIM = 256
CHUNKS = 8
GROUP = CHUNKS * P
E_GNN, E_FFN = 106250, 131072
GROUPS = {"gnn": 104, "ffn": 128}
ROUNDS = 4
STEPS = 4
STEP_COLS = 264
MAX_STEPS = P * STEP_COLS
FILL = 64
BIG_KEY = 8191
NONE = -1.0e30
EPS = 1e-5
EXPERTS, HID = 4, 512
FCH = HID // P


def width(d):
    return HEADS * (d + 1)


class Line:

    def __init__(self, eng, sem, spare):
        self.eng, self.sem, self.spare, self.at, self.k, self.per = eng, sem, spare, 0, None, 0

    def value(self):
        return self.at if self.k is None else self.k * self.per + self.at

    def __call__(self, ins):
        ins.then_inc(self.sem, 1)
        self.at += 1
        self.eng.wait_ge(self.sem, self.value())

    def hold(self, ins):
        self(ins)
        self.eng.sem_inc(self.spare, 1)

    def enter(self, k, per):
        assert self.k is None
        self.k, self.per, self.base = k, per, self.at

    def leave(self, trips):
        assert self.at - self.base == self.per, (self.at, self.base, self.per)
        self.k = None
        self.at = self.base + self.per * trips if trips is not None else None


def build(nc, t, out):
    ctx = ExitStack()
    with ctx:
        def sb(name, shape, dt=FP):
            return ctx.enter_context(nc.sbuf_tensor(name, shape, dt))

        def dram(name, shape, dt=FP):
            return nc.dram_tensor(name, shape, dt, kind="Internal").ap()

        sems = {}

        def S(name):
            if name not in sems:
                sems[name] = ctx.enter_context(nc.semaphore(name))
            return sems[name]

        tile_uses = {"index": (["proj1", "proj2", "fin2", "projf", "mix"], PAIRS), "x_in": (["proj1", "fin2", "projf"], 16 * PAIRS),
                     "x_free": (["proj1", "fin2", "projf"], PAIRS + 1), "out_ready": (["proj1", "proj2", "fin2", "projf", "mix"], PAIRS),
                     "out": (["proj1", "proj2", "fin2", "projf", "mix"], 16 * PAIRS),
                     "out_free": (["proj1", "proj2", "fin2", "projf", "mix"], PAIRS + 1),
                     "var": (["proj1", "projf"], PAIRS), "std": (["proj1", "projf"], PAIRS),
                     "neg": (["proj2", "fin2"], PAIRS), "exp": (["proj2", "fin2"], PAIRS),
                     "xn": (["proj1", "proj2", "projf"], PAIRS), "T": (["proj1", "proj2", "projf"], PAIRS),
                     "T_copied": (["proj1", "proj2", "projf"], PAIRS), "feat": (["proj1", "proj2", "projf"], PAIRS)}

        phase_of = {"gnn1": 0, "gnn2": 1, "ffn": 2}

        def bodies(eng, L):
            most = MAX_STEPS // STEPS - 1
            n = eng.value_load(counts[layers[L]["g"]][0:1, 0:1], min_val=1, max_val=most)
            if L == "gnn1":
                return 0, n
            if L == "gnn2":
                return n, n
            return eng.value_load(counts["gnn"][0:1, 0:1], min_val=1, max_val=most) * 2, n

        def tile_sem(kind, i):
            return S(f"tile_{kind}{i}")

        def tile_base(name, kind):
            names, each = tile_uses[kind]
            return names.index(name) * each

        half = GROUPS["gnn"] // 2
        list_adds = dict(dst_in=16, src_in=16, lo_ready=1, lo_out=16, keyT_ready=1, key_out=16, keyB_in=16, order_out=16 * TILES,
                         order_in=32, counts_ready=1, steps_out=16, row_in=16 * half, row_used=half, slot_out=16 * CHUNKS * half,
                         slot_free=half, slots_done=1, scattered=1, ranked=1, hist_done=1, hot_ready=2 * half, hot_used=half + 1,
                         key_ready=1, keyT=1, steps_ready=1, tb=1, base_ready=1, counted=1 + 2 * half * CHUNKS, loT=half,
                         same_ps=half, hot2_ready=4 * half, looked=half + 1, copied=2 * half * CHUNKS, placed=half)

        def list_base(g, kind):
            return 0 if g == "gnn" else list_adds[kind]

        def hold(eng, sem, value):
            eng.wait_ge(sem, value)
            eng.sem_inc(S("spare_" + eng_name[id(eng)]), 1)

        eng_name = {}

        G = ["gnn", "ffn"]
        lo_dram = {g: dram(f"{g}_lo", [GROUPS[g] * GROUP], BF) for g in G}
        key_dram = {g: dram(f"{g}_key", [SLOTS]) for g in G}
        order_dram = {g: dram(f"{g}_order", [SLOTS, 2], I32) for g in G}
        step_dram = {g: dram(f"{g}_step_tile", [MAX_STEPS], I32) for g in G}
        slot_dram = {g: dram(f"{g}_slots", [MAX_STEPS * ROUNDS * P, 1], I32) for g in G}
        table = {"gnn1": dram("table1", [SLOTS + 1, width(64) + 4]),
                 "gnn2": dram("table2", [SLOTS + 1, width(64) + 4]),
                 "ffn": dram("table3", [SLOTS + 1, width(4) + 4])}
        x2_dram = dram("x2", [SLOTS, DIM])

        big1 = sb("big1", [P, TILES * width(64)])
        big2 = sb("big2", [P, TILES * DIM])
        region = sb("region", [P, 12600])
        wpair = sb("wpair", [P, 2, 2, DIM])
        wgat = sb("wgat", [P, 2, 16])
        vecs = sb("vecs", [P, 6, DIM])
        small = sb("small", [P, 5, 16])
        b1cols = sb("b1cols", [P, EXPERTS * FCH])
        b2rows = sb("b2rows", [1, EXPERTS, DIM])
        ones_row = sb("ones_row", [1, P])
        iota_i = sb("iota_i", [P, P], I32)
        iota_f = sb("iota_f", [P, P])
        iota_b = sb("iota_b", [P, P], BF)
        part_i = sb("part_i", [P, 1], I32)
        part_f = sb("part_f", [P, 1])
        before = sb("before", [P, P])
        ident = sb("ident", [P, P])
        zero_b = sb("zero_b", [P, P], BF)
        nkey = sb("nkey", [P, TILES])
        nkey_i = sb("nkey_i", [P, TILES], I32)
        dummy = sb("dummy_index", [P, FILL * ROUNDS], I32)
        dummy_row = sb("dummy_row", [1, width(64) + 4])
        dummy_row_f = sb("dummy_row_f", [1, width(4) + 4])
        rank = sb("rank", [P, TILES])
        order = {g: sb(f"{g}_order_sb", [P, TILES, 2], I32) for g in G}
        counts = {g: sb(f"{g}_counts", [P, 2], I32) for g in G}
        er = sb("er", [P, TILES * HEADS])
        top = sb("top", [P, TILES * HEADS])
        sums_f = sb("sums_f", [P, TILES * width(4)])
        gates = sb("gates", [P, TILES * EXPERTS])
        ring_all = sb("ring", [P, STEPS * ROUNDS * (width(64) + 4)])
        ring_cols = ROUNDS * (width(64) + 4)
        ring = [ring_all[:, s * ring_cols:(s + 1) * ring_cols].rearrange("p (r w) -> p r w", r=ROUNDS) for s in range(STEPS)]
        junk = ring_all[:, 0:SLOTS // 2].bitcast(BF)
        prod = sb("prod", [P, ROUNDS, width(64)])
        part_sum = sb("part_sum", [P, width(64)])
        escore = [sb(f"escore{s}", [P, ROUNDS + 1, HEADS]) for s in range(STEPS)]
        eprob = [sb(f"eprob{s}", [P, ROUNDS + 1, HEADS]) for s in range(STEPS)]
        zbuf = sb("zbuf", [P, ROUNDS, HEADS])
        tmax = sb("tmax", [P, HEADS])
        idx = [sb(f"idx{h}", [P, 2 * ROUNDS], I32) for h in range(2)]
        tid = [sb(f"tid{h}", [1, 2], I32) for h in range(2)]
        xt, xn, tmp, tmp2 = ([ring_all[:, (2 * n + i) * DIM:(2 * n + i + 1) * DIM] for i in range(2)] for n in range(4))
        xnT = [ring_all[:, (8 + i) * DIM:(9 + i) * DIM].rearrange("p (k n) -> p k n", k=2) for i in range(2)]
        row = [sb(f"row{i}", [P, width(64) + 4]) for i in range(2)]
        row_f = [sb(f"row_f{i}", [P, width(4) + 4]) for i in range(2)]
        gi = [sb(f"gi{i}", [P, 1], I32) for i in range(2)]
        stats = [sb(f"stats{i}", [P, 6]) for i in range(2)]
        mv = [sb(f"mv{i}", [P, 2]) for i in range(2)]
        rstd = [sb(f"rstd{i}", [P, HEADS]) for i in range(2)]
        eps_col = sb("eps_col", [P, 1])

        at = [0]

        def carve(cols_fp, dt=FP):
            a = at[0]
            at[0] += cols_fp
            v = region[:, a:a + cols_fp]
            return v if dt == FP else v.bitcast(dt)
        MG = max(GROUPS.values()) * CHUNKS
        dst_i = carve(MG, I32)
        src_i = carve(MG, I32)
        off_f = carve(MG)
        hi_b = carve(MG // 2, BF)
        lo_b = carve(MG // 2, BF)
        tmp_i = carve(MG, I32)
        step_f = big2[:, 0:STEP_COLS]
        step_acc = big2[:, STEP_COLS:2 * STEP_COLS]
        step_i = big2[:, 2 * STEP_COLS:3 * STEP_COLS].bitcast(I32)
        lo_row = [carve(GROUP // 2, BF) for _ in range(2)]
        lo_T = [carve(GROUP) for _ in range(2)]
        one_lo = [carve(CHUNKS * P // 2, BF).rearrange("p (j c) -> p j c", c=P) for _ in range(2)]
        one_hi = [carve(CHUNKS * TILES // 2, BF).rearrange("p (j c) -> p j c", c=TILES) for _ in range(2)]
        same = [carve(GROUP // 2, BF).rearrange("p (j c) -> p j c", c=P) for _ in range(2)]
        count_sb = [carve(TILES) for _ in range(CHUNKS)]
        pick = carve(CHUNKS * TILES)
        found = carve(CHUNKS)
        ints = [carve(CHUNKS, I32) for _ in range(5)]
        slot_st = [carve(CHUNKS, I32) for _ in range(2)]
        src_st = [carve(CHUNKS, I32) for _ in range(2)]
        key = carve(TILES)
        neg_key = carve(TILES)
        deg = carve(TILES)
        rank_i = carve(TILES, I32)
        node_deg = carve(2 * TILES, I32).rearrange("p (t c) -> p t c", c=2)
        tile_f = carve(TILES)
        place_f = carve(TILES)
        base = carve(TILES)
        tb = carve(TILES + 1)
        keyT = carve(P)
        ordT = carve(2 * P, I32).rearrange("p (q c) -> p q c", c=2)
        maxdeg = carve(1)
        steps_i = carve(1, I32)
        steps_f = carve(1)
        steps_b = carve(P)
        total_i = carve(1, I32)
        assert at[0] <= 12600, at[0]
        keyB = big2[:, 0:SLOTS]
        spread = big2[:, 0:TILES * TILES].rearrange("p (n t) -> p n t", t=TILES)
        w1_sb = region[:, 0:EXPERTS * 2 * HID].rearrange("p (e k f) -> p e k f", e=EXPERTS, k=2)
        w2_sb = region[:, 4096:4096 + EXPERTS * FCH * DIM].rearrange("p (e f n) -> p e f n", e=EXPERTS, f=FCH)
        hT = [region[:, 8192 + i * FCH * 256:8192 + (i + 1) * FCH * 256].rearrange("p (f n) -> p f n", f=FCH)
              for i in range(2)]
        yout = [prod[:, i, 0:DIM] for i in range(2)]

        bank = [ctx.enter_context(nc.psum_tensor(f"bank{b}", [P, 512], FP)) for b in range(8)]
        run_ps = bank[0][:, 0:TILES]

        layers = {
            "gnn1": dict(g="gnn", d=64, sums=big1, ring=ring, row=row, al=vecs[:, 0, :], ar=vecs[:, 1, :]),
            "gnn2": dict(g="gnn", d=64, sums=big1, ring=ring, row=row, al=vecs[:, 3, :], ar=vecs[:, 4, :]),
            "ffn": dict(g="ffn", d=4, sums=sums_f, ring=[ring_all[:, s * ring_cols:s * ring_cols + ROUNDS * 24].rearrange("p (r w) -> p r w", r=ROUNDS) for s in range(STEPS)], row=row_f, al=small[:, 0, :], ar=small[:, 1, :]),
        }
        def tile_cols():
            return er[:, 0:TILES]

        block = ctx.enter_context(nc.Block())

        @block.sync
        def _(sp):
            eng_name[id(sp)] = "sp"
            cst = S("constants_loaded")
            for i, n in enumerate(["L0_gnn_al1", "L0_gnn_ar1", "L0_gnn_b1", "L0_gnn_al2", "L0_gnn_ar2", "L0_gnn_b2"]):
                sp.dma_start(vecs[:, i, :], t[n].partition_broadcast(P)).then_inc(cst, 16)
            for i, n in enumerate(["L0_ffn_att_src", "L0_ffn_att_dst", "L0_ffn_b_gat", "L0_ffn_ln_gamma", "L0_ffn_ln_beta"]):
                sp.dma_start(small[:, i, :], t[n].partition_broadcast(P)).then_inc(cst, 16)
            sp.dma_start(wpair[:, 0, :, :], t["L0_gnn_W1"].rearrange("(k p) n -> p k n", p=P)).then_inc(cst, 16)
            sp.dma_start(wpair[:, 1, :, :], t["L0_gnn_W2"].rearrange("(k p) n -> p k n", p=P)).then_inc(cst, 16)
            sp.dma_start(wgat[:, :, :], t["L0_ffn_W_gat"].rearrange("(k p) n -> p k n", p=P)).then_inc(cst, 16)
            sp.dma_start(b2rows[:, :, :], t["L0_ffn_b2"].rearrange("(o e) n -> o e n", o=1)).then_inc(cst, 16)
            with nc.allow_non_contiguous_dma(reason="a bias column per hidden chunk, 8 KB in all"):
                sp.dma_start(b1cols[:, :], t["L0_ffn_b1"].rearrange("e (f p) -> p (e f)", p=P)).then_inc(cst, 16)
            sp.wait_ge(S("consts"), 1)
            for n in ["gnn1", "gnn2"]:
                sp.dma_start(table[n][DUMMY:DUMMY + 1, :], dummy_row[:, :]).then_inc(S("dummies_out"), 16)
            sp.dma_start(table["ffn"][DUMMY:DUMMY + 1, :], dummy_row_f[:, :]).then_inc(S("dummies_out"), 16)

            def layout(g):
                ng = GROUPS[g]
                if g == "ffn":
                    sp.wait_ge(S("list_scattered"), list_base("gnn", "scattered") + 1)
                sp.dma_start(dst_i[:, 0:ng * CHUNKS].rearrange("p (g j) -> p g j", j=CHUNKS),
                             t[g + "_dst"].rearrange("(g p j) -> p g j", p=P, j=CHUNKS)).then_inc(S("list_dst_in"), 16)
                sp.dma_start(src_i[:, 0:ng * CHUNKS].rearrange("p (g j) -> p g j", j=CHUNKS),
                             t[g + "_src"].rearrange("(g p j) -> p g j", p=P, j=CHUNKS)).then_inc(S("list_src_in"), 16)
                sp.wait_ge(S("list_lo_ready"), list_base(g, "lo_ready") + 1)
                sp.dma_start(lo_dram[g].rearrange("(g p j) -> p g j", p=P, j=CHUNKS),
                             lo_b[:, 0:ng * CHUNKS].rearrange("p (g j) -> p g j", j=CHUNKS)).then_inc(S("list_lo_out"), 16)
                sp.wait_ge(S("list_lo_out"), list_base(g, "lo_out") + 16)
                sp.wait_ge(S("list_keyT_ready"), list_base(g, "keyT_ready") + 1)
                sp.dma_start(key_dram[g].rearrange("(t p) -> t p", p=P), keyT[0:TILES, :]).then_inc(S("list_key_out"), 16)
                sp.wait_ge(S("list_key_out"), list_base(g, "key_out") + 16)
                sp.dma_start(keyB, key_dram[g].partition_broadcast(P)).then_inc(S("list_keyB_in"), 16)
                sp.wait_ge(S("list_order_out"), list_base(g, "order_out") + 16 * TILES)
                with nc.allow_non_contiguous_dma(reason="6400 pairs"):
                    sp.dma_start(order[g][:, :, :], order_dram[g].rearrange("(t p) c -> p t c", p=P)).then_inc(S("list_order_in"), 16)
                sp.dma_start(ordT[0:TILES, :, :], order_dram[g].rearrange("(t p) c -> t p c", p=P)).then_inc(S("list_order_in"), 16)
                sp.wait_ge(S("list_counts_ready"), list_base(g, "counts_ready") + 1)
                fills = sp.value_load(counts[g][0:1, 1:2], min_val=2, max_val=MAX_STEPS // FILL)
                view = slot_dram[g].rearrange("(k p f) o -> k p (f o)", p=P, f=FILL * ROUNDS)
                with sp.Fori(0, fills) as k:
                    sp.dma_start(view[bass.ds(k, 1), :, :].rearrange("k p f -> (k p) f"), dummy[:, :]).then_inc(S(g + "_filled"), 16)
                sp.dma_start(step_dram[g].rearrange("(p f) -> p f", p=P), step_i).then_inc(S("list_steps_out"), 16)
                lows = lo_dram[g].rearrange("(g n) -> g n", n=GROUP)
                for i in range(2):
                    sp.dma_start(lo_row[i], lows[i:i + 1, :].to_broadcast([P, GROUP])).then_inc(S(f"list_row_in{i}"), 16)
                with sp.Fori(0, ng // 2 - 1) as k:
                    for i in range(2):
                        hold(sp, S(f"list_row_used{i}"), list_base(g, "row_used") + k + 1)
                        sp.dma_start(lo_row[i], lows[bass.ds(2 * k + (2 + i), 1), :].to_broadcast([P, GROUP])).then_inc(S(f"list_row_in{i}"), 16)
                    for i in range(2):
                        hold(sp, S(f"list_slot_out{i}"), list_base(g, "slot_out") + k * (16 * CHUNKS) + 16 * CHUNKS)
                        sp.sem_inc(S(f"list_slot_free{i}"), 1)

            def tiles_out(name):
                with sp.Fori(0, PAIRS) as k:
                    for i in range(2):
                        hold(sp, tile_sem("out", i), tile_base(name, "out") + k * 16 + 16)
                        sp.sem_inc(tile_sem("out_free", i), 1)

            def walk(L):
                c = layers[L]
                g = c["g"]
                sp.wait_ge(S("list_slots_done"), list_base(g, "slots_done") + 1)
                slots = slot_dram[g].rearrange("(s p r) o -> s p (r o)", p=P, r=2 * ROUNDS)
                tiles = step_dram[g].rearrange("(s c) -> s c", c=2)

                def load(h, s):
                    sp.dma_start(idx[h][:, :], slots[s, :, :].rearrange("s p r -> (s p) r")).then_inc(S(f"walk_idx_in{h}"), 16)
                    sp.dma_start(tid[h][:, :], tiles[s, :]).then_inc(S(f"walk_idx_in{h}"), 16)
                if L == "gnn2":
                    sp.wait_ge(S("gnn1_walked"), 1)
                for h in range(2):
                    load(h, slice(h, h + 1))
                done, n = bodies(sp, L)
                with sp.Fori(0, n) as k:
                    for h in range(2):
                        for s in (2 * h, 2 * h + 1):
                            hold(sp, S(f"walk_rows_in{s}"), (done + k) * (16 * ROUNDS) + 16 * ROUNDS)
                        hold(sp, S(f"walk_tid_read{h}"), done + k + 1)
                        load(h, bass.ds(2 * k + (2 + h), 1))
                for h in range(2):
                    hold(sp, S(f"walk_idx_in{h}"), (done + n) * 32 + 32 * (phase_of[L] + 1))
            layout("gnn")
            tiles_out("proj1")
            walk("gnn1")
            tiles_out("proj2")
            walk("gnn2")
            tiles_out("fin2")
            layout("ffn")
            tiles_out("projf")
            sp.wait_ge(S("list_scattered"), list_base("ffn", "scattered") + 1)
            sp.dma_start(w1_sb, t["L0_ffn_W1"].rearrange("e (k p) f -> p e k f", p=P)).then_inc(S("experts_in"), 16)
            sp.dma_start(w2_sb, t["L0_ffn_W2"].rearrange("e (f p) n -> p e f n", p=P)).then_inc(S("experts_in"), 16)
            walk("ffn")
            tiles_out("mix")

        @block.gpsimd
        def _(pool):
            eng_name[id(pool)] = "pool"
            line = Line(pool, S("pool_line"), S("spare_pool"))
            line(pool.iota(iota_i[:, :], [[1, P]], base=0, channel_multiplier=0))
            line(pool.iota(part_i[:, :], [[0, 1]], base=0, channel_multiplier=1))
            line(pool.iota(nkey_i[:, :], [[-P, TILES]], base=BIG_KEY, channel_multiplier=-1))
            line(pool.memset(dummy[:, :], DUMMY))
            pool.sem_inc(S("iotas"), 1)

            def gather(tile, tab, index, sem):
                pool.indirect_dma_start(tile, None, tab, bass.IndirectOffsetOnAxis(ap=index.bitcast(U32), axis=0)).then_inc(sem, 16)

            def scatter(tab, index, tile, sem, bound=None):
                kw = {} if bound is None else dict(bounds_check=bound, oob_is_err=False)
                pool.indirect_dma_start(tab, bass.IndirectOffsetOnAxis(ap=index.bitcast(U32), axis=0), tile, None, **kw).then_inc(sem, 16)

            def layout(g):
                pool.wait_ge(S("list_ranked"), list_base(g, "ranked") + 1)
                for n in range(TILES):
                    scatter(order_dram[g], rank_i[:, n:n + 1], node_deg[:, n, :], S("list_order_out"))
                pool.wait_ge(S("list_counts_ready"), list_base(g, "counts_ready") + 1)
                fills = pool.value_load(counts[g][0:1, 1:2], min_val=2, max_val=MAX_STEPS // FILL)
                hold(pool, S(g + "_filled"), fills * 16)
                with pool.Fori(0, GROUPS[g] // 2) as k:
                    for i in range(2):
                        hold(pool, S(f"list_placed{i}"), list_base(g, "placed") + k + 1)
                        for j in range(CHUNKS):
                            scatter(slot_dram[g], slot_st[i][:, j:j + 1], src_st[i][:, j:j + 1], S(f"list_slot_out{i}"),
                                    MAX_STEPS * ROUNDS * P - 1)
                for i in range(2):
                    pool.wait_ge(S(f"list_slot_out{i}"), list_base(g, "slot_out") + 16 * CHUNKS * GROUPS[g] // 2)
                pool.sem_inc(S("list_scattered"), 1)
                pool.wait_ge(S("list_steps_out"), list_base(g, "steps_out") + 16)
                pool.sem_inc(S("list_slots_done"), 1)

            def walk(L):
                c = layers[L]
                g = c["g"]
                done, n = bodies(pool, L)
                with pool.Fori(0, n) as k:
                    for s in range(STEPS):
                        if s % 2 == 0:
                            hold(pool, S(f"walk_idx_in{s // 2}"), (done + k) * 32 + 32 * (phase_of[L] + 1))
                        hold(pool, S(f"walk_rows_free{s}"), done + k + (phase_of[L] + 1))
                        for r in range(ROUNDS):
                            gather(c["ring"][s][:, r, :], table[L], idx[s // 2][:, (s % 2) * ROUNDS + r:(s % 2) * ROUNDS + r + 1],
                                   S(f"walk_rows_in{s}"))

            def tiles_loop(name, source, target, tiles_out, bound=None):
                with pool.Fori(0, PAIRS) as k:
                    for i in range(2):
                        hold(pool, tile_sem("index", i), tile_base(name, "index") + k + 1)
                        if source is not None:
                            hold(pool, tile_sem("x_free", i), tile_base(name, "x_free") + k + 1)
                            gather(xt[i][:, :], source, gi[i][:, :], tile_sem("x_in", i))
                    for i in range(2):
                        hold(pool, tile_sem("out_ready", i), tile_base(name, "out_ready") + k + 1)
                        scatter(target, gi[i][:, :], tiles_out[i][:, :] if not isinstance(tiles_out[i], bass.AP) else tiles_out[i],
                                tile_sem("out", i), bound)
                for i in range(2):
                    pool.wait_ge(tile_sem("out", i), tile_base(name, "out") + 16 * PAIRS)

            layout("gnn")
            pool.wait_ge(S("dummies_out"), 48)
            tiles_loop("proj1", t["x"], table["gnn1"], row)
            walk("gnn1")
            tiles_loop("proj2", None, table["gnn2"], row)
            walk("gnn2")
            tiles_loop("fin2", t["x"], x2_dram, tmp)
            layout("ffn")
            tiles_loop("projf", x2_dram, table["ffn"], row_f)
            walk("ffn")
            tiles_loop("mix", None, out, yout, NODES - 1)

        @block.scalar
        def _(act):
            eng_name[id(act)] = "act"

            def layout(g):
                act.wait_ge(S("list_keyB_in"), list_base(g, "keyB_in") + 16)
                act.wait_ge(S("list_key_ready"), list_base(g, "key_ready") + 1)
                act.drain()
                with act.Fori(0, GROUPS[g] // 2) as k:
                    for i in range(2):
                        for j in range(CHUNKS):
                            act.wait_ge(S("list_counted"), list_base(g, "counted") + (k * 2 + i) * CHUNKS + (j + 1))
                            act.activation(count_sb[j], run_ps, ACT.Copy).then_inc(S("list_copied"), 1)

            def walk(L):
                g = layers[L]["g"]
                done, n = bodies(act, L)
                with act.Fori(0, n) as k:
                    for s in range(STEPS):
                        act.wait_ge(S(f"walk_scores{s}"), done + k + 1)
                        act.activation(eprob[s][:, :, :], escore[s][:, :, :], ACT.Exp).then_inc(S(f"walk_probs{s}"), 1)

            def norm_and_copy(name, keep_x=False):
                with act.Fori(0, PAIRS) as k:
                    if name in ("proj1", "projf"):
                        for i in range(2):
                            act.wait_ge(tile_sem("var", i), tile_base(name, "var") + k + 1)
                            act.activation(rstd[i][:, 0:1], mv[i][:, 1:2], ACT.Sqrt, bias=eps_col[:, :]).then_inc(tile_sem("std", i), 1)
                    else:
                        for i in range(2):
                            act.wait_ge(tile_sem("neg", i), tile_base(name, "neg") + k + 1)
                            act.activation(tmp2[i][:, :], tmp2[i][:, :], ACT.Exp).then_inc(tile_sem("exp", i), 1)
                    for i in range(2 if name != "fin2" else 0):
                        hold(act, tile_sem("T", i), tile_base(name, "T") + k + 1)
                        act.activation(xnT[i][:, :, :], bank[i][:, 0:DIM].rearrange("p (k n) -> p k n", k=2), ACT.Copy).then_inc(tile_sem("T_copied", i), 1)
                        if name == "projf":
                            act.activation(big2[:, bass.ds(k * 512 + i * DIM, DIM)], bank[i][:, 0:DIM], ACT.Copy).then_inc(S("expert_in_kept"), 1)

            layout("gnn")
            norm_and_copy("proj1")
            walk("gnn1")
            norm_and_copy("proj2")
            walk("gnn2")
            norm_and_copy("fin2")
            layout("ffn")
            norm_and_copy("projf")
            walk("ffn")
            act.wait_ge(S("gat_var"), 1)
            act.activation(tile_cols(), tile_cols(), ACT.Sqrt, bias=eps_col[:, :]).then_inc(S("gat_std"), 1)
            act.wait_ge(S("gat_top"), 1)
            act.activation(gates[:, :], gates[:, :], ACT.Exp).then_inc(S("gat_exp"), 1)
            act.sem_inc(S("gelued"), 2 * FCH)
            with act.Fori(0, PAIRS) as k:
                for e in range(EXPERTS):
                    for f in range(FCH):
                        act.wait_ge(S("hidden"), (k * EXPERTS + e) * FCH + ((f | 1) + 1))
                        act.wait_ge(S("hidden_free"), k * EXPERTS + (e + 1)) if f == 0 else None
                        act.activation(hT[e % 2][:, f, :], bank[2 * (e % 2) + f // 2][:, (f % 2) * 256:(f % 2) * 256 + 256], ACT.Gelu,
                                       bias=b1cols[:, e * FCH + f:e * FCH + f + 1]).then_inc(S("gelued"), 1)

        @block.tensor
        def _(pe):
            eng_name[id(pe)] = "pe"
            pe.wait_ge(S("consts"), 1)

            def layout(g):
                ng = GROUPS[g]
                if g == "ffn":
                    pe.wait_ge(S("fin2_done"), 1)
                pe.matmul(run_ps, zero_b[:, :], zero_b[:, 0:TILES], start=True, stop=False, skip_group_check=True)
                with pe.Fori(0, ng // 2) as k:
                    for i in range(2):
                        pe.wait_ge(S(f"list_hot_ready{i}"), list_base(g, "hot_ready") + k * 2 + 2)
                        for j in range(CHUNKS):
                            m = pe.matmul(run_ps, one_lo[i][:, j, :], one_hi[i][:, j, :], start=False, stop=False, skip_group_check=True)
                        m.then_inc(S(f"list_hot_used{i}"), 1)
                m = pe.matmul(run_ps, zero_b[:, :], zero_b[:, 0:TILES], start=False, stop=True, skip_group_check=True)
                m.then_inc(S("list_hist_done"), 1)
                pe.wait_ge(S("list_key_ready"), list_base(g, "key_ready") + 1)
                pe.transpose(bank[1][0:TILES, 0:P], key, ident[:, :]).then_inc(S("list_keyT"), 1)
                pe.wait_ge(S("list_steps_ready"), list_base(g, "steps_ready") + 1)
                pe.matmul(bank[2][:, 0:TILES + 1], steps_b[0:TILES, :], before[0:TILES, 0:TILES + 1], start=True, stop=True).then_inc(S("list_tb"), 1)
                pe.wait_ge(S("list_base_ready"), list_base(g, "base_ready") + 1)
                pe.matmul(run_ps, ident[:, :], base, start=True, stop=False, skip_group_check=True).then_inc(S("list_counted"), 1)
                with pe.Fori(0, ng // 2) as k:
                    for i in range(2):
                        chunk = lo_T[i].rearrange("p (q j) -> p j q", j=CHUNKS)
                        pe.wait_ge(S(f"list_loT{i}"), list_base(g, "loT") + k + 1)
                        for j in range(CHUNKS):
                            m = pe.matmul(bank[3 + 2 * i + j // 4][:, (j % 4) * P:(j % 4 + 1) * P], chunk[:, j, :], chunk[:, j, :],
                                          start=True, stop=True)
                        m.then_inc(S(f"list_same_ps{i}"), 1)
                        pe.wait_ge(S(f"list_hot2_ready{i}"), list_base(g, "hot2_ready") + k * 4 + 4)
                        for j in range(CHUNKS):
                            c = (k * 2 + i) * CHUNKS + (j + 1)
                            pe.wait_ge(S("list_copied"), list_base(g, "copied") + c)
                            pe.matmul(run_ps, one_lo[i][:, j, :], one_hi[i][:, j, :], start=False, stop=False, skip_group_check=True).then_inc(S("list_counted"), 1)
                            look = bank[1 + i][:, j * TILES:(j + 1) * TILES]
                            pe.matmul(look, chunk[:, j, :], count_sb[j], start=True, stop=False, skip_group_check=True)
                            m = pe.matmul(look, same[i][:, j, :], one_hi[i][:, j, :], start=False, stop=True, skip_group_check=True)
                        m.then_inc(S(f"list_looked{i}"), 1)

            def project(name, w, cols):
                with pe.Fori(0, PAIRS) as k:
                    for i in range(2):
                        pe.wait_ge(tile_sem("xn", i), tile_base(name, "xn") + k + 1)
                        for h in range(2):
                            m = pe.transpose(bank[i][:, h * P:(h + 1) * P], xn[i][:, h * P:(h + 1) * P], ident[:, :])
                        m.then_inc(tile_sem("T", i), 1)
                    for i in range(2):
                        pe.wait_ge(tile_sem("T_copied", i), tile_base(name, "T_copied") + k + 1)
                        for h in range(2):
                            m = pe.matmul(bank[2 + i][:, 0:cols], xnT[i][:, h, :], w(h), start=(h == 0), stop=(h == 1))
                        m.then_inc(tile_sem("feat", i), 1)

            layout("gnn")
            pe.wait_ge(S("constants_loaded"), 16 * 16)
            project("proj1", lambda h: wpair[:, 0, h, :], DIM)
            project("proj2", lambda h: wpair[:, 1, h, :], DIM)
            layout("ffn")
            project("projf", lambda h: wgat[:, h, :], 16)
            pe.wait_ge(S("experts_in"), 32)
            pe.wait_ge(S("expert_in_kept"), TILES)
            inputs = big2[:, :].rearrange("p (t k n) -> p t k n", t=TILES, k=2)
            pe.wait_ge(S("gates_ready"), 1)
            with pe.Fori(0, PAIRS) as k:
                def up(e):
                    pe.wait_ge(S("gelued"), (k * EXPERTS + e) * FCH + FCH)
                    for f in range(FCH):
                        for h in range(2):
                            m = pe.matmul(bank[2 * (e % 2) + f // 2][:, (f % 2) * 256:(f % 2) * 256 + 256],
                                          w1_sb[:, e, h, f * P:(f + 1) * P], inputs[:, bass.ds(2 * k, 2), h, :],
                                          start=(h == 0), stop=(h == 1))
                        m.then_inc(S("hidden"), 1)

                def down(e):
                    pe.wait_ge(S("gelued"), (k * EXPERTS + e) * FCH + 3 * FCH)
                    pe.wait_ge(S("mixed_free"), (k * EXPERTS + e) * 2 + 2)
                    for i in range(2):
                        y = bank[4 + 2 * (e % 2) + i][:, 0:DIM]
                        for f in range(FCH):
                            pe.matmul(y, hT[e % 2][:, f, i * P:(i + 1) * P], w2_sb[:, e, f, :], start=(f == 0), stop=False)
                        pe.matmul(y, ones_row[:, :], b2rows[:, e, :], start=False, stop=True).then_inc(S("expert_out"), 1)
                    pe.sem_inc(S("spare_pe"), 1)
                up(0)
                for e in range(EXPERTS):
                    if e + 1 < EXPERTS:
                        up(e + 1)
                    down(e)

        @block.vector
        def _(dve):
            eng_name[id(dve)] = "dve"
            line = Line(dve, S("dve_line"), S("spare_dve"))
            V = nc.vector
            dve.wait_ge(S("iotas"), 1)
            line(V.tensor_copy(iota_f[:, :], iota_i[:, :]))
            line(V.tensor_copy(iota_b[:, :], iota_i[:, :]))
            line(V.tensor_copy(part_f[:, :], part_i[:, :]))
            line(V.tensor_copy(nkey[:, :], nkey_i[:, :]))
            line(V.tensor_scalar(before[:, :], iota_f[:, :], part_f[:, :], None, ALU.is_gt))
            line(V.tensor_scalar(ident[:, :], iota_f[:, :], part_f[:, :], None, ALU.is_equal))
            line(V.memset(zero_b[:, :], 0.0))
            line(V.memset(eps_col[:, :], EPS))
            line(V.memset(ones_row[:, :], 1.0))
            for r, w in ((dummy_row, width(64)), (dummy_row_f, width(4))):
                line(V.memset(r[:, 0:w], 0.0))
                line(V.memset(r[:, w:w + 4], NONE))
            for i in range(2):
                line(V.memset(row[i][:, :], 1.0))
                line(V.memset(row_f[i][:, :], 1.0))
            dve.sem_inc(S("consts"), 1)

            def one_hots(g, i, k, dst_lo, dst_hi, sem):
                c = bass.ds((2 * k + i) * CHUNKS, CHUNKS)
                V.tensor_tensor(dst_lo[i], iota_b[:, :].unsqueeze(1).to_broadcast([P, CHUNKS, P]),
                                lo_b[:, c].unsqueeze(2).to_broadcast([P, CHUNKS, P]), ALU.is_equal).then_inc(sem, 1)
                V.tensor_tensor(dst_hi[i], iota_b[:, 0:TILES].unsqueeze(1).to_broadcast([P, CHUNKS, TILES]),
                                hi_b[:, c].unsqueeze(2).to_broadcast([P, CHUNKS, TILES]), ALU.is_equal).then_inc(sem, 1)

            def layout(g):
                ng = GROUPS[g]
                n = ng * CHUNKS
                last = NODES - 1
                dve.wait_ge(S("list_dst_in"), list_base(g, "dst_in") + 16)
                dve.wait_ge(S("list_src_in"), list_base(g, "src_in") + 16)
                line(V.tensor_scalar(src_i[:, 0:n], src_i[:, 0:n], float(last), None, ALU.min))
                line(V.tensor_scalar(tmp_i[:, 0:n], dst_i[:, 0:n], 127, None, ALU.bitwise_and))
                line(V.tensor_copy(lo_b[:, 0:n], tmp_i[:, 0:n]))
                dve.sem_inc(S("list_lo_ready"), 1)
                line(V.tensor_scalar(off_f[:, 0:n], dst_i[:, 0:n], float(NODES), None, ALU.is_ge))
                line(V.tensor_scalar(tmp_i[:, 0:n], dst_i[:, 0:n], 7, None, ALU.logical_shift_right))
                line(V.scalar_tensor_tensor(hi_b[:, 0:n], off_f[:, 0:n], 64.0, tmp_i[:, 0:n], ALU.mult, ALU.add))
                line(V.tensor_scalar(off_f[:, 0:n], off_f[:, 0:n], float(2 ** 18), 8192.0, ALU.mult, ALU.add))
                for i in range(2):
                    dve.sem_inc(S(f"list_hot_used{i}"), 1)
                with dve.Fori(0, ng // 2) as k:
                    for i in range(2):
                        dve.wait_ge(S(f"list_hot_used{i}"), list_base(g, "hot_used") + k + 1)
                        one_hots(g, i, k, one_lo, one_hi, S(f"list_hot_ready{i}"))
                dve.wait_ge(S("list_hist_done"), list_base(g, "hist_done") + 1)
                line(V.tensor_copy(deg, run_ps))
                line(V.tensor_scalar(key, deg, 2047.0, 8192.0, ALU.min, ALU.mult))
                line(V.tensor_tensor(key, key, nkey[:, :], ALU.add))
                dve.sem_inc(S("list_key_ready"), 1)
                dve.wait_ge(S("list_keyT"), list_base(g, "keyT") + 1)
                line(V.tensor_copy(keyT[0:TILES, :], bank[1][0:TILES, 0:P]))
                dve.sem_inc(S("list_keyT_ready"), 1)
                dve.wait_ge(S("list_keyB_in"), list_base(g, "keyB_in") + 16)
                for n_ in range(TILES):
                    line(V.tensor_scalar(junk, keyB, key[:, n_:n_ + 1], None, ALU.is_gt, ALU.add, accum_out=rank[:, n_:n_ + 1]))
                line(V.tensor_copy(rank_i, rank[:, :]))
                line(V.tensor_scalar(tmp_i[:, 0:TILES], nkey[:, :], -1.0, float(BIG_KEY), ALU.mult, ALU.add))
                line(V.tensor_copy(node_deg[:, :, 0], tmp_i[:, 0:TILES]))
                line(V.tensor_copy(node_deg[:, :, 1], deg))
                dve.sem_inc(S("list_ranked"), 1)
                dve.wait_ge(S("list_order_in"), list_base(g, "order_in") + 32)
                line(V.tensor_reduce(maxdeg[0:TILES, :], ordT[0:TILES, :, 1], X, ALU.max))
                line(V.tensor_scalar(steps_f[0:TILES, :], maxdeg[0:TILES, :], float(ROUNDS - 1), None, ALU.add))
                line(V.tensor_copy(steps_i[0:TILES, :], steps_f[0:TILES, :]))
                line(V.tensor_scalar(steps_i[0:TILES, :], steps_i[0:TILES, :], 2, None, ALU.logical_shift_right))
                line(V.tensor_copy(steps_f[0:TILES, :], steps_i[0:TILES, :]))
                line(V.tensor_copy(steps_b[0:TILES, :], steps_f[0:TILES, :].to_broadcast([TILES, P])))
                dve.sem_inc(S("list_steps_ready"), 1)
                dve.wait_ge(S("list_tb"), list_base(g, "tb") + 1)
                line(V.tensor_copy(tb, bank[2][:, 0:TILES + 1]))
                line(V.tensor_copy(total_i, tb[:, TILES:TILES + 1]))
                line(V.tensor_scalar(tmp_i[:, 0:1], total_i, 2, None, ALU.logical_shift_right))
                line(V.tensor_scalar(counts[g][:, 0:1], tmp_i[:, 0:1], 1.0, None, ALU.add))
                line(V.tensor_scalar(tmp_i[:, 0:1], total_i, 6, None, ALU.logical_shift_right))
                line(V.tensor_scalar(counts[g][:, 1:2], tmp_i[:, 0:1], 2.0, None, ALU.add))
                line(V.memset(step_acc, 0.0))
                line(V.tensor_scalar(step_f, iota_f[:, 0:1].to_broadcast([P, STEP_COLS]), 0.0, None, ALU.mult))
                line(V.tensor_scalar(step_f[:, 0:P], iota_f[:, :], 0.0, None, ALU.add))
                line(V.tensor_scalar(step_f[:, P:2 * P], iota_f[:, :], float(P), None, ALU.add))
                line(V.tensor_scalar(step_f[:, 2 * P:STEP_COLS], iota_f[:, 0:STEP_COLS - 2 * P], float(2 * P), None, ALU.add))
                line(V.tensor_scalar(steps_f, part_f[:, :], float(STEP_COLS), None, ALU.mult))
                line(V.tensor_scalar(step_f, step_f, steps_f, None, ALU.add))
                for n_ in range(1, TILES):
                    line(V.scalar_tensor_tensor(step_acc, step_f, tb[:, n_:n_ + 1], step_acc, ALU.is_ge, ALU.add))
                line(V.tensor_copy(step_i, step_acc))
                dve.sem_inc(S("list_counts_ready"), 1)
                line(V.tensor_scalar(tmp_i[:, 0:TILES], rank_i, 7, None, ALU.logical_shift_right))
                line(V.tensor_copy(tile_f, tmp_i[:, 0:TILES]))
                line(V.tensor_scalar(tmp_i[:, 0:TILES], rank_i, 127, None, ALU.bitwise_and))
                line(V.tensor_copy(place_f, tmp_i[:, 0:TILES]))
                dve.wait_ge(S("list_steps_out"), list_base(g, "steps_out") + 16)
                line(V.tensor_tensor(spread, tile_f.unsqueeze(2).to_broadcast([P, TILES, TILES]),
                                     iota_f[:, 0:TILES].unsqueeze(1).to_broadcast([P, TILES, TILES]), ALU.is_equal))
                line(V.tensor_tensor(spread, spread, tb[:, 0:TILES].unsqueeze(1).to_broadcast([P, TILES, TILES]), ALU.mult))
                line(V.tensor_reduce(base, spread, X, ALU.add))
                line(V.tensor_scalar(base, base, float(ROUNDS), -65536.0, ALU.mult, ALU.add))
                line(V.scalar_tensor_tensor(base, place_f, 1.0 / P, base, ALU.mult, ALU.add))
                dve.sem_inc(S("list_base_ready"), 1)
                for i in range(2):
                    dve.sem_inc(S(f"list_looked{i}"), 1)
                    dve.sem_inc(S(f"list_slot_free{i}"), 1)
                with dve.Fori(0, ng // 2) as k:
                    line.enter(k, 2 * 11)
                    for i in range(2):
                        c = bass.ds((2 * k + i) * CHUNKS, CHUNKS)
                        dve.wait_ge(S(f"list_looked{i}"), list_base(g, "looked") + k + 1)
                        dve.wait_ge(S(f"list_row_in{i}"), list_base(g, "row_in") + k * 16 + 16)
                        V.tensor_scalar(lo_T[i], lo_row[i], part_f[:, :], None, ALU.is_equal).then_inc(S(f"list_loT{i}"), 1)
                        one_hots(g, i, k, one_lo, one_hi, S(f"list_hot2_ready{i}"))
                        dve.wait_ge(S(f"list_loT{i}"), list_base(g, "loT") + k + 1)
                        dve.sem_inc(S(f"list_row_used{i}"), 1)
                        dve.wait_ge(S(f"list_same_ps{i}"), list_base(g, "same_ps") + k + 1)
                        for h in range(2):
                            V.tensor_tensor(same[i][:, 4 * h:4 * h + 4, :], bank[3 + 2 * i + h][:, :].rearrange("p (j c) -> p j c", c=P),
                                            before[:, :].unsqueeze(1).to_broadcast([P, 4, P]), ALU.mult).then_inc(S(f"list_hot2_ready{i}"), 1)
                    for i in range(2):
                        c = bass.ds((2 * k + i) * CHUNKS, CHUNKS)
                        dve.wait_ge(S(f"list_hot2_ready{i}"), list_base(g, "hot2_ready") + k * 4 + 4)
                        dve.wait_ge(S(f"list_looked{i}"), list_base(g, "looked") + k + 2)
                        line(V.tensor_tensor(pick.rearrange("p (j c) -> p j c", j=CHUNKS), bank[1 + i][:, 0:CHUNKS * TILES].rearrange("p (j c) -> p j c", j=CHUNKS),
                                             one_hi[i], ALU.mult))
                        line(V.tensor_reduce(found, pick.rearrange("p (j c) -> p j c", j=CHUNKS), X, ALU.add))
                        line(V.tensor_scalar(ints[0], found, float(P), None, ALU.mult))
                        line(V.tensor_scalar(ints[1], ints[0], 127, 3, ALU.bitwise_and, ALU.logical_shift_left))
                        line(V.tensor_scalar(ints[2], ints[0], 7, 7, ALU.arith_shift_right, ALU.bitwise_and))
                        line(V.tensor_scalar(ints[3], ints[0], 10, None, ALU.arith_shift_right))
                        line(V.tensor_tensor(ints[4], ints[3], off_f[:, c], ALU.add))
                        line(V.tensor_scalar(ints[3], ints[4], 10, None, ALU.logical_shift_left))
                        line(V.tensor_tensor(ints[1], ints[1], ints[2], ALU.bitwise_or))
                        dve.wait_ge(S(f"list_slot_free{i}"), list_base(g, "slot_free") + k + 1)
                        line(V.tensor_tensor(slot_st[i], ints[3], ints[1], ALU.bitwise_or))
                        line.hold(V.tensor_tensor(src_st[i], src_i[:, c], src_i[:, c], ALU.max))
                        dve.sem_inc(S(f"list_placed{i}"), 1)
                    line.leave(ng // 2)

            def walk(L):
                nonlocal line
                c = layers[L]
                g, d, sums, rg = c["g"], c["d"], c["sums"], c["ring"]
                w = width(d)
                for s in range(STEPS):
                    dve.sem_inc(S(f"walk_rows_free{s}"), 1)
                done, n = bodies(dve, L)
                mine = Line(dve, S(L + "_line"), S("spare_dve"))
                with dve.Fori(0, n) as k:
                    mine.enter(k, 11 * STEPS)
                    tiles = {}

                    def score(s):
                        if s % 2 == 0:
                            hold(dve, S(f"walk_idx_in{s // 2}"), (done + k) * 32 + 32 * (phase_of[L] + 1))
                            for q in range(2):
                                tiles[s + q] = dve.value_load(tid[s // 2][0:1, q:q + 1], min_val=0, max_val=TILES - 1)
                            dve.sem_inc(S(f"walk_tid_read{s // 2}"), 1)
                        tl = tiles[s]
                        hc = bass.ds(tl * HEADS, HEADS)
                        dve.wait_ge(S(f"walk_rows_in{s}"), (done + k) * (16 * ROUNDS) + 16 * ROUNDS)
                        mine(V.tensor_tensor(zbuf[:, :, :], rg[s][:, :, w:w + 4], er[:, hc].unsqueeze(1).to_broadcast([P, ROUNDS, HEADS]), ALU.add))
                        mine(V.scalar_tensor_tensor(zbuf[:, :, :], zbuf[:, :, :], 0.2, zbuf[:, :, :], ALU.mult, ALU.max))
                        mine(V.tensor_reduce(tmax[:, :], zbuf[:, :, :].rearrange("p r h -> p h r"), X, ALU.max))
                        mine(V.tensor_tensor(tmax[:, :], tmax[:, :], top[:, hc], ALU.max))
                        mine(V.tensor_tensor(escore[s][:, 0:ROUNDS, :], zbuf[:, :, :], tmax[:, :].unsqueeze(1).to_broadcast([P, ROUNDS, HEADS]), ALU.subtract))
                        mine(V.tensor_tensor(escore[s][:, ROUNDS, :], top[:, hc], tmax[:, :], ALU.subtract))
                        dve.sem_inc(S(f"walk_scores{s}"), 1)
                        mine(V.tensor_tensor(top[:, hc], tmax[:, :], tmax[:, :], ALU.max))

                    def add(s):
                        tl = tiles[s]
                        dve.wait_ge(S(f"walk_probs{s}"), done + k + 1)
                        pr = prod[:, :, 0:w].rearrange("p r (h d) -> p r h d", h=HEADS)
                        mine.hold(V.tensor_tensor(pr, rg[s][:, :, 0:w].rearrange("p r (h d) -> p r h d", h=HEADS),
                                                  eprob[s][:, 0:ROUNDS, :].unsqueeze(3).to_broadcast([P, ROUNDS, HEADS, d + 1]), ALU.mult))
                        dve.sem_inc(S(f"walk_rows_free{s}"), 1)
                        mine(V.tensor_reduce(part_sum[:, 0:w], prod[:, :, 0:w].rearrange("p r w -> p w r"), X, ALU.add))
                        mysum = sums[:, bass.ds(tl * w, w)]
                        mine(V.tensor_tensor(mysum.rearrange("p (h d) -> p h d", h=HEADS), mysum.rearrange("p (h d) -> p h d", h=HEADS),
                                             eprob[s][:, ROUNDS, :].unsqueeze(2).to_broadcast([P, HEADS, d + 1]), ALU.mult))
                        mine(V.tensor_tensor(mysum, mysum, part_sum[:, 0:w], ALU.add))

                    score(0)
                    for s in range(STEPS):
                        if s + 1 < STEPS:
                            score(s + 1)
                        add(s)
                    mine.leave(None)

            def index(name, g, k, i):
                hold(dve, tile_sem("out_free", i), tile_base(name, "out_free") + k + 1)
                line.hold(V.tensor_copy(gi[i][:, :], order[g][:, bass.ds(2 * k + i, 1), 0]))
                dve.sem_inc(tile_sem("index", i), 1)

            def norm(name, k, src):
                for i in range(2):
                    dve.wait_ge(tile_sem("x_in", i), tile_base(name, "x_in") + k * 16 + 16)
                    line.hold(V.bn_stats(stats[i][:, :], src[i][:, :]))
                    line.hold(V.bn_aggr(mv[i][:, :], stats[i][:, :]))
                    dve.sem_inc(tile_sem("var", i), 1)
                for i in range(2):
                    dve.wait_ge(tile_sem("std", i), tile_base(name, "std") + k + 1)
                    line(V.reciprocal(rstd[i][:, 1:2], rstd[i][:, 0:1]))
                    line(V.tensor_scalar(xn[i][:, :], src[i][:, :], mv[i][:, 0:1], rstd[i][:, 1:2], ALU.subtract, ALU.mult))
                    dve.sem_inc(tile_sem("xn", i), 1)
                    if name == "proj1":
                        dve.sem_inc(tile_sem("x_free", i), 1)

            def rows(name, L, k):
                c = layers[L]
                d = c["d"]
                w = width(d)
                n = HEADS * d
                for i in range(2):
                    dve.wait_ge(tile_sem("feat", i), tile_base(name, "feat") + k + 1)
                    f = bank[2 + i][:, 0:n]
                    line(V.tensor_copy(c["row"][i][:, 0:w].rearrange("p (h d) -> p h d", h=HEADS)[:, :, 0:d], f.rearrange("p (h d) -> p h d", h=HEADS)))
                    line(V.tensor_tensor(tmp[i][:, 0:n], f, c["al"], ALU.mult))
                    line(V.tensor_reduce(c["row"][i][:, w:w + 4], tmp[i][:, 0:n].rearrange("p (h d) -> p h d", h=HEADS), X, ALU.add))
                    line(V.tensor_tensor(tmp[i][:, 0:n], f, c["ar"], ALU.mult))
                    line.hold(V.tensor_reduce(rstd[i][:, :], tmp[i][:, 0:n].rearrange("p (h d) -> p h d", h=HEADS), X, ALU.add))
                    hc = bass.ds((2 * k + i) * HEADS, HEADS)
                    line(V.tensor_tensor(er[:, hc], rstd[i][:, :], rstd[i][:, :], ALU.max))
                    if name == "projf":
                        line(V.tensor_tensor(zbuf[:, i, :], c["row"][i][:, w:w + 4], rstd[i][:, :], ALU.add))
                        line(V.scalar_tensor_tensor(top[:, hc], zbuf[:, i, :], 0.2, zbuf[:, i, :], ALU.mult, ALU.max))
                        sc = sums_f[:, bass.ds((2 * k + i) * w, w)]
                        line(V.tensor_tensor(sc, c["row"][i][:, 0:w], c["row"][i][:, 0:w], ALU.max))
                    dve.sem_inc(tile_sem("out_ready", i), 1)

            def aggregate(name, k, bias, residual):
                for i in range(2):
                    w = width(64)
                    sv = big1[:, bass.ds((2 * k + i) * w, w)].rearrange("p (h d) -> p h d", h=HEADS)
                    hd = xn[i][:, :].rearrange("p (h d) -> p h d", h=HEADS)
                    line(V.scalar_tensor_tensor(rstd[i][:, :].unsqueeze(2), sv[:, :, 64:65], 0.0, sv[:, :, 64:65], ALU.is_le, ALU.add))
                    line(V.reciprocal(rstd[i][:, :], rstd[i][:, :]))
                    line(V.tensor_tensor(hd, sv[:, :, 0:64], rstd[i][:, :].unsqueeze(2).to_broadcast([P, HEADS, 64]), ALU.mult))
                    if residual:
                        line(V.tensor_tensor(xn[i][:, :], xn[i][:, :], big2[:, bass.ds((2 * k + i) * DIM, DIM)], ALU.add))
                    line(V.tensor_tensor(xn[i][:, :], xn[i][:, :], bias, ALU.add))
                    line(V.tensor_scalar(tmp2[i][:, :], xn[i][:, :], 0.0, None, ALU.min))
                    dve.sem_inc(tile_sem("neg", i), 1)
                    line(V.tensor_scalar(xn[i][:, :], xn[i][:, :], 0.0, None, ALU.max))
                for i in range(2):
                    dve.wait_ge(tile_sem("exp", i), tile_base(name, "exp") + k + 1)
                    line(V.scalar_tensor_tensor(xn[i][:, :], tmp2[i][:, :], -1.0, xn[i][:, :], ALU.add, ALU.add))

            def credits(name, free=True):
                for i in range(2):
                    dve.sem_inc(tile_sem("out_free", i), 1)
                    if free:
                        dve.sem_inc(tile_sem("x_free", i), 1)

            layout("gnn")
            dve.wait_ge(S("constants_loaded"), 16 * 16)
            credits("proj1")
            with dve.Fori(0, PAIRS) as k:
                line.enter(k, 22)
                for i in range(2):
                    index("proj1", "gnn", k, i)
                norm("proj1", k, xt)
                rows("proj1", "gnn1", k)
                line.leave(PAIRS)
            line(V.memset(big1[:, :], 0.0))
            line(V.memset(top[:, :], NONE))
            walk("gnn1")
            dve.sem_inc(S("gnn1_walked"), 1)
            credits("proj2", False)
            with dve.Fori(0, PAIRS) as k:
                line.enter(k, 30)
                for i in range(2):
                    index("proj2", "gnn", k, i)
                aggregate("proj2", k, vecs[:, 2, :], False)
                for i in range(2):
                    line.hold(V.tensor_tensor(big2[:, bass.ds((2 * k + i) * DIM, DIM)], xn[i][:, :], xn[i][:, :], ALU.max))
                    dve.sem_inc(tile_sem("xn", i), 1)
                rows("proj2", "gnn2", k)
                line.leave(PAIRS)
            line(V.memset(big1[:, :], 0.0))
            line(V.memset(top[:, :], NONE))
            walk("gnn2")
            credits("fin2")
            with dve.Fori(0, PAIRS) as k:
                line.enter(k, 20)
                for i in range(2):
                    index("fin2", "gnn", k, i)
                aggregate("fin2", k, vecs[:, 5, :], True)
                for i in range(2):
                    dve.wait_ge(tile_sem("x_in", i), tile_base("fin2", "x_in") + k * 16 + 16)
                    line.hold(V.tensor_tensor(tmp[i][:, :], xt[i][:, :], xn[i][:, :], ALU.add))
                    dve.sem_inc(tile_sem("x_free", i), 1)
                    dve.sem_inc(tile_sem("out_ready", i), 1)
                line.leave(PAIRS)
            for i in range(2):
                dve.wait_ge(tile_sem("out", i), tile_base("fin2", "out") + 16 * PAIRS)
            dve.sem_inc(S("fin2_done"), 1)
            layout("ffn")
            credits("projf")
            with dve.Fori(0, PAIRS) as k:
                line.enter(k, 30)
                for i in range(2):
                    index("projf", "ffn", k, i)
                norm("projf", k, xt)
                for i in range(2):
                    line.hold(V.tensor_tensor(big1[:, bass.ds((2 * k + i) * DIM, DIM)], xt[i][:, :], xt[i][:, :], ALU.max))
                    dve.sem_inc(tile_sem("x_free", i), 1)
                rows("projf", "ffn", k)
                line.leave(PAIRS)
            walk("ffn")
            sf = sums_f[:, :].rearrange("p (t h d) -> p t h d", t=TILES, h=HEADS)
            n16 = TILES * 16
            reg = ring_all[:, 0:SLOTS // 2]
            agg = reg[:, 0:n16]
            agg4 = agg.rearrange("p (t h e) -> p t h e", t=TILES, h=HEADS)
            agg3 = agg.rearrange("p (t c) -> p t c", t=TILES)
            sq = reg[:, n16:2 * n16]
            sq3 = sq.rearrange("p (t c) -> p t c", t=TILES)
            den = reg[:, 2 * n16:2 * n16 + TILES * HEADS].rearrange("p (t h) -> p t h", t=TILES)
            mean = reg[:, 2 * n16 + 200:2 * n16 + 250]
            std = tile_cols()
            sc = reg[:, 2 * n16 + 256:2 * n16 + 456]
            sc3 = sc.rearrange("p (t e) -> p t e", t=TILES)
            cmp_ = reg[:, n16:2 * n16].rearrange("p (t e j) -> p t e j", t=TILES, e=EXPERTS)
            g3 = gates[:, :].rearrange("p (t e) -> p t e", t=TILES)

            def cols(v):
                return v.unsqueeze(2).to_broadcast([P, TILES, 16])
            line(V.tensor_scalar(den.unsqueeze(3), sf[:, :, :, 4:5], 1e-16, None, ALU.add))
            line(V.reciprocal(den, den))
            for h in range(HEADS):
                line(V.tensor_tensor(agg4[:, :, h, :], sf[:, :, h, 0:4], den[:, :, h:h + 1].to_broadcast([P, TILES, 4]), ALU.mult))
            line(V.tensor_tensor(agg3, agg3, small[:, 2, :].unsqueeze(1).to_broadcast([P, TILES, 16]), ALU.add))
            line(V.tensor_reduce(mean, agg3, X, ALU.add))
            line(V.tensor_scalar(mean, mean, 1.0 / 16, None, ALU.mult))
            line(V.tensor_tensor(agg3, agg3, cols(mean), ALU.subtract))
            line(V.tensor_tensor(sq, agg, agg, ALU.mult))
            line(V.tensor_reduce(std, sq3, X, ALU.add))
            line(V.tensor_scalar(std, std, 1.0 / 16, None, ALU.mult))
            dve.sem_inc(S("gat_var"), 1)
            dve.wait_ge(S("gat_std"), 1)
            line(V.reciprocal(std, std))
            line(V.tensor_tensor(agg3, agg3, cols(std), ALU.mult))
            line(V.tensor_tensor(agg3, agg3, small[:, 3, :].unsqueeze(1).to_broadcast([P, TILES, 16]), ALU.mult))
            line(V.tensor_tensor(agg3, agg3, small[:, 4, :].unsqueeze(1).to_broadcast([P, TILES, 16]), ALU.add))
            line(V.tensor_reduce(sc3, agg4.rearrange("p t h e -> p t e h"), X, ALU.add))
            line(V.tensor_scalar(sc, sc, 0.25, None, ALU.mult))
            take = reg[:, 2 * n16 + 456:2 * n16 + 656].rearrange("p (t e) -> p t e", t=TILES)
            eq = reg[:, 0:n16].rearrange("p (t e j) -> p t e j", t=TILES, e=EXPERTS)
            for e in range(EXPERTS):
                line(V.tensor_tensor(cmp_[:, :, e, :], sc3, sc3[:, :, e:e + 1].to_broadcast([P, TILES, EXPERTS]), ALU.is_gt))
                if e:
                    line(V.tensor_tensor(eq[:, :, e, 0:e], sc3[:, :, 0:e], sc3[:, :, e:e + 1].to_broadcast([P, TILES, e]), ALU.is_equal))
                    line(V.tensor_tensor(cmp_[:, :, e, 0:e], cmp_[:, :, e, 0:e], eq[:, :, e, 0:e], ALU.add))
            line(V.tensor_reduce(take, cmp_, X, ALU.add))
            line(V.tensor_scalar(take, take, 2.0, None, ALU.is_lt))
            line(V.tensor_reduce(mean, sc3, X, ALU.max))
            line(V.tensor_tensor(g3, sc3, mean.unsqueeze(2).to_broadcast([P, TILES, EXPERTS]), ALU.subtract))
            dve.sem_inc(S("gat_top"), 1)
            dve.wait_ge(S("gat_exp"), 1)
            line(V.tensor_tensor(g3, g3, take, ALU.mult))
            line(V.tensor_reduce(mean, g3, X, ALU.add))
            line(V.reciprocal(mean, mean))
            line(V.tensor_tensor(g3, g3, mean.unsqueeze(2).to_broadcast([P, TILES, EXPERTS]), ALU.mult))
            dve.sem_inc(S("gates_ready"), 1)
            for i in range(2):
                dve.sem_inc(S("hidden_free"), 1)
            for _ in range(4):
                dve.sem_inc(S("mixed_free"), 1)
            credits("mix", False)
            with dve.Fori(0, PAIRS) as k:
                line.enter(k, 2 + 2 * EXPERTS)
                for i in range(2):
                    index("mix", "ffn", k, i)
                for e in range(EXPERTS):
                    for i in range(2):
                        dve.wait_ge(S("expert_out"), (k * EXPERTS + e) * 2 + (i + 1))
                        prev = big1[:, bass.ds((2 * k + i) * DIM, DIM)] if e == 0 else yout[i]
                        line.hold(V.scalar_tensor_tensor(yout[i], bank[4 + 2 * (e % 2) + i][:, 0:DIM], gates[:, bass.ds((2 * k + i) * EXPERTS + e, 1)],
                                                         prev, ALU.mult, ALU.add))
                        dve.sem_inc(S("mixed_free"), 1)
                    dve.sem_inc(S("hidden_free"), 1)
                for i in range(2):
                    dve.sem_inc(tile_sem("out_ready", i), 1)
                line.leave(PAIRS)


NAMES = ["x", "gnn_src", "gnn_dst", "ffn_src", "ffn_dst", "L0_gnn_W1", "L0_gnn_al1", "L0_gnn_ar1", "L0_gnn_b1",
         "L0_gnn_W2", "L0_gnn_al2", "L0_gnn_ar2", "L0_gnn_b2", "L0_ffn_W_gat", "L0_ffn_att_src", "L0_ffn_att_dst",
         "L0_ffn_b_gat", "L0_ffn_ln_gamma", "L0_ffn_ln_beta", "L0_ffn_W1", "L0_ffn_b1", "L0_ffn_W2", "L0_ffn_b2"]


def kernel(**inputs):
    import numpy as np
    import concourse.bacc as bacc
    from concourse import mybir as mb
    from concourse.bass_utils import run_bass_kernel_spmd

    def padded(a, n, fill):
        a = np.asarray(a)
        return np.concatenate([a, np.full((n - a.shape[0],) + a.shape[1:], fill, a.dtype)])

    a = {k: np.asarray(v) for k, v in inputs.items()}
    edges = a.pop("L0_ffn_edge_index")
    a["x"] = padded(a["x"], SLOTS, 0)
    a["gnn_src"] = padded(a.pop("src"), GROUPS["gnn"] * GROUP, 0)
    a["gnn_dst"] = padded(a.pop("dst"), GROUPS["gnn"] * GROUP, BIG_KEY)
    a["ffn_src"], a["ffn_dst"] = edges[0], edges[1]
    for n in ("L0_gnn_al1", "L0_gnn_ar1", "L0_gnn_al2", "L0_gnn_ar2", "L0_ffn_att_src", "L0_ffn_att_dst"):
        a[n] = a[n].reshape(-1)

    nc = bacc.Bacc("TRN2", target_bir_lowering=False, num_devices=1)
    arrays, aps = {}, {}
    for n in NAMES:
        v = np.ascontiguousarray(a[n])
        arrays[f"in_{n}"] = v
        aps[n] = nc.dram_tensor(f"in_{n}", v.shape, mb.dt.from_np(v.dtype), kind="ExternalInput").ap()
    out = nc.dram_tensor("result", (NODES, DIM), mb.dt.float32, kind="ExternalOutput").ap()
    build(nc, aps, out)
    r = run_bass_kernel_spmd(nc, [arrays], core_ids=[0])
    return r.results[0]["result"]
```

```python
import concourse.bass as bass
from concourse import mybir
from contextlib import ExitStack

FP = mybir.dt.float32
BF = mybir.dt.bfloat16
I32 = mybir.dt.int32
U32 = mybir.dt.uint32
ALU = mybir.AluOpType
ACT = mybir.ActivationFunctionType
X = mybir.AxisListType.X

P = 128
NODES = 6250
TILES = 50
PAIRS = TILES // 2
SLOTS = TILES * P
DUMMY = SLOTS
HEADS = 4
DIM = 256
CHUNKS = 8
GROUP = CHUNKS * P
E_GNN, E_FFN = 106250, 131072
GROUPS = {"gnn": 104, "ffn": 128}
ROUNDS = 4
STEPS = 4
STEP_COLS = 264
MAX_STEPS = P * STEP_COLS
FILL = 64
BIG_KEY = 8191
NONE = -1.0e30
EPS = 1e-5
EXPERTS, HID = 4, 512
FCH = HID // P


def width(d):
    return HEADS * (d + 1)


class Line:

    def __init__(self, eng, sem, spare):
        self.eng, self.sem, self.spare, self.at, self.k, self.per = eng, sem, spare, 0, None, 0

    def put(self, ins):
        ins.then_inc(self.sem, 1)
        self.at += 1
        return self.at

    def need(self, mark):
        self.eng.wait_ge(self.sem, mark if self.k is None else self.k * self.per + mark)

    def __call__(self, ins):
        self.need(self.put(ins))

    def hold(self, ins):
        self(ins)
        self.eng.sem_inc(self.spare, 1)

    def enter(self, k, per):
        assert self.k is None
        self.k, self.per, self.base = k, per, self.at

    def leave(self, trips):
        assert self.at - self.base == self.per, (self.at, self.base, self.per)
        self.k = None
        self.at = self.base + self.per * trips if trips is not None else None

    def settle(self):
        self.need(self.at)


def build(nc, t, out):
    ctx = ExitStack()
    with ctx:
        def sb(name, shape, dt=FP):
            return ctx.enter_context(nc.sbuf_tensor(name, shape, dt))

        def dram(name, shape, dt=FP):
            return nc.dram_tensor(name, shape, dt, kind="Internal").ap()

        sems = {}

        def S(name):
            if name not in sems:
                sems[name] = ctx.enter_context(nc.semaphore(name))
            return sems[name]

        tile_uses = {"index": (["proj1", "proj2", "fin2", "projf", "mix"], PAIRS), "x_in": (["proj1", "fin2", "projf"], 16 * PAIRS + 16),
                     "index_in": (["proj1", "fin2", "projf"], PAIRS + 1),
                     "x_free": (["proj1", "fin2", "projf"], PAIRS), "out_ready": (["proj1", "proj2", "fin2", "projf", "mix"], PAIRS),
                     "out": (["proj1", "proj2", "fin2", "projf", "mix"], 16 * PAIRS),
                     "out_free": (["proj1", "proj2", "fin2", "projf", "mix"], PAIRS + 1),
                     "var": (["proj1", "projf"], PAIRS), "std": (["proj1", "projf"], PAIRS),
                     "neg": (["proj2", "fin2"], PAIRS), "exp": (["proj2", "fin2"], PAIRS),
                     "xn": (["proj1", "proj2", "projf"], PAIRS), "T": (["proj1", "proj2", "projf"], PAIRS),
                     "T_copied": (["proj1", "proj2", "projf"], PAIRS), "feat": (["proj1", "proj2", "projf"], PAIRS)}

        phase_of = {"gnn1": 0, "gnn2": 1, "ffn": 2}

        def bodies(eng, L):
            most = MAX_STEPS // STEPS - 1
            n = eng.value_load(counts[layers[L]["g"]][0:1, 0:1], min_val=1, max_val=most)
            if L == "gnn1":
                return 0, n
            if L == "gnn2":
                return n, n
            return eng.value_load(counts["gnn"][0:1, 0:1], min_val=1, max_val=most) * 2, n

        def tile_sem(kind, i):
            return S(f"tile_{kind}{i}")

        def tile_base(name, kind):
            names, each = tile_uses[kind]
            return names.index(name) * each

        half = GROUPS["gnn"] // 2
        list_adds = dict(dst_in=16, src_in=16, lo_ready=1, lo_out=16, keyT_ready=1, key_out=16, keyB_in=16, order_out=16 * TILES,
                         order_in=16, counts_ready=1, steps_out=16, row_in=16 * half, row_used=half, slot_out=16 * CHUNKS * half,
                         slot_free=half, slots_done=1, scattered=1, ranked=1, hist_done=1, hot_ready=2 * half, hot_used=half + 1,
                         key_ready=1, keyT=1, steps_ready=1, tb=1, base_ready=1, counted=1 + 2 * half * CHUNKS, loT=half,
                         same_ps=half, hot2_ready=4 * half, looked=half + 1, copied=2 * half * CHUNKS, act_ranked=1, step_tiles=1, maxT=1, maxT_ps=1, placed=half)

        def list_base(g, kind):
            return 0 if g == "gnn" else list_adds[kind]

        def hold(eng, sem, value):
            eng.wait_ge(sem, value)
            eng.sem_inc(S("spare_" + eng_name[id(eng)]), 1)

        eng_name = {}

        G = ["gnn", "ffn"]
        lo_dram = {g: dram(f"{g}_lo", [GROUPS[g] * GROUP], BF) for g in G}
        key_dram = {g: dram(f"{g}_key", [SLOTS]) for g in G}
        order_dram = {g: dram(f"{g}_order", [SLOTS, 1], I32) for g in G}
        step_dram = {g: dram(f"{g}_step_tile", [MAX_STEPS], I32) for g in G}
        slot_dram = {g: dram(f"{g}_slots", [MAX_STEPS * ROUNDS * P, 1], I32) for g in G}
        table = {"gnn1": dram("table1", [SLOTS + 1, width(64) + 4]),
                 "gnn2": dram("table2", [SLOTS + 1, width(64) + 4]),
                 "ffn": dram("table3", [SLOTS + 1, width(4) + 4])}
        y_dram = dram("expert_outputs", [TILES, P, EXPERTS * DIM])
        x2_dram = dram("x2", [SLOTS, DIM])

        big1 = sb("big1", [P, TILES * width(64)])
        big2 = sb("big2", [P, TILES * DIM])
        region = sb("region", [P, 12600])
        wpair = sb("wpair", [P, 2, 2, DIM])
        wgat = sb("wgat", [P, 2, 16])
        vecs = sb("vecs", [P, 6, DIM])
        small = sb("small", [P, 5, 16])
        b1cols = sb("b1cols", [P, EXPERTS * FCH])
        b2rows = sb("b2rows", [1, EXPERTS, DIM])
        ones_row = sb("ones_row", [1, P])
        iota_i = sb("iota_i", [P, P], I32)
        iota_f = sb("iota_f", [P, P])
        iota_b = sb("iota_b", [P, P], BF)
        part_i = sb("part_i", [P, 1], I32)
        part_f = sb("part_f", [P, 1])
        before = sb("before", [P, P])
        ident = sb("ident", [P, P])
        zero_b = sb("zero_b", [P, P], BF)
        nkey = sb("nkey", [P, TILES])
        nkey_i = sb("nkey_i", [P, TILES], I32)
        dummy = sb("dummy_index", [P, FILL * ROUNDS], I32)
        dummy_row = sb("dummy_row", [1, width(64) + 4])
        dummy_row_f = sb("dummy_row_f", [1, width(4) + 4])
        rank = sb("rank", [P, TILES])
        order = {g: sb(f"{g}_order_sb", [P, TILES + 2], I32) for g in G}
        counts = {g: sb(f"{g}_counts", [P, 2], I32) for g in G}
        er = sb("er", [P, TILES * HEADS])
        top = sb("top", [P, TILES * HEADS])
        sums_f = sb("sums_f", [P, TILES * width(4)])
        gates = sb("gates", [P, TILES * EXPERTS])
        ring_all = sb("ring", [P, STEPS * ROUNDS * (width(64) + 4)])
        ring_cols = ROUNDS * (width(64) + 4)
        ring = [ring_all[:, s * ring_cols:(s + 1) * ring_cols].rearrange("p (r w) -> p r w", r=ROUNDS) for s in range(STEPS)]
        junk = ring_all[:, 0:SLOTS // 2].bitcast(BF)
        DVE_RANKS = 22
        prod_all = sb("prod", [P, 2, ROUNDS, width(64)])
        prod = [prod_all[:, i, :, :] for i in range(2)]
        part_sum = sb("part_sum", [P, width(64)])
        escore = [sb(f"escore{s}", [P, ROUNDS + 1, HEADS]) for s in range(STEPS)]
        eprob = [sb(f"eprob{s}", [P, ROUNDS + 1, HEADS]) for s in range(STEPS)]
        zbuf = sb("zbuf", [P, ROUNDS, HEADS])
        tmax = sb("tmax", [P, HEADS])
        idx = [sb(f"idx{h}", [P, 2 * ROUNDS], I32) for h in range(2)]
        tid = [sb(f"tid{h}", [1, 2], I32) for h in range(2)]
        xt, xn, tmp, tmp2 = ([ring_all[:, (2 * n + i) * DIM:(2 * n + i + 1) * DIM] for i in range(2)] for n in range(4))
        xnT = [ring_all[:, (8 + i) * DIM:(9 + i) * DIM].rearrange("p (k n) -> p k n", k=2) for i in range(2)]
        row = [sb(f"row{i}", [P, width(64) + 4]) for i in range(2)]
        row_f = [sb(f"row_f{i}", [P, width(4) + 4]) for i in range(2)]
        gi = [sb(f"gi{i}", [P, 1], I32) for i in range(2)]
        gi_in = [sb(f"gi_in{i}", [P, 1], I32) for i in range(2)]
        stats = [sb(f"stats{i}", [P, 6]) for i in range(2)]
        mv = [sb(f"mv{i}", [P, 2]) for i in range(2)]
        rstd = [sb(f"rstd{i}", [P, HEADS]) for i in range(2)]
        eps_col = sb("eps_col", [P, 1])

        at = [0]

        def carve(cols_fp, dt=FP):
            a = at[0]
            at[0] += cols_fp
            v = region[:, a:a + cols_fp]
            return v if dt == FP else v.bitcast(dt)
        MG = max(GROUPS.values()) * CHUNKS
        dst_i = carve(MG, I32)
        src_i = carve(MG, I32)
        off_f = carve(MG)
        hi_b = carve(MG // 2, BF)
        lo_b = carve(MG // 2, BF)
        tmp_i = carve(MG, I32)
        step_f = big2[:, 0:STEP_COLS]
        step_acc = big2[:, STEP_COLS:2 * STEP_COLS]
        step_i = big2[:, 2 * STEP_COLS:3 * STEP_COLS].bitcast(I32)
        junk_act = region[:, at[0]:at[0] + SLOTS // 2].bitcast(BF)
        lo_row = [carve(GROUP // 2, BF) for _ in range(2)]
        lo_T = [carve(GROUP) for _ in range(2)]
        one_lo = [carve(CHUNKS * P // 2, BF).rearrange("p (j c) -> p j c", c=P) for _ in range(2)]
        one_hi = [carve(CHUNKS * TILES // 2, BF).rearrange("p (j c) -> p j c", c=TILES) for _ in range(2)]
        same = [carve(GROUP // 2, BF).rearrange("p (j c) -> p j c", c=P) for _ in range(2)]
        count_sb = [carve(TILES) for _ in range(CHUNKS)]
        pick = carve(CHUNKS * TILES)
        found = carve(CHUNKS)
        ints = [carve(CHUNKS, I32) for _ in range(5)]
        slot_st = [carve(CHUNKS, I32) for _ in range(2)]
        src_st = [carve(CHUNKS, I32) for _ in range(2)]
        key = carve(TILES)
        neg_key = carve(TILES)
        deg = carve(TILES)
        rank_i = carve(TILES, I32)
        node_no = carve(TILES, I32)
        tile_f = carve(TILES)
        place_f = carve(TILES)
        base = carve(TILES)
        tb = carve(TILES + 1)
        keyT = carve(P)
        maxdeg = carve(1)
        steps_i = carve(1, I32)
        steps_f = carve(1)
        steps_b = carve(P)
        total_i = carve(1, I32)
        assert at[0] <= 12600, at[0]
        keyB = big2[:, 0:SLOTS]
        spread, in_tile = (big2[:, SLOTS + n * TILES * TILES:SLOTS + (n + 1) * TILES * TILES].rearrange("p (n t) -> p n t", t=TILES)
                           for n in range(2))
        w1_sb = region[:, 0:EXPERTS * 2 * HID].rearrange("p (e k f) -> p e k f", e=EXPERTS, k=2)
        w2_sb = region[:, 4096:4096 + EXPERTS * FCH * DIM].rearrange("p (e f n) -> p e f n", e=EXPERTS, f=FCH)
        hT = [region[:, 8192 + i * HID:8192 + (i + 1) * HID].rearrange("p (f n) -> p f n", f=FCH) for i in range(2)]
        y_keep = region[:, 9216:9216 + EXPERTS * DIM]
        y_back = [region[:, i * EXPERTS * DIM:(i + 1) * EXPERTS * DIM] for i in range(2)]
        yout = [prod_all[:, i, 0, 0:DIM] for i in range(2)]

        bank = [ctx.enter_context(nc.psum_tensor(f"bank{b}", [P, 512], FP)) for b in range(8)]
        run_ps = bank[0][:, 0:TILES]

        layers = {
            "gnn1": dict(g="gnn", d=64, sums=big1, ring=ring, row=row, al=vecs[:, 0, :], ar=vecs[:, 1, :]),
            "gnn2": dict(g="gnn", d=64, sums=big1, ring=ring, row=row, al=vecs[:, 3, :], ar=vecs[:, 4, :]),
            "ffn": dict(g="ffn", d=4, sums=sums_f, ring=[ring_all[:, s * ring_cols:s * ring_cols + ROUNDS * 24].rearrange("p (r w) -> p r w", r=ROUNDS) for s in range(STEPS)], row=row_f, al=small[:, 0, :], ar=small[:, 1, :]),
        }
        def tile_cols():
            return er[:, 0:TILES]

        block = ctx.enter_context(nc.Block())

        @block.sync
        def _(sp):
            eng_name[id(sp)] = "sp"
            cst = S("constants_loaded")
            for i, n in enumerate(["L0_gnn_al1", "L0_gnn_ar1", "L0_gnn_b1", "L0_gnn_al2", "L0_gnn_ar2", "L0_gnn_b2"]):
                sp.dma_start(vecs[:, i, :], t[n].partition_broadcast(P)).then_inc(cst, 16)
            for i, n in enumerate(["L0_ffn_att_src", "L0_ffn_att_dst", "L0_ffn_b_gat", "L0_ffn_ln_gamma", "L0_ffn_ln_beta"]):
                sp.dma_start(small[:, i, :], t[n].partition_broadcast(P)).then_inc(cst, 16)
            sp.dma_start(wpair[:, 0, :, :], t["L0_gnn_W1"].rearrange("(k p) n -> p k n", p=P)).then_inc(cst, 16)
            sp.dma_start(wpair[:, 1, :, :], t["L0_gnn_W2"].rearrange("(k p) n -> p k n", p=P)).then_inc(cst, 16)
            sp.dma_start(wgat[:, :, :], t["L0_ffn_W_gat"].rearrange("(k p) n -> p k n", p=P)).then_inc(cst, 16)
            sp.dma_start(b2rows[:, :, :], t["L0_ffn_b2"].rearrange("(o e) n -> o e n", o=1)).then_inc(cst, 16)
            with nc.allow_non_contiguous_dma(reason="a bias column per hidden chunk, 8 KB in all"):
                sp.dma_start(b1cols[:, :], t["L0_ffn_b1"].rearrange("e (f p) -> p (e f)", p=P)).then_inc(cst, 16)
            sp.wait_ge(S("consts"), 1)
            for n in ["gnn1", "gnn2"]:
                sp.dma_start(table[n][DUMMY:DUMMY + 1, :], dummy_row[:, :]).then_inc(S("dummies_out"), 16)
            sp.dma_start(table["ffn"][DUMMY:DUMMY + 1, :], dummy_row_f[:, :]).then_inc(S("dummies_out"), 16)

            def layout(g):
                ng = GROUPS[g]
                if g == "ffn":
                    sp.wait_ge(S("list_scattered"), list_base("gnn", "scattered") + 1)
                sp.dma_start(dst_i[:, 0:ng * CHUNKS].rearrange("p (g j) -> p g j", j=CHUNKS),
                             t[g + "_dst"].rearrange("(g p j) -> p g j", p=P, j=CHUNKS)).then_inc(S("list_dst_in"), 16)
                sp.dma_start(src_i[:, 0:ng * CHUNKS].rearrange("p (g j) -> p g j", j=CHUNKS),
                             t[g + "_src"].rearrange("(g p j) -> p g j", p=P, j=CHUNKS)).then_inc(S("list_src_in"), 16)
                sp.wait_ge(S("list_lo_ready"), list_base(g, "lo_ready") + 1)
                sp.dma_start(lo_dram[g].rearrange("(g p j) -> p g j", p=P, j=CHUNKS),
                             lo_b[:, 0:ng * CHUNKS].rearrange("p (g j) -> p g j", j=CHUNKS)).then_inc(S("list_lo_out"), 16)
                sp.wait_ge(S("list_lo_out"), list_base(g, "lo_out") + 16)
                sp.wait_ge(S("list_keyT_ready"), list_base(g, "keyT_ready") + 1)
                sp.dma_start(key_dram[g].rearrange("(t p) -> t p", p=P), keyT[0:TILES, :]).then_inc(S("list_key_out"), 16)
                sp.wait_ge(S("list_key_out"), list_base(g, "key_out") + 16)
                sp.dma_start(keyB, key_dram[g].partition_broadcast(P)).then_inc(S("list_keyB_in"), 16)
                sp.wait_ge(S("list_counts_ready"), list_base(g, "counts_ready") + 1)
                fills = sp.value_load(counts[g][0:1, 1:2], min_val=2, max_val=MAX_STEPS // FILL)
                view = slot_dram[g].rearrange("(k p f) o -> k p (f o)", p=P, f=FILL * ROUNDS)
                with sp.Fori(0, fills) as k:
                    sp.dma_start(view[bass.ds(k, 1), :, :].rearrange("k p f -> (k p) f"), dummy[:, :]).then_inc(S(g + "_filled"), 16)
                lows = lo_dram[g].rearrange("(g n) -> g n", n=GROUP)
                for i in range(2):
                    sp.dma_start(lo_row[i], lows[i:i + 1, :].to_broadcast([P, GROUP])).then_inc(S(f"list_row_in{i}"), 16)
                sp.wait_ge(S("list_order_out"), list_base(g, "order_out") + 16 * TILES)
                with nc.allow_non_contiguous_dma(reason="6400 numbers"):
                    sp.dma_start(order[g][:, 0:TILES], order_dram[g].rearrange("(t p) c -> p (t c)", p=P)).then_inc(S("list_order_in"), 16)
                with sp.Fori(0, ng // 2 - 1) as k:
                    for i in range(2):
                        hold(sp, S(f"list_row_used{i}"), list_base(g, "row_used") + k + 1)
                        sp.dma_start(lo_row[i], lows[bass.ds(2 * k + (2 + i), 1), :].to_broadcast([P, GROUP])).then_inc(S(f"list_row_in{i}"), 16)
                    for i in range(2):
                        hold(sp, S(f"list_slot_out{i}"), list_base(g, "slot_out") + k * (16 * CHUNKS) + 16 * CHUNKS)
                        sp.sem_inc(S(f"list_slot_free{i}"), 1)
                sp.wait_ge(S("list_step_tiles"), list_base(g, "step_tiles") + 1)
                sp.dma_start(step_dram[g].rearrange("(p f) -> p f", p=P), step_i).then_inc(S("list_steps_out"), 16)

            def tiles_out(name):
                with sp.Fori(0, PAIRS) as k:
                    for i in range(2):
                        hold(sp, tile_sem("out", i), tile_base(name, "out") + k * 16 + 16)
                        sp.sem_inc(tile_sem("out_free", i), 1)

            def walk(L):
                c = layers[L]
                g = c["g"]
                sp.wait_ge(S("list_slots_done"), list_base(g, "slots_done") + 1)
                slots = slot_dram[g].rearrange("(s p r) o -> s p (r o)", p=P, r=2 * ROUNDS)
                tiles = step_dram[g].rearrange("(s c) -> s c", c=2)

                def load(h, s):
                    sp.dma_start(idx[h][:, :], slots[s, :, :].rearrange("s p r -> (s p) r")).then_inc(S(f"walk_idx_in{h}"), 16)
                    sp.dma_start(tid[h][:, :], tiles[s, :]).then_inc(S(f"walk_idx_in{h}"), 16)
                if L == "gnn2":
                    sp.wait_ge(S("gnn1_walked"), 1)
                for h in range(2):
                    load(h, slice(h, h + 1))
                done, n = bodies(sp, L)
                with sp.Fori(0, n) as k:
                    for h in range(2):
                        for s in (2 * h, 2 * h + 1):
                            hold(sp, S(f"walk_rows_in{s}"), (done + k) * (16 * ROUNDS) + 16 * ROUNDS)
                        hold(sp, S(f"walk_tid_read{h}"), done + k + 1)
                        load(h, bass.ds(2 * k + (2 + h), 1))
                for h in range(2):
                    hold(sp, S(f"walk_idx_in{h}"), (done + n) * 32 + 32 * (phase_of[L] + 1))
            layout("gnn")
            tiles_out("proj1")
            walk("gnn1")
            tiles_out("proj2")
            walk("gnn2")
            tiles_out("fin2")
            layout("ffn")
            tiles_out("projf")
            sp.wait_ge(S("list_scattered"), list_base("ffn", "scattered") + 1)
            sp.dma_start(w1_sb, t["L0_ffn_W1"].rearrange("e (k p) f -> p e k f", p=P)).then_inc(S("experts_in"), 16)
            sp.dma_start(w2_sb, t["L0_ffn_W2"].rearrange("e (f p) n -> p e f n", p=P)).then_inc(S("experts_in"), 16)
            walk("ffn")
            sp.wait_ge(S("experts_done"), 1)
            for i in range(2):
                sp.dma_start(y_back[i], y_dram[i, :, :]).then_inc(S(f"y_in{i}"), 16)
            with sp.Fori(0, PAIRS - 1) as k:
                for i in range(2):
                    hold(sp, S(f"y_used{i}"), k + 1)
                    sp.dma_start(y_back[i], y_dram[bass.ds(2 * k + (2 + i), 1), :, :].rearrange("t p n -> (t p) n")).then_inc(S(f"y_in{i}"), 16)
                for i in range(2):
                    hold(sp, tile_sem("out", i), tile_base("mix", "out") + k * 16 + 16)
                    sp.sem_inc(tile_sem("out_free", i), 1)

        @block.gpsimd
        def _(pool):
            eng_name[id(pool)] = "pool"
            line = Line(pool, S("pool_line"), S("spare_pool"))
            line(pool.iota(iota_i[:, :], [[1, P]], base=0, channel_multiplier=0))
            line(pool.iota(part_i[:, :], [[0, 1]], base=0, channel_multiplier=1))
            line(pool.iota(nkey_i[:, :], [[-P, TILES]], base=BIG_KEY, channel_multiplier=-1))
            line(pool.memset(dummy[:, :], DUMMY))
            pool.sem_inc(S("iotas"), 1)

            def gather(tile, tab, index, sem):
                pool.indirect_dma_start(tile, None, tab, bass.IndirectOffsetOnAxis(ap=index.bitcast(U32), axis=0)).then_inc(sem, 16)

            def scatter(tab, index, tile, sem, bound=None):
                kw = {} if bound is None else dict(bounds_check=bound, oob_is_err=False)
                pool.indirect_dma_start(tab, bass.IndirectOffsetOnAxis(ap=index.bitcast(U32), axis=0), tile, None, **kw).then_inc(sem, 16)

            def layout(g):
                pool.wait_ge(S("list_ranked"), list_base(g, "ranked") + 1)
                for n in range(TILES):
                    scatter(order_dram[g], rank_i[:, n:n + 1], node_no[:, n:n + 1], S("list_order_out"))
                pool.wait_ge(S("list_counts_ready"), list_base(g, "counts_ready") + 1)
                fills = pool.value_load(counts[g][0:1, 1:2], min_val=2, max_val=MAX_STEPS // FILL)
                hold(pool, S(g + "_filled"), fills * 16)
                with pool.Fori(0, GROUPS[g] // 2) as k:
                    for i in range(2):
                        hold(pool, S(f"list_placed{i}"), list_base(g, "placed") + k + 1)
                        for j in range(CHUNKS):
                            scatter(slot_dram[g], slot_st[i][:, j:j + 1], src_st[i][:, j:j + 1], S(f"list_slot_out{i}"),
                                    MAX_STEPS * ROUNDS * P - 1)
                for i in range(2):
                    pool.wait_ge(S(f"list_slot_out{i}"), list_base(g, "slot_out") + 16 * CHUNKS * GROUPS[g] // 2)
                pool.sem_inc(S("list_scattered"), 1)
                pool.wait_ge(S("list_steps_out"), list_base(g, "steps_out") + 16)
                pool.sem_inc(S("list_slots_done"), 1)

            def walk(L):
                c = layers[L]
                g = c["g"]
                done, n = bodies(pool, L)
                with pool.Fori(0, n) as k:
                    for s in range(STEPS):
                        if s % 2 == 0:
                            hold(pool, S(f"walk_idx_in{s // 2}"), (done + k) * 32 + 32 * (phase_of[L] + 1))
                        hold(pool, S(f"walk_rows_free{s}"), done + k + (phase_of[L] + 1))
                        for r in range(ROUNDS):
                            gather(c["ring"][s][:, r, :], table[L], idx[s // 2][:, (s % 2) * ROUNDS + r:(s % 2) * ROUNDS + r + 1],
                                   S(f"walk_rows_in{s}"))

            def tiles_loop(name, source, target, tiles_out, bound=None):
                if source is not None:
                    for i in range(2):
                        pool.wait_ge(tile_sem("index_in", i), tile_base(name, "index_in") + 1)
                        gather(xt[i], source, gi_in[i][:, :], tile_sem("x_in", i))
                with pool.Fori(0, PAIRS) as k:
                    for i in range(2 if source is not None else 0):
                        hold(pool, tile_sem("index_in", i), tile_base(name, "index_in") + k + 2)
                        hold(pool, tile_sem("x_free", i), tile_base(name, "x_free") + k + 1)
                        gather(xt[i], source, gi_in[i][:, :], tile_sem("x_in", i))
                    for i in range(2):
                        hold(pool, tile_sem("index", i), tile_base(name, "index") + k + 1)
                        hold(pool, tile_sem("out_ready", i), tile_base(name, "out_ready") + k + 1)
                        scatter(target, gi[i][:, :], tiles_out[i] if isinstance(tiles_out[i], bass.AP) else tiles_out[i][:, :],
                                tile_sem("out", i), bound)
                for i in range(2):
                    pool.wait_ge(tile_sem("out", i), tile_base(name, "out") + 16 * PAIRS)

            layout("gnn")
            pool.wait_ge(S("dummies_out"), 48)
            tiles_loop("proj1", t["x"], table["gnn1"], row)
            walk("gnn1")
            tiles_loop("proj2", None, table["gnn2"], row)
            walk("gnn2")
            tiles_loop("fin2", t["x"], x2_dram, tmp)
            layout("ffn")
            tiles_loop("projf", x2_dram, table["ffn"], row_f)
            walk("ffn")
            tiles_loop("mix", None, out, yout, NODES - 1)

        @block.scalar
        def _(act):
            eng_name[id(act)] = "act"
            act_line = Line(act, S("act_line"), S("spare_act"))

            def layout(g):
                act.wait_ge(S("list_keyB_in"), list_base(g, "keyB_in") + 16)
                act.wait_ge(S("list_key_ready"), list_base(g, "key_ready") + 1)
                for n in range(DVE_RANKS, TILES):
                    act_line(act.activation(junk_act, keyB, ACT.Sign, bias=neg_key[:, n:n + 1], accum_out=rank[:, n:n + 1]))
                act.sem_inc(S("list_act_ranked"), 1)
                with act.Fori(0, GROUPS[g] // 2) as k:
                    for i in range(2):
                        for j in range(CHUNKS):
                            act.wait_ge(S("list_counted"), list_base(g, "counted") + (k * 2 + i) * CHUNKS + (j + 1))
                            act.activation(count_sb[j], run_ps, ACT.Copy).then_inc(S("list_copied"), 1)

            def walk(L):
                g = layers[L]["g"]
                done, n = bodies(act, L)
                with act.Fori(0, n) as k:
                    for s in range(STEPS):
                        act.wait_ge(S(f"walk_scores{s}"), done + k + 1)
                        act.activation(eprob[s][:, :, :], escore[s][:, :, :], ACT.Exp).then_inc(S(f"walk_probs{s}"), 1)

            def norm_and_copy(name, keep_x=False):
                with act.Fori(0, PAIRS) as k:
                    if name in ("proj1", "projf"):
                        for i in range(2):
                            act.wait_ge(tile_sem("var", i), tile_base(name, "var") + k + 1)
                            act.activation(rstd[i][:, 0:1], mv[i][:, 1:2], ACT.Sqrt, bias=eps_col[:, :]).then_inc(tile_sem("std", i), 1)
                    else:
                        for i in range(2):
                            act.wait_ge(tile_sem("neg", i), tile_base(name, "neg") + k + 1)
                            act.activation(tmp2[i][:, :], tmp2[i][:, :], ACT.Exp).then_inc(tile_sem("exp", i), 1)
                    for i in range(2 if name != "fin2" else 0):
                        hold(act, tile_sem("T", i), tile_base(name, "T") + k + 1)
                        act.activation(xnT[i][:, :, :], bank[i][:, 0:DIM].rearrange("p (k n) -> p k n", k=2), ACT.Copy).then_inc(tile_sem("T_copied", i), 1)
                        if name == "projf":
                            act.activation(big2[:, bass.ds(k * 512 + i * DIM, DIM)], bank[i][:, 0:DIM], ACT.Copy).then_inc(S("expert_in_kept"), 1)

            layout("gnn")
            norm_and_copy("proj1")
            walk("gnn1")
            norm_and_copy("proj2")
            walk("gnn2")
            norm_and_copy("fin2")
            layout("ffn")
            norm_and_copy("projf")
            done, n = bodies(act, "ffn")

            def probabilities(k, s):
                act.wait_ge(S(f"walk_scores{s}"), done + k + 1)
                act.activation(eprob[s][:, :, :], escore[s][:, :, :], ACT.Exp).then_inc(S(f"walk_probs{s}"), 1)

            act.sem_inc(S("gelued"), 2)
            act.sem_inc(S("y_kept"), 2)
            with act.Fori(0, TILES) as k:
                def hidden(e):
                    act.wait_ge(S("hidden"), k * EXPERTS + (e + 1))
                    act.wait_ge(S("expert_out"), k * EXPERTS + (e + 1))
                    for f in range(FCH):
                        a = act.activation(hT[e % 2][:, f, :], bank[e % 2][:, f * P:(f + 1) * P], ACT.Gelu,
                                           bias=b1cols[:, e * FCH + f:e * FCH + f + 1])
                    a.then_inc(S("gelued"), 1)

                def keep(e):
                    act.wait_ge(S("expert_out"), k * EXPERTS + (e + 3))
                    act.activation(y_keep[:, e * DIM:(e + 1) * DIM], bank[2 + e % 2][:, 0:DIM], ACT.Copy).then_inc(S("y_kept"), 1)

                hidden(0)
                for e in range(EXPERTS):
                    if e + 1 < EXPERTS:
                        hidden(e + 1)
                    if e < STEPS - 1:
                        probabilities(k, e)
                    keep(e)
                act.wait_ge(S("y_kept"), k * EXPERTS + (EXPERTS + 2))
                act.dma_start(y_dram[bass.ds(k, 1), :, :].rearrange("t p n -> (t p) n"), y_keep).then_inc(S("y_out"), 16)
                probabilities(k, STEPS - 1)
                act.wait_ge(S("y_out"), k * 16 + 16)
                act.sem_inc(S("spare_act"), 1)
            act.sem_inc(S("experts_done"), 1)
            with act.Fori(0, n - TILES) as k:
                for s in range(STEPS):
                    probabilities(k + TILES, s)
            act.wait_ge(S("gat_var"), 1)
            act.activation(tile_cols(), tile_cols(), ACT.Sqrt, bias=eps_col[:, :]).then_inc(S("gat_std"), 1)
            act.wait_ge(S("gat_top"), 1)
            act.activation(gates[:, :], gates[:, :], ACT.Exp).then_inc(S("gat_exp"), 1)

        @block.tensor
        def _(pe):
            eng_name[id(pe)] = "pe"
            pe.wait_ge(S("consts"), 1)

            def layout(g):
                ng = GROUPS[g]
                if g == "ffn":
                    pe.wait_ge(S("fin2_done"), 1)
                pe.matmul(run_ps, zero_b[:, :], zero_b[:, 0:TILES], start=True, stop=False, skip_group_check=True)
                with pe.Fori(0, ng // 2) as k:
                    for i in range(2):
                        pe.wait_ge(S(f"list_hot_ready{i}"), list_base(g, "hot_ready") + k * 2 + 2)
                        for j in range(CHUNKS):
                            m = pe.matmul(run_ps, one_lo[i][:, j, :], one_hi[i][:, j, :], start=False, stop=False, skip_group_check=True)
                        m.then_inc(S(f"list_hot_used{i}"), 1)
                m = pe.matmul(run_ps, zero_b[:, :], zero_b[:, 0:TILES], start=False, stop=True, skip_group_check=True)
                m.then_inc(S("list_hist_done"), 1)
                pe.wait_ge(S("list_key_ready"), list_base(g, "key_ready") + 1)
                pe.transpose(bank[1][0:TILES, 0:P], key, ident[:, :]).then_inc(S("list_keyT"), 1)
                pe.wait_ge(S("list_maxT"), list_base(g, "maxT") + 1)
                pe.transpose(bank[1][0:TILES, 0:P], base, ident[:, :]).then_inc(S("list_maxT_ps"), 1)
                pe.wait_ge(S("list_steps_ready"), list_base(g, "steps_ready") + 1)
                pe.matmul(bank[2][:, 0:TILES + 1], steps_b[0:TILES, :], before[0:TILES, 0:TILES + 1], start=True, stop=True).then_inc(S("list_tb"), 1)
                pe.wait_ge(S("list_base_ready"), list_base(g, "base_ready") + 1)
                pe.matmul(run_ps, ident[:, :], base, start=True, stop=False, skip_group_check=True).then_inc(S("list_counted"), 1)

                def pairs(k, i):
                    chunk = lo_T[i].rearrange("p (q j) -> p j q", j=CHUNKS)
                    pe.wait_ge(S(f"list_loT{i}"), list_base(g, "loT") + k + 1)
                    for j in range(CHUNKS):
                        m = pe.matmul(bank[3 + 2 * i + j // 4][:, (j % 4) * P:(j % 4 + 1) * P], chunk[:, j, :], chunk[:, j, :],
                                      start=True, stop=True)
                    m.then_inc(S(f"list_same_ps{i}"), 1)

                def count(k, i):
                    chunk = lo_T[i].rearrange("p (q j) -> p j q", j=CHUNKS)
                    pe.wait_ge(S(f"list_hot2_ready{i}"), list_base(g, "hot2_ready") + k * 4 + 4)
                    for j in range(CHUNKS):
                        c = (k * 2 + i) * CHUNKS + (j + 1)
                        pe.wait_ge(S("list_copied"), list_base(g, "copied") + c)
                        pe.matmul(run_ps, one_lo[i][:, j, :], one_hi[i][:, j, :], start=False, stop=False, skip_group_check=True).then_inc(S("list_counted"), 1)
                        look = bank[1 + i][:, j * TILES:(j + 1) * TILES]
                        pe.matmul(look, chunk[:, j, :], count_sb[j], start=True, stop=False, skip_group_check=True)
                        m = pe.matmul(look, same[i][:, j, :], one_hi[i][:, j, :], start=False, stop=True, skip_group_check=True)
                    m.then_inc(S(f"list_looked{i}"), 1)

                pairs(0, 0)
                with pe.Fori(0, ng // 2 - 1) as k:
                    for i in range(2):
                        count(k, i)
                        pairs(k + i, 1 - i)
                last_pair = ng // 2 - 1
                count(last_pair, 0)
                pairs(last_pair, 1)
                count(last_pair, 1)

            def walk(L):
                done, n = bodies(pe, L)
                w = width(64)
                with pe.Fori(0, n) as k:
                    for s in range(STEPS):
                        pe.wait_ge(S(f"walk_rows_free{s}"), done + k + (phase_of[L] + 2))
                        pe.wait_ge(S("walk_added"), (done + k) * STEPS + (s + 1 + 2 * phase_of[L]))
                        for r in range(ROUNDS):
                            m = pe.matmul(bank[s % 2][:, 0:w], ident[:, :], prod[s % 2][:, r, :], start=(r == 0), stop=(r == ROUNDS - 1))
                        m.then_inc(S("walk_summed"), 1)

            def project(name, w, cols):
                with pe.Fori(0, PAIRS) as k:
                    for i in range(2):
                        pe.wait_ge(tile_sem("xn", i), tile_base(name, "xn") + k + 1)
                        for h in range(2):
                            m = pe.transpose(bank[i][:, h * P:(h + 1) * P], xn[i][:, h * P:(h + 1) * P], ident[:, :])
                        m.then_inc(tile_sem("T", i), 1)
                    for i in range(2):
                        pe.wait_ge(tile_sem("T_copied", i), tile_base(name, "T_copied") + k + 1)
                        for h in range(2):
                            m = pe.matmul(bank[2 + i][:, 0:cols], xnT[i][:, h, :], w(h), start=(h == 0), stop=(h == 1))
                        m.then_inc(tile_sem("feat", i), 1)

            layout("gnn")
            pe.wait_ge(S("constants_loaded"), 16 * 16)
            project("proj1", lambda h: wpair[:, 0, h, :], DIM)
            walk("gnn1")
            project("proj2", lambda h: wpair[:, 1, h, :], DIM)
            walk("gnn2")
            layout("ffn")
            project("projf", lambda h: wgat[:, h, :], 16)
            pe.wait_ge(S("experts_in"), 32)
            pe.wait_ge(S("expert_in_kept"), TILES)
            pe.sem_inc(S("expert_out"), 2)
            with pe.Fori(0, TILES) as k:
                def up(e):
                    pe.wait_ge(S("gelued"), k * EXPERTS + (e + 1))
                    for f in range(FCH):
                        for h in range(2):
                            m = pe.matmul(bank[e % 2][:, f * P:(f + 1) * P], w1_sb[:, e, h, f * P:(f + 1) * P],
                                          big2[:, bass.ds(k * DIM + h * P, P)], start=(h == 0), stop=(h == 1))
                    m.then_inc(S("hidden"), 1)

                def down(e):
                    pe.wait_ge(S("gelued"), k * EXPERTS + (e + 3))
                    pe.wait_ge(S("y_kept"), k * EXPERTS + (e + 1))
                    y = bank[2 + e % 2][:, 0:DIM]
                    for f in range(FCH):
                        pe.matmul(y, hT[e % 2][:, f, :], w2_sb[:, e, f, :], start=(f == 0), stop=False)
                    pe.matmul(y, ones_row[:, :], b2rows[:, e, :], start=False, stop=True).then_inc(S("expert_out"), 1)
                up(0)
                for e in range(EXPERTS):
                    if e + 1 < EXPERTS:
                        up(e + 1)
                    down(e)

        @block.vector
        def _(dve):
            eng_name[id(dve)] = "dve"
            line = Line(dve, S("dve_line"), S("spare_dve"))
            V = nc.vector
            dve.wait_ge(S("iotas"), 1)
            line(V.tensor_copy(iota_f[:, :], iota_i[:, :]))
            line(V.tensor_copy(iota_b[:, :], iota_i[:, :]))
            line(V.tensor_copy(part_f[:, :], part_i[:, :]))
            line(V.tensor_copy(nkey[:, :], nkey_i[:, :]))
            line(V.tensor_scalar(before[:, :], iota_f[:, :], part_f[:, :], None, ALU.is_gt))
            line(V.tensor_scalar(ident[:, :], iota_f[:, :], part_f[:, :], None, ALU.is_equal))
            line(V.memset(zero_b[:, :], 0.0))
            line(V.memset(eps_col[:, :], EPS))
            line(V.memset(ones_row[:, :], 1.0))
            for r, w in ((dummy_row, width(64)), (dummy_row_f, width(4))):
                line(V.memset(r[:, 0:w], 0.0))
                line(V.memset(r[:, w:w + 4], NONE))
            for g in G:
                line(V.memset(order[g][:, TILES:TILES + 2], 0))
            for i in range(2):
                line(V.memset(row[i][:, :], 1.0))
                line(V.memset(row_f[i][:, :], 1.0))
            dve.sem_inc(S("consts"), 1)

            def one_hots(g, i, k, dst_lo, dst_hi, sem):
                c = bass.ds((2 * k + i) * CHUNKS, CHUNKS)
                V.tensor_tensor(dst_lo[i], iota_b[:, :].unsqueeze(1).to_broadcast([P, CHUNKS, P]),
                                lo_b[:, c].unsqueeze(2).to_broadcast([P, CHUNKS, P]), ALU.is_equal).then_inc(sem, 1)
                V.tensor_tensor(dst_hi[i], iota_b[:, 0:TILES].unsqueeze(1).to_broadcast([P, CHUNKS, TILES]),
                                hi_b[:, c].unsqueeze(2).to_broadcast([P, CHUNKS, TILES]), ALU.is_equal).then_inc(sem, 1)

            def layout(g):
                ng = GROUPS[g]
                n = ng * CHUNKS
                last = NODES - 1
                dve.wait_ge(S("list_dst_in"), list_base(g, "dst_in") + 16)
                dve.wait_ge(S("list_src_in"), list_base(g, "src_in") + 16)
                line(V.tensor_scalar(src_i[:, 0:n], src_i[:, 0:n], float(last), None, ALU.min))
                line(V.tensor_scalar(tmp_i[:, 0:n], dst_i[:, 0:n], 127, None, ALU.bitwise_and))
                line(V.tensor_copy(lo_b[:, 0:n], tmp_i[:, 0:n]))
                dve.sem_inc(S("list_lo_ready"), 1)
                line(V.tensor_scalar(off_f[:, 0:n], dst_i[:, 0:n], float(NODES), None, ALU.is_ge))
                line(V.tensor_scalar(tmp_i[:, 0:n], dst_i[:, 0:n], 7, None, ALU.logical_shift_right))
                line(V.scalar_tensor_tensor(hi_b[:, 0:n], off_f[:, 0:n], 64.0, tmp_i[:, 0:n], ALU.mult, ALU.add))
                line(V.tensor_scalar(off_f[:, 0:n], off_f[:, 0:n], float(2 ** 18), 8192.0, ALU.mult, ALU.add))
                for i in range(2):
                    dve.sem_inc(S(f"list_hot_used{i}"), 1)
                with dve.Fori(0, ng // 2) as k:
                    for i in range(2):
                        dve.wait_ge(S(f"list_hot_used{i}"), list_base(g, "hot_used") + k + 1)
                        one_hots(g, i, k, one_lo, one_hi, S(f"list_hot_ready{i}"))
                dve.wait_ge(S("list_hist_done"), list_base(g, "hist_done") + 1)
                line(V.tensor_copy(deg, run_ps))
                line(V.tensor_scalar(key, deg, 2047.0, 8192.0, ALU.min, ALU.mult))
                line(V.tensor_tensor(key, key, nkey[:, :], ALU.add))
                line(V.tensor_scalar(neg_key, key, -1.0, None, ALU.mult))
                dve.sem_inc(S("list_key_ready"), 1)
                dve.wait_ge(S("list_keyT"), list_base(g, "keyT") + 1)
                line(V.tensor_copy(keyT[0:TILES, :], bank[1][0:TILES, 0:P]))
                dve.sem_inc(S("list_keyT_ready"), 1)
                dve.wait_ge(S("list_keyB_in"), list_base(g, "keyB_in") + 16)
                for n_ in range(DVE_RANKS):
                    line(V.tensor_scalar(junk, keyB, key[:, n_:n_ + 1], None, ALU.is_gt, ALU.add, accum_out=rank[:, n_:n_ + 1]))
                dve.wait_ge(S("list_act_ranked"), list_base(g, "act_ranked") + 1)
                late = rank[:, DVE_RANKS:TILES]
                line(V.tensor_scalar(late, late, float(SLOTS - 1), 0.5, ALU.add, ALU.mult))
                line(V.tensor_copy(rank_i, rank[:, :]))
                line(V.tensor_scalar(tmp_i[:, 0:TILES], nkey[:, :], -1.0, float(BIG_KEY), ALU.mult, ALU.add))
                line(V.tensor_copy(node_no, tmp_i[:, 0:TILES]))
                dve.sem_inc(S("list_ranked"), 1)
                line(V.tensor_scalar(tmp_i[:, 0:TILES], rank_i, 7, None, ALU.logical_shift_right))
                line(V.tensor_copy(tile_f, tmp_i[:, 0:TILES]))
                line(V.tensor_scalar(tmp_i[:, 0:TILES], rank_i, 127, None, ALU.bitwise_and))
                line(V.tensor_copy(place_f, tmp_i[:, 0:TILES]))
                line(V.tensor_tensor(in_tile, tile_f.unsqueeze(2).to_broadcast([P, TILES, TILES]),
                                     iota_f[:, 0:TILES].unsqueeze(1).to_broadcast([P, TILES, TILES]), ALU.is_equal))
                line(V.tensor_tensor(spread, in_tile, deg.unsqueeze(2).to_broadcast([P, TILES, TILES]), ALU.mult))
                line(V.tensor_reduce(base, spread.rearrange("p n t -> p t n"), X, ALU.max))
                dve.sem_inc(S("list_maxT"), 1)
                dve.wait_ge(S("list_maxT_ps"), list_base(g, "maxT_ps") + 1)
                line(V.tensor_reduce(maxdeg[0:TILES, :], bank[1][0:TILES, 0:P], X, ALU.max))
                line(V.tensor_scalar(steps_f[0:TILES, :], maxdeg[0:TILES, :], float(ROUNDS - 1), None, ALU.add))
                line(V.tensor_copy(steps_i[0:TILES, :], steps_f[0:TILES, :]))
                line(V.tensor_scalar(steps_i[0:TILES, :], steps_i[0:TILES, :], 2, None, ALU.logical_shift_right))
                line(V.tensor_copy(steps_f[0:TILES, :], steps_i[0:TILES, :]))
                line(V.tensor_copy(steps_b[0:TILES, :], steps_f[0:TILES, :].to_broadcast([TILES, P])))
                dve.sem_inc(S("list_steps_ready"), 1)
                dve.wait_ge(S("list_tb"), list_base(g, "tb") + 1)
                line(V.tensor_copy(tb, bank[2][:, 0:TILES + 1]))
                line(V.tensor_copy(total_i, tb[:, TILES:TILES + 1]))
                line(V.tensor_scalar(tmp_i[:, 0:1], total_i, 2, None, ALU.logical_shift_right))
                least = TILES if g == "ffn" else 1
                line(V.tensor_scalar(counts[g][:, 0:1], tmp_i[:, 0:1], 1.0, float(least), ALU.add, ALU.max))
                line(V.tensor_scalar(tmp_i[:, 0:1], total_i, 6, None, ALU.logical_shift_right))
                line(V.tensor_scalar(counts[g][:, 1:2], tmp_i[:, 0:1], 2.0, float(least * STEPS // FILL + 2), ALU.add, ALU.max))
                dve.sem_inc(S("list_counts_ready"), 1)
                line(V.tensor_tensor(spread, in_tile, tb[:, 0:TILES].unsqueeze(1).to_broadcast([P, TILES, TILES]), ALU.mult))
                line(V.tensor_reduce(base, spread, X, ALU.add))
                line(V.tensor_scalar(base, base, float(ROUNDS), -65536.0, ALU.mult, ALU.add))
                line(V.scalar_tensor_tensor(base, place_f, 1.0 / P, base, ALU.mult, ALU.add))
                dve.sem_inc(S("list_base_ready"), 1)
                for i in range(2):
                    dve.sem_inc(S(f"list_looked{i}"), 1)
                    dve.sem_inc(S(f"list_slot_free{i}"), 1)

                def first(k, i):
                    dve.wait_ge(S(f"list_looked{i}"), list_base(g, "looked") + k + 1)
                    dve.wait_ge(S(f"list_row_in{i}"), list_base(g, "row_in") + k * 16 + 16)
                    V.tensor_scalar(lo_T[i], lo_row[i], part_f[:, :], None, ALU.is_equal).then_inc(S(f"list_loT{i}"), 1)
                    one_hots(g, i, k, one_lo, one_hi, S(f"list_hot2_ready{i}"))
                    dve.wait_ge(S(f"list_loT{i}"), list_base(g, "loT") + k + 1)
                    dve.sem_inc(S(f"list_row_used{i}"), 1)

                def second(k, i):
                    dve.wait_ge(S(f"list_same_ps{i}"), list_base(g, "same_ps") + k + 1)
                    for h in range(2):
                        V.tensor_tensor(same[i][:, 4 * h:4 * h + 4, :], bank[3 + 2 * i + h][:, :].rearrange("p (j c) -> p j c", c=P),
                                        before[:, :].unsqueeze(1).to_broadcast([P, 4, P]), ALU.mult).then_inc(S(f"list_hot2_ready{i}"), 1)

                def place(k, i):
                    c = bass.ds((2 * k + i) * CHUNKS, CHUNKS)
                    dve.wait_ge(S(f"list_looked{i}"), list_base(g, "looked") + k + 2)
                    line(V.tensor_tensor(pick.rearrange("p (j c) -> p j c", j=CHUNKS), bank[1 + i][:, 0:CHUNKS * TILES].rearrange("p (j c) -> p j c", j=CHUNKS),
                                         one_hi[i], ALU.mult))
                    line(V.tensor_reduce(found, pick.rearrange("p (j c) -> p j c", j=CHUNKS), X, ALU.add))
                    a = line.put(V.tensor_scalar(ints[0], found, float(P), None, ALU.mult))
                    line.need(a)
                    b = line.put(V.tensor_scalar(ints[3], ints[0], 10, None, ALU.arith_shift_right))
                    c1 = line.put(V.tensor_scalar(ints[1], ints[0], 127, 3, ALU.bitwise_and, ALU.logical_shift_left))
                    c2 = line.put(V.tensor_scalar(ints[2], ints[0], 7, 7, ALU.arith_shift_right, ALU.bitwise_and))
                    line.need(b)
                    b = line.put(V.tensor_tensor(ints[4], ints[3], off_f[:, c], ALU.add))
                    line.need(c2)
                    c1 = line.put(V.tensor_tensor(ints[1], ints[1], ints[2], ALU.bitwise_or))
                    line.need(b)
                    b = line.put(V.tensor_scalar(ints[3], ints[4], 10, None, ALU.logical_shift_left))
                    dve.wait_ge(S(f"list_slot_free{i}"), list_base(g, "slot_free") + k + 1)
                    line.put(V.tensor_tensor(src_st[i], src_i[:, c], src_i[:, c], ALU.max))
                    line.need(b)
                    line(V.tensor_tensor(slot_st[i], ints[3], ints[1], ALU.bitwise_or))
                    dve.sem_inc(S(f"list_placed{i}"), 1)

                first(0, 0)
                second(0, 0)
                with dve.Fori(0, ng // 2 - 1) as k:
                    line.enter(k, 2 * 11)
                    for i in range(2):
                        first(k + i, 1 - i)
                        place(k, i)
                        second(k + i, 1 - i)
                    line.leave(ng // 2 - 1)
                last_pair = ng // 2 - 1
                first(last_pair, 1)
                place(last_pair, 0)
                second(last_pair, 1)
                place(last_pair, 1)
                line(V.memset(step_acc, 0.0))
                line(V.tensor_scalar(step_f, iota_f[:, 0:1].to_broadcast([P, STEP_COLS]), 0.0, None, ALU.mult))
                line(V.tensor_scalar(step_f[:, 0:P], iota_f[:, :], 0.0, None, ALU.add))
                line(V.tensor_scalar(step_f[:, P:2 * P], iota_f[:, :], float(P), None, ALU.add))
                line(V.tensor_scalar(step_f[:, 2 * P:STEP_COLS], iota_f[:, 0:STEP_COLS - 2 * P], float(2 * P), None, ALU.add))
                line(V.tensor_scalar(steps_f, part_f[:, :], float(STEP_COLS), None, ALU.mult))
                line(V.tensor_scalar(step_f, step_f, steps_f, None, ALU.add))
                for n_ in range(1, TILES):
                    line(V.scalar_tensor_tensor(step_acc, step_f, tb[:, n_:n_ + 1], step_acc, ALU.is_ge, ALU.add))
                line(V.tensor_copy(step_i, step_acc))
                dve.sem_inc(S("list_step_tiles"), 1)

            def walk(L):
                nonlocal line
                c = layers[L]
                g, d, sums, rg = c["g"], c["d"], c["sums"], c["ring"]
                w = width(d)
                for s in range(STEPS):
                    dve.sem_inc(S(f"walk_rows_free{s}"), 1)
                done, n = bodies(dve, L)
                mine = Line(dve, S(L + "_line"), S("spare_dve"))
                on_pe = L != "ffn"
                if on_pe:
                    dve.sem_inc(S("walk_added"), 2)
                with dve.Fori(0, n) as k:
                    mine.enter(k, (7 if on_pe else 9) * STEPS)
                    tiles = {}
                    free_z = [None]

                    def score(s):
                        if s % 2 == 0:
                            hold(dve, S(f"walk_idx_in{s // 2}"), (done + k) * 32 + 32 * (phase_of[L] + 1))
                            for q in range(2):
                                tiles[s + q] = dve.value_load(tid[s // 2][0:1, q:q + 1], min_val=0, max_val=TILES - 1)
                            dve.sem_inc(S(f"walk_tid_read{s // 2}"), 1)
                        tl = tiles[s]
                        hc = bass.ds(tl * HEADS, HEADS)
                        dve.wait_ge(S(f"walk_rows_in{s}"), (done + k) * (16 * ROUNDS) + 16 * ROUNDS)
                        m = mine.put(V.tensor_tensor(zbuf[:, :, :], rg[s][:, :, w:w + 4], er[:, hc].unsqueeze(1).to_broadcast([P, ROUNDS, HEADS]), ALU.add))
                        yield
                        mine.need(m)
                        m = mine.put(V.scalar_tensor_tensor(zbuf[:, :, :], zbuf[:, :, :], 0.2, zbuf[:, :, :], ALU.mult, ALU.max))
                        yield
                        mine.need(m)
                        m = mine.put(V.tensor_reduce(tmax[:, :], zbuf[:, :, :].rearrange("p r h -> p h r"), X, ALU.max))
                        yield
                        mine.need(m)
                        m = mine.put(V.tensor_tensor(tmax[:, :], tmax[:, :], top[:, hc], ALU.max))
                        yield
                        mine.need(m)
                        mine.put(V.tensor_tensor(escore[s][:, 0:ROUNDS, :], zbuf[:, :, :], tmax[:, :].unsqueeze(1).to_broadcast([P, ROUNDS, HEADS]), ALU.subtract))
                        V.tensor_tensor(escore[s][:, ROUNDS, :], top[:, hc], tmax[:, :], ALU.subtract).then_inc(S(f"walk_scores{s}"), 1)
                        yield
                        dve.wait_ge(S(f"walk_scores{s}"), done + k + 1)
                        mine.put(V.tensor_tensor(top[:, hc], tmax[:, :], tmax[:, :], ALU.max))

                    def weigh(s):
                        dve.wait_ge(S(f"walk_probs{s}"), done + k + 1)
                        pr = prod[s % 2][:, :, 0:w].rearrange("p r (h d) -> p r h d", h=HEADS)
                        V.tensor_tensor(pr, rg[s][:, :, 0:w].rearrange("p r (h d) -> p r h d", h=HEADS),
                                        eprob[s][:, 0:ROUNDS, :].unsqueeze(3).to_broadcast([P, ROUNDS, HEADS, d + 1]), ALU.mult).then_inc(S(f"walk_rows_free{s}"), 1)

                    def total(s):
                        return sums[:, bass.ds(tiles[s] * w, w)]

                    def rescale(s):
                        tot = total(s).rearrange("p (h d) -> p h d", h=HEADS)
                        return mine.put(V.tensor_tensor(tot, tot, eprob[s][:, ROUNDS, :].unsqueeze(2).to_broadcast([P, HEADS, d + 1]), ALU.mult))

                    def add(s):
                        if on_pe:
                            dve.wait_ge(S("walk_summed"), (done + k) * STEPS + (s + 1))
                            part = bank[s % 2][:, 0:w]
                            V.tensor_tensor(total(s), total(s), part, ALU.add).then_inc(S("walk_added"), 1)
                            return (S("walk_added"), (done + k) * STEPS + (s + 1 + 2 * (phase_of[L] + 1)))
                        dve.wait_ge(S(f"walk_rows_free{s}"), done + k + (phase_of[L] + 2))
                        m = mine.put(V.tensor_reduce(part_sum[:, 0:w], prod[s % 2][:, :, 0:w].rearrange("p r w -> p w r"), X, ALU.add))
                        mine.need(m)
                        m = mine.put(V.tensor_tensor(total(s), total(s), part_sum[:, 0:w], ALU.add))
                        mine.need(m)
                        return None

                    for _ in score(0):
                        pass
                    scaled = None
                    for s in range(STEPS):
                        nxt = score(s + 1) if s + 1 < STEPS else iter(())
                        next(nxt, None)
                        weigh(s)
                        next(nxt, None)
                        if s and on_pe:
                            mine.need(scaled)
                            sem, value = add(s - 1)
                            next(nxt, None)
                            dve.wait_ge(sem, value)
                        else:
                            next(nxt, None)
                        scaled = rescale(s)
                        for _ in nxt:
                            pass
                        if not on_pe:
                            mine.need(scaled)
                            add(s)
                    if on_pe:
                        mine.need(scaled)
                        sem, value = add(STEPS - 1)
                        hold(dve, sem, value)
                    mine.leave(None)

            def index(name, g, k, i):
                hold(dve, tile_sem("out_free", i), tile_base(name, "out_free") + k + 1)
                line.hold(V.tensor_copy(gi[i][:, :], order[g][:, bass.ds(2 * k + i, 1)]))
                dve.sem_inc(tile_sem("index", i), 1)

            def zipped(part):
                both = [part(i) for i in range(2)]
                while both:
                    both = [b for b in both if next(b, StopIteration) is not StopIteration]

            def index_in(name, g, k, i, first=False):
                c = slice(i, i + 1) if first else bass.ds(2 * k + (2 + i), 1)
                V.tensor_copy(gi_in[i][:, :], order[g][:, c]).then_inc(tile_sem("index_in", i), 1)

            def norm(name, g, k):
                def part(i):
                    dve.wait_ge(tile_sem("x_in", i), tile_base(name, "x_in") + k * 16 + 16)
                    m = line.put(V.bn_stats(stats[i][:, :], xt[i]))
                    yield True
                    line.need(m)
                    dve.sem_inc(S("spare_dve"), 1)
                    V.bn_aggr(mv[i][:, :], stats[i][:, :]).then_inc(tile_sem("var", i), 1)
                    index_in(name, g, k, i)
                    yield True
                    dve.wait_ge(tile_sem("std", i), tile_base(name, "std") + k + 1)
                    m = line.put(V.reciprocal(rstd[i][:, 1:2], rstd[i][:, 0:1]))
                    yield True
                    line.need(m)
                    V.tensor_scalar(xn[i], xt[i], mv[i][:, 0:1], rstd[i][:, 1:2], ALU.subtract, ALU.mult).then_inc(tile_sem("xn", i), 1)
                    yield True
                    if name == "projf":
                        V.tensor_tensor(big1[:, bass.ds((2 * k + i) * DIM, DIM)], xt[i], xt[i], ALU.max).then_inc(tile_sem("x_free", i), 1)
                zipped(part)

            def rows(name, L, k):
                c = layers[L]
                d = c["d"]
                w = width(d)
                n = HEADS * d

                def part(i):
                    r = c["row"][i]
                    hc = bass.ds((2 * k + i) * HEADS, HEADS)
                    f = bank[2 + i][:, 0:n]
                    dve.wait_ge(tile_sem("feat", i), tile_base(name, "feat") + k + 1)
                    a = line.put(V.tensor_tensor(tmp[i][:, 0:n], f, c["al"], ALU.mult))
                    b = line.put(V.tensor_tensor(tmp2[i][:, 0:n], f, c["ar"], ALU.mult))
                    yield True
                    line.need(a)
                    line.put(V.tensor_reduce(r[:, w:w + 4], tmp[i][:, 0:n].rearrange("p (h d) -> p h d", h=HEADS), X, ALU.add))
                    yield True
                    line.need(b)
                    e = line.put(V.tensor_reduce(rstd[i][:, :], tmp2[i][:, 0:n].rearrange("p (h d) -> p h d", h=HEADS), X, ALU.add))
                    V.tensor_copy(r[:, 0:w].rearrange("p (h d) -> p h d", h=HEADS)[:, :, 0:d], f.rearrange("p (h d) -> p h d", h=HEADS)).then_inc(tile_sem("out_ready", i), 1)
                    yield True
                    line.need(e)
                    line.put(V.tensor_tensor(er[:, hc], rstd[i][:, :], rstd[i][:, :], ALU.max))
                    if name == "projf":
                        m = line.put(V.tensor_tensor(zbuf[:, i, :], r[:, w:w + 4], rstd[i][:, :], ALU.add))
                        yield True
                        line.need(m)
                        line.put(V.scalar_tensor_tensor(top[:, hc], zbuf[:, i, :], 0.2, zbuf[:, i, :], ALU.mult, ALU.max))
                        dve.wait_ge(tile_sem("out_ready", i), tile_base(name, "out_ready") + k + 1)
                        line.put(V.tensor_tensor(sums_f[:, bass.ds((2 * k + i) * w, w)], r[:, 0:w], r[:, 0:w], ALU.max))
                zipped(part)

            def aggregate(name, k, bias, residual):
                w = width(64)

                def part(i):
                    sv = big1[:, bass.ds((2 * k + i) * w, w)].rearrange("p (h d) -> p h d", h=HEADS)
                    hd = xn[i].rearrange("p (h d) -> p h d", h=HEADS)
                    m = line.put(V.scalar_tensor_tensor(rstd[i][:, :].unsqueeze(2), sv[:, :, 64:65], 0.0, sv[:, :, 64:65], ALU.is_le, ALU.add))
                    yield True
                    line.need(m)
                    m = line.put(V.reciprocal(rstd[i][:, :], rstd[i][:, :]))
                    yield True
                    line.need(m)
                    m = line.put(V.tensor_tensor(hd, sv[:, :, 0:64], rstd[i][:, :].unsqueeze(2).to_broadcast([P, HEADS, 64]), ALU.mult))
                    yield True
                    if residual:
                        line.need(m)
                        m = line.put(V.tensor_tensor(xn[i], xn[i], big2[:, bass.ds((2 * k + i) * DIM, DIM)], ALU.add))
                        yield True
                    line.need(m)
                    m = line.put(V.tensor_tensor(xn[i], xn[i], bias, ALU.add))
                    yield True
                    line.need(m)
                    V.tensor_scalar(tmp2[i], xn[i], 0.0, None, ALU.min).then_inc(tile_sem("neg", i), 1)
                    yield True
                    dve.wait_ge(tile_sem("neg", i), tile_base(name, "neg") + k + 1)
                    m = line.put(V.tensor_scalar(xn[i], xn[i], 0.0, None, ALU.max))
                    yield True
                    line.need(m)
                    dve.wait_ge(tile_sem("exp", i), tile_base(name, "exp") + k + 1)
                    a = V.scalar_tensor_tensor(xn[i], tmp2[i], -1.0, xn[i], ALU.add, ALU.add)
                    if not residual:
                        a.then_inc(tile_sem("xn", i), 1)
                        yield True
                        dve.wait_ge(tile_sem("xn", i), tile_base(name, "xn") + k + 1)
                        line.put(V.tensor_tensor(big2[:, bass.ds((2 * k + i) * DIM, DIM)], xn[i], xn[i], ALU.max))
                    else:
                        m = line.put(a)
                        yield True
                        line.need(m)
                        dve.wait_ge(tile_sem("x_in", i), tile_base(name, "x_in") + k * 16 + 16)
                        V.tensor_tensor(tmp[i], xt[i], xn[i], ALU.add).then_inc(tile_sem("out_ready", i), 1)
                zipped(part)

            def credits(name):
                for i in range(2):
                    dve.sem_inc(tile_sem("out_free", i), 1)

            def first_gather(name, g):
                for i in range(2):
                    index_in(name, g, None, i, True)

            def last_gather(name):
                for i in range(2):
                    dve.wait_ge(tile_sem("x_in", i), tile_base(name, "x_in") + 16 * PAIRS + 16)

            layout("gnn")
            dve.wait_ge(S("constants_loaded"), 16 * 16)
            dve.wait_ge(S("list_order_in"), list_base("gnn", "order_in") + 16)
            credits("proj1")
            first_gather("proj1", "gnn")
            with dve.Fori(0, PAIRS) as k:
                line.enter(k, 2 * 8)
                norm("proj1", "gnn", k)
                for i in range(2):
                    dve.wait_ge(tile_sem("xn", i), tile_base("proj1", "xn") + k + 1)
                    dve.sem_inc(tile_sem("x_free", i), 1)
                    index("proj1", "gnn", k, i)
                rows("proj1", "gnn1", k)
                line.leave(PAIRS)
            line.settle()
            last_gather("proj1")
            line(V.memset(big1[:, :], 0.0))
            line(V.memset(top[:, :], NONE))
            walk("gnn1")
            dve.sem_inc(S("gnn1_walked"), 1)
            credits("proj2")
            with dve.Fori(0, PAIRS) as k:
                line.enter(k, 2 * 12)
                for i in range(2):
                    index("proj2", "gnn", k, i)
                aggregate("proj2", k, vecs[:, 2, :], False)
                rows("proj2", "gnn2", k)
                line.leave(PAIRS)
            line.settle()
            line(V.memset(big1[:, :], 0.0))
            line(V.memset(top[:, :], NONE))
            walk("gnn2")
            credits("fin2")
            first_gather("fin2", "gnn")
            with dve.Fori(0, PAIRS) as k:
                line.enter(k, 2 * 8)
                for i in range(2):
                    index("fin2", "gnn", k, i)
                aggregate("fin2", k, vecs[:, 5, :], True)
                for i in range(2):
                    dve.wait_ge(tile_sem("out_ready", i), tile_base("fin2", "out_ready") + k + 1)
                    dve.sem_inc(tile_sem("x_free", i), 1)
                    index_in("fin2", "gnn", k, i)
                line.leave(PAIRS)
            line.settle()
            last_gather("fin2")
            for i in range(2):
                dve.wait_ge(tile_sem("out", i), tile_base("fin2", "out") + 16 * PAIRS)
            dve.sem_inc(S("fin2_done"), 1)
            layout("ffn")
            dve.wait_ge(S("list_order_in"), list_base("ffn", "order_in") + 16)
            credits("projf")
            first_gather("projf", "ffn")
            with dve.Fori(0, PAIRS) as k:
                line.enter(k, 2 * 11)
                norm("projf", "ffn", k)
                for i in range(2):
                    index("projf", "ffn", k, i)
                rows("projf", "ffn", k)
                line.leave(PAIRS)
            line.settle()
            last_gather("projf")
            walk("ffn")
            sf = sums_f[:, :].rearrange("p (t h d) -> p t h d", t=TILES, h=HEADS)
            n16 = TILES * 16
            reg = ring_all[:, 0:SLOTS // 2]
            agg = reg[:, 0:n16]
            agg4 = agg.rearrange("p (t h e) -> p t h e", t=TILES, h=HEADS)
            agg3 = agg.rearrange("p (t c) -> p t c", t=TILES)
            sq = reg[:, n16:2 * n16]
            sq3 = sq.rearrange("p (t c) -> p t c", t=TILES)
            den = reg[:, 2 * n16:2 * n16 + TILES * HEADS].rearrange("p (t h) -> p t h", t=TILES)
            mean = reg[:, 2 * n16 + 200:2 * n16 + 250]
            std = tile_cols()
            sc = reg[:, 2 * n16 + 256:2 * n16 + 456]
            sc3 = sc.rearrange("p (t e) -> p t e", t=TILES)
            cmp_ = reg[:, n16:2 * n16].rearrange("p (t e j) -> p t e j", t=TILES, e=EXPERTS)
            g3 = gates[:, :].rearrange("p (t e) -> p t e", t=TILES)

            def cols(v):
                return v.unsqueeze(2).to_broadcast([P, TILES, 16])
            line(V.tensor_scalar(den.unsqueeze(3), sf[:, :, :, 4:5], 1e-16, None, ALU.add))
            line(V.reciprocal(den, den))
            for h in range(HEADS):
                line(V.tensor_tensor(agg4[:, :, h, :], sf[:, :, h, 0:4], den[:, :, h:h + 1].to_broadcast([P, TILES, 4]), ALU.mult))
            line(V.tensor_tensor(agg3, agg3, small[:, 2, :].unsqueeze(1).to_broadcast([P, TILES, 16]), ALU.add))
            line(V.tensor_reduce(mean, agg3, X, ALU.add))
            line(V.tensor_scalar(mean, mean, 1.0 / 16, None, ALU.mult))
            line(V.tensor_tensor(agg3, agg3, cols(mean), ALU.subtract))
            line(V.tensor_tensor(sq, agg, agg, ALU.mult))
            line(V.tensor_reduce(std, sq3, X, ALU.add))
            line(V.tensor_scalar(std, std, 1.0 / 16, None, ALU.mult))
            dve.sem_inc(S("gat_var"), 1)
            dve.wait_ge(S("gat_std"), 1)
            line(V.reciprocal(std, std))
            line(V.tensor_tensor(agg3, agg3, cols(std), ALU.mult))
            line(V.tensor_tensor(agg3, agg3, small[:, 3, :].unsqueeze(1).to_broadcast([P, TILES, 16]), ALU.mult))
            line(V.tensor_tensor(agg3, agg3, small[:, 4, :].unsqueeze(1).to_broadcast([P, TILES, 16]), ALU.add))
            line(V.tensor_reduce(sc3, agg4.rearrange("p t h e -> p t e h"), X, ALU.add))
            line(V.tensor_scalar(sc, sc, 0.25, None, ALU.mult))
            take = reg[:, 2 * n16 + 456:2 * n16 + 656].rearrange("p (t e) -> p t e", t=TILES)
            eq = reg[:, 0:n16].rearrange("p (t e j) -> p t e j", t=TILES, e=EXPERTS)
            for e in range(EXPERTS):
                line(V.tensor_tensor(cmp_[:, :, e, :], sc3, sc3[:, :, e:e + 1].to_broadcast([P, TILES, EXPERTS]), ALU.is_gt))
                if e:
                    line(V.tensor_tensor(eq[:, :, e, 0:e], sc3[:, :, 0:e], sc3[:, :, e:e + 1].to_broadcast([P, TILES, e]), ALU.is_equal))
                    line(V.tensor_tensor(cmp_[:, :, e, 0:e], cmp_[:, :, e, 0:e], eq[:, :, e, 0:e], ALU.add))
            line(V.tensor_reduce(take, cmp_, X, ALU.add))
            line(V.tensor_scalar(take, take, 2.0, None, ALU.is_lt))
            line(V.tensor_reduce(mean, sc3, X, ALU.max))
            line(V.tensor_tensor(g3, sc3, mean.unsqueeze(2).to_broadcast([P, TILES, EXPERTS]), ALU.subtract))
            dve.sem_inc(S("gat_top"), 1)
            dve.wait_ge(S("gat_exp"), 1)
            line(V.tensor_tensor(g3, g3, take, ALU.mult))
            line(V.tensor_reduce(mean, g3, X, ALU.add))
            line(V.reciprocal(mean, mean))
            line(V.tensor_tensor(g3, g3, mean.unsqueeze(2).to_broadcast([P, TILES, EXPERTS]), ALU.mult))
            credits("mix")
            with dve.Fori(0, PAIRS) as k:
                line.enter(k, 2 + 2 * (EXPERTS - 1))

                def mixed(i):
                    dve.wait_ge(S(f"y_in{i}"), k * 16 + 16)
                    for e in range(EXPERTS):
                        prev = big1[:, bass.ds((2 * k + i) * DIM, DIM)] if e == 0 else yout[i]
                        a = V.scalar_tensor_tensor(yout[i], y_back[i][:, e * DIM:(e + 1) * DIM], gates[:, bass.ds((2 * k + i) * EXPERTS + e, 1)],
                                                   prev, ALU.mult, ALU.add)
                        if e < EXPERTS - 1:
                            m = line.put(a)
                            yield
                            line.need(m)
                        else:
                            a.then_inc(tile_sem("out_ready", i), 1)
                            yield
                for i in range(2):
                    index("mix", "ffn", k, i)
                zipped(mixed)
                for i in range(2):
                    dve.wait_ge(tile_sem("out_ready", i), tile_base("mix", "out_ready") + k + 1)
                    dve.sem_inc(S(f"y_used{i}"), 1)
                line.leave(PAIRS)
            line.settle()


NAMES = ["x", "gnn_src", "gnn_dst", "ffn_src", "ffn_dst", "L0_gnn_W1", "L0_gnn_al1", "L0_gnn_ar1", "L0_gnn_b1",
         "L0_gnn_W2", "L0_gnn_al2", "L0_gnn_ar2", "L0_gnn_b2", "L0_ffn_W_gat", "L0_ffn_att_src", "L0_ffn_att_dst",
         "L0_ffn_b_gat", "L0_ffn_ln_gamma", "L0_ffn_ln_beta", "L0_ffn_W1", "L0_ffn_b1", "L0_ffn_W2", "L0_ffn_b2"]


def kernel(**inputs):
    import numpy as np
    import concourse.bacc as bacc
    from concourse import mybir as mb
    from concourse.bass_utils import run_bass_kernel_spmd

    def padded(a, n, fill):
        a = np.asarray(a)
        return np.concatenate([a, np.full((n - a.shape[0],) + a.shape[1:], fill, a.dtype)])

    a = {k: np.asarray(v) for k, v in inputs.items()}
    edges = a.pop("L0_ffn_edge_index")
    a["x"] = padded(a["x"], SLOTS, 0)
    a["gnn_src"] = padded(a.pop("src"), GROUPS["gnn"] * GROUP, 0)
    a["gnn_dst"] = padded(a.pop("dst"), GROUPS["gnn"] * GROUP, BIG_KEY)
    a["ffn_src"], a["ffn_dst"] = edges[0], edges[1]
    for n in ("L0_gnn_al1", "L0_gnn_ar1", "L0_gnn_al2", "L0_gnn_ar2", "L0_ffn_att_src", "L0_ffn_att_dst"):
        a[n] = a[n].reshape(-1)

    nc = bacc.Bacc("TRN2", target_bir_lowering=False, num_devices=1)
    arrays, aps = {}, {}
    for n in NAMES:
        v = np.ascontiguousarray(a[n])
        arrays[f"in_{n}"] = v
        aps[n] = nc.dram_tensor(f"in_{n}", v.shape, mb.dt.from_np(v.dtype), kind="ExternalInput").ap()
    out = nc.dram_tensor("result", (NODES, DIM), mb.dt.float32, kind="ExternalOutput").ap()
    build(nc, aps, out)
    r = run_bass_kernel_spmd(nc, [arrays], core_ids=[0])
    return r.results[0]["result"]
```

```python
import concourse.bass as bass
from concourse import mybir
from contextlib import ExitStack

FP = mybir.dt.float32
BF = mybir.dt.bfloat16
I32 = mybir.dt.int32
U32 = mybir.dt.uint32
ALU = mybir.AluOpType
ACT = mybir.ActivationFunctionType
X = mybir.AxisListType.X

P = 128
NODES = 6250
TILES = 50
PAIRS = TILES // 2
SLOTS = TILES * P
DUMMY = SLOTS
HEADS = 4
DIM = 256
CHUNKS = 8
GROUP = CHUNKS * P
E_GNN, E_FFN = 106250, 131072
GROUPS = {"gnn": 104, "ffn": 128}
ROUNDS = 4
STEPS = 4
STEP_COLS = 264
MAX_STEPS = P * STEP_COLS
FILL = 64
BIG_KEY = 8191
NONE = -1.0e30
EPS = 1e-5
EXPERTS, HID = 4, 512
FCH = HID // P


def width(d):
    return HEADS * (d + 1)


class Line:

    def __init__(self, eng, sem, spare):
        self.eng, self.sem, self.spare, self.at, self.k, self.per = eng, sem, spare, 0, None, 0

    def put(self, ins):
        ins.then_inc(self.sem, 1)
        self.at += 1
        return self.at

    def need(self, mark):
        self.eng.wait_ge(self.sem, mark if self.k is None else self.k * self.per + mark)

    def __call__(self, ins):
        self.need(self.put(ins))

    def hold(self, ins):
        self(ins)
        self.eng.sem_inc(self.spare, 1)

    def enter(self, k, per):
        assert self.k is None
        self.k, self.per, self.base = k, per, self.at

    def leave(self, trips):
        assert self.at - self.base == self.per, (self.at, self.base, self.per)
        self.k = None
        self.at = self.base + self.per * trips if trips is not None else None

    def settle(self):
        self.need(self.at)


def build(nc, t, out):
    ctx = ExitStack()
    with ctx:
        def sb(name, shape, dt=FP):
            return ctx.enter_context(nc.sbuf_tensor(name, shape, dt))

        def dram(name, shape, dt=FP):
            return nc.dram_tensor(name, shape, dt, kind="Internal").ap()

        sems = {}

        def S(name):
            if name not in sems:
                sems[name] = ctx.enter_context(nc.semaphore(name))
            return sems[name]

        tile_uses = {"index": (["proj1", "proj2", "fin2", "projf", "mix"], PAIRS), "x_in": (["proj1", "fin2", "projf"], 16 * PAIRS + 16),
                     "index_in": (["proj1", "fin2", "projf"], PAIRS + 1),
                     "x_free": (["proj1", "fin2", "projf"], PAIRS), "out_ready": (["proj1", "proj2", "fin2", "projf", "mix"], PAIRS),
                     "out": (["proj1", "proj2", "fin2", "projf", "mix"], 16 * PAIRS),
                     "var": (["proj1", "projf"], PAIRS), "std": (["proj1", "projf"], PAIRS),
                     "neg": (["proj2", "fin2"], PAIRS), "exp": (["proj2", "fin2"], PAIRS),
                     "xn": (["proj1", "proj2", "projf"], PAIRS), "T": (["proj1", "proj2", "projf"], PAIRS),
                     "T_copied": (["proj1", "proj2", "projf"], PAIRS), "feat": (["proj1", "proj2", "projf"], PAIRS)}

        phase_of = {"gnn1": 0, "gnn2": 1, "ffn": 2}

        def bodies(eng, L):
            most = MAX_STEPS // STEPS - 1
            g = layers[L]["g"]
            n = eng.value_load(counts[g][0:1, 0:1], min_val=least_bodies[g], max_val=most)
            if L == "gnn1":
                return 0, n
            if L == "gnn2":
                return n, n
            return eng.value_load(counts["gnn"][0:1, 0:1], min_val=least_bodies["gnn"], max_val=most) * 2, n

        def tile_sem(kind, i):
            return S(f"tile_{kind}{i}")

        def tile_base(name, kind):
            names, each = tile_uses[kind]
            return names.index(name) * each + (16 if kind == "out" else 0)

        half = GROUPS["gnn"] // 2
        list_adds = dict(dst_in=16, src_in=16, lo_ready=1, lo_out=16, keyT_ready=1, key_out=16, keyB_in=16, order_out=16 * (TILES - 2),
                         order_in=16, counts_ready=1, steps_out=16, row_in=16 * half, row_used=half, slot_out=16 + 16 * CHUNKS * half,
                         slots_done=1, scattered=1, ranked=1, hist_done=1, hot_ready=2 * half, hot_used=half + 1,
                         key_ready=1, keyT=1, steps_ready=1, tb=1, base_ready=1, counted=1 + 2 * half * CHUNKS, loT=2 * half,
                         same_ps=half, hot2_ready=4 * half, looked=half + 1, copied=2 * half * CHUNKS, act_ranked=1, step_tiles=1, maxT=1, maxT_ps=1, placed=half)

        def list_base(g, kind):
            return 0 if g == "gnn" else list_adds[kind]

        def hold(eng, sem, value):
            eng.wait_ge(sem, value)
            eng.sem_inc(S("spare_" + eng_name[id(eng)]), 1)

        eng_name = {}

        G = ["gnn", "ffn"]
        lo_dram = {g: dram(f"{g}_lo", [GROUPS[g] * GROUP], BF) for g in G}
        key_dram = {g: dram(f"{g}_key", [SLOTS]) for g in G}
        order_dram = {g: dram(f"{g}_order", [SLOTS, 1], I32) for g in G}
        step_dram = {g: dram(f"{g}_step_tile", [MAX_STEPS], I32) for g in G}
        slot_dram = {g: dram(f"{g}_slots", [MAX_STEPS * ROUNDS * P, 1], I32) for g in G}
        table = {"gnn1": dram("table1", [SLOTS + 1, width(64) + 4]),
                 "gnn2": dram("table2", [SLOTS + 1, width(64) + 4]),
                 "ffn": dram("table3", [SLOTS + 1, width(4) + 4])}
        y_dram = dram("expert_outputs", [TILES, P, EXPERTS * DIM])
        x2_dram = dram("x2", [SLOTS, DIM])

        big1 = sb("big1", [P, TILES * width(64)])
        big2 = sb("big2", [P, TILES * DIM])
        region = sb("region", [P, 12600])
        wpair = sb("wpair", [P, 2, 2, DIM])
        wgat = sb("wgat", [P, 2, 16])
        vecs = sb("vecs", [P, 6, DIM])
        small = sb("small", [P, 5, 16])
        b1cols = sb("b1cols", [P, EXPERTS * FCH])
        b2rows = sb("b2rows", [1, EXPERTS, DIM])
        ones_row = sb("ones_row", [1, P])
        iota_i = sb("iota_i", [P, P], I32)
        iota_f = sb("iota_f", [P, P])
        iota_b = sb("iota_b", [P, P], BF)
        part_i = sb("part_i", [P, 1], I32)
        part_f = sb("part_f", [P, 1])
        before = sb("before", [P, P])
        ident = sb("ident", [P, P])
        zero_b = sb("zero_b", [P, P], BF)
        nkey = sb("nkey", [P, TILES])
        nkey_i = sb("nkey_i", [P, TILES], I32)
        dummy = sb("dummy_index", [P, FILL * ROUNDS], I32)
        dummy_row = sb("dummy_row", [1, width(64) + 4])
        dummy_row_f = sb("dummy_row_f", [1, width(4) + 4])
        rank = sb("rank", [P, TILES])
        order = {g: sb(f"{g}_order_sb", [P, TILES + 2], I32) for g in G}
        counts = {g: sb(f"{g}_counts", [P, 2], I32) for g in G}
        er = sb("er", [P, TILES * HEADS])
        top = sb("top", [P, TILES * HEADS])
        sums_f = sb("sums_f", [P, TILES * width(4)])
        gates = sb("gates", [P, TILES * EXPERTS])
        ring_all = sb("ring", [P, STEPS * ROUNDS * (width(64) + 4)])
        ring_cols = ROUNDS * (width(64) + 4)
        ring = [ring_all[:, s * ring_cols:(s + 1) * ring_cols].rearrange("p (r w) -> p r w", r=ROUNDS) for s in range(STEPS)]
        ACT_RANKS = {"gnn": 28, "ffn": 34}
        HIST_BODIES = GROUPS["ffn"] // STEPS
        KEY_BODIES = 2
        DVE_RANK_BODIES = TILES - ACT_RANKS["ffn"]
        ACT_RANK_BODIES = ACT_RANKS["ffn"] // 2
        TURN = 4
        assert HIST_BODIES % TURN == DVE_RANK_BODIES % TURN == 0
        least_bodies = {"gnn": HIST_BODIES + KEY_BODIES + max(DVE_RANK_BODIES, ACT_RANK_BODIES) + 1, "ffn": TILES + 1}
        prod_all = sb("prod", [P, 2, ROUNDS, width(64)])
        prod = [prod_all[:, i, :, :] for i in range(2)]
        part_sum = sb("part_sum", [P, width(64)])
        escore = [sb(f"escore{s}", [P, ROUNDS + 1, HEADS]) for s in range(STEPS)]
        eprob = [sb(f"eprob{s}", [P, ROUNDS + 1, HEADS]) for s in range(STEPS)]
        zbuf = sb("zbuf", [P, ROUNDS, HEADS])
        tmax = sb("tmax", [P, HEADS])
        idx = [sb(f"idx{h}", [P, 2 * ROUNDS], I32) for h in range(2)]
        tid = [sb(f"tid{h}", [1, 2], I32) for h in range(2)]
        xt, xn, tmp, tmp2 = ([ring_all[:, (2 * n + i) * DIM:(2 * n + i + 1) * DIM] for i in range(2)] for n in range(4))
        xnT = [ring_all[:, (8 + i) * DIM:(9 + i) * DIM].rearrange("p (k n) -> p k n", k=2) for i in range(2)]
        rtmp = [ring_all[:, (10 + i) * DIM:(11 + i) * DIM] for i in range(2)]
        er_new = [sb(f"er_new{i}", [P, HEADS]) for i in range(2)]
        row = [sb(f"row{i}", [P, width(64) + 4]) for i in range(2)]
        row_f = [sb(f"row_f{i}", [P, width(4) + 4]) for i in range(2)]
        gi = [sb(f"gi{i}", [P, 1], I32) for i in range(2)]
        gi_in = [sb(f"gi_in{i}", [P, 1], I32) for i in range(2)]
        stats = [sb(f"stats{i}", [P, 6]) for i in range(2)]
        mv = [sb(f"mv{i}", [P, 2]) for i in range(2)]
        rstd = [sb(f"rstd{i}", [P, HEADS]) for i in range(2)]
        eps_col = sb("eps_col", [P, 1])

        at = [0]

        def carve(cols_fp, dt=FP):
            a = at[0]
            at[0] += cols_fp
            v = region[:, a:a + cols_fp]
            return v if dt == FP else v.bitcast(dt)
        MG = max(GROUPS.values()) * CHUNKS
        dst_i = carve(MG, I32)
        src_i = carve(MG, I32)
        off_f = carve(MG)
        hi_b = carve(MG // 2, BF)
        lo_b = carve(MG // 2, BF)
        tmp_i = carve(MG, I32)
        step_f = big2[:, 0:STEP_COLS]
        step_acc = big2[:, STEP_COLS:2 * STEP_COLS]
        step_i = big2[:, 2 * STEP_COLS:3 * STEP_COLS].bitcast(I32)
        junk_act = region[:, at[0]:at[0] + SLOTS // 2].bitcast(BF)
        junk = region[:, at[0] + SLOTS // 2:at[0] + SLOTS].bitcast(BF)
        junk_end = at[0] + SLOTS
        lo_row = [carve(GROUP // 2, BF) for _ in range(2)]
        lo_T = [carve(GROUP) for _ in range(2)]
        one_lo = [carve(CHUNKS * P // 2, BF).rearrange("p (j c) -> p j c", c=P) for _ in range(2)]
        one_hi = [carve(CHUNKS * TILES // 2, BF).rearrange("p (j c) -> p j c", c=TILES) for _ in range(2)]
        same = [carve(GROUP // 2, BF).rearrange("p (j c) -> p j c", c=P) for _ in range(2)]
        count_sb = [carve(TILES) for _ in range(CHUNKS)]
        pick = carve(CHUNKS * TILES)
        found = carve(CHUNKS)
        ints = [carve(CHUNKS, I32) for _ in range(5)]
        slot_st = [carve(CHUNKS, I32) for _ in range(2)]
        src_st = [carve(CHUNKS, I32) for _ in range(2)]
        assert at[0] >= junk_end
        key = carve(TILES)
        neg_key = carve(TILES)
        deg = carve(TILES)
        rank_i = carve(TILES, I32)
        node_no = carve(TILES, I32)
        tile_f = carve(TILES)
        place_f = carve(TILES)
        base = carve(TILES)
        tb = carve(TILES + 1)
        keyT = carve(P)
        maxdeg = carve(1)
        steps_i = carve(1, I32)
        steps_f = carve(1)
        steps_b = carve(P)
        total_i = carve(1, I32)
        assert at[0] <= 12600, at[0]
        keyB = big2[:, 0:SLOTS]
        lo_Tb = [big2[:, (1 + i) * GROUP:(1 + i) * GROUP + GROUP // 2].bitcast(BF) for i in range(2)]
        rank_parts = sums_f[:, 0:STEPS * TILES].rearrange("p (q t) -> p q t", q=STEPS)
        spread, in_tile = (big2[:, SLOTS + n * TILES * TILES:SLOTS + (n + 1) * TILES * TILES].rearrange("p (n t) -> p n t", t=TILES)
                           for n in range(2))
        w1_sb = region[:, 0:EXPERTS * 2 * HID].rearrange("p (e k f) -> p e k f", e=EXPERTS, k=2)
        w2_sb = region[:, 4096:4096 + EXPERTS * FCH * DIM].rearrange("p (e f n) -> p e f n", e=EXPERTS, f=FCH)
        hT = [region[:, 8192 + e * HID:8192 + (e + 1) * HID].rearrange("p (f n) -> p f n", f=FCH) for e in range(EXPERTS)]
        y_keep = [region[:, 8192 + EXPERTS * HID + h * 2 * DIM:8192 + EXPERTS * HID + (h + 1) * 2 * DIM] for h in range(2)]
        y_back = [region[:, j * EXPERTS * DIM:(j + 1) * EXPERTS * DIM] for j in range(4)]
        yacc, yout = ([prod_all[:, i, r, 0:DIM] for i in range(2)] for r in range(2))

        bank = [ctx.enter_context(nc.psum_tensor(f"bank{b}", [P, 512], FP)) for b in range(8)]
        run_ps = bank[0][:, 0:TILES]
        hist_ps = bank[7][:, 0:TILES]

        layers = {
            "gnn1": dict(g="gnn", d=64, sums=big1, ring=ring, row=row, al=vecs[:, 0, :], ar=vecs[:, 1, :]),
            "gnn2": dict(g="gnn", d=64, sums=big1, ring=ring, row=row, al=vecs[:, 3, :], ar=vecs[:, 4, :]),
            "ffn": dict(g="ffn", d=4, sums=sums_f, ring=[ring_all[:, s * ring_cols:s * ring_cols + ROUNDS * 24].rearrange("p (r w) -> p r w", r=ROUNDS) for s in range(STEPS)], row=row_f, al=small[:, 0, :], ar=small[:, 1, :]),
        }
        def tile_cols():
            return er[:, 0:TILES]

        block = ctx.enter_context(nc.Block())

        @block.sync
        def _(sp):
            eng_name[id(sp)] = "sp"
            cst = S("constants_loaded")
            for i, n in enumerate(["L0_gnn_al1", "L0_gnn_ar1", "L0_gnn_b1", "L0_gnn_al2", "L0_gnn_ar2", "L0_gnn_b2"]):
                sp.dma_start(vecs[:, i, :], t[n].partition_broadcast(P)).then_inc(cst, 16)
            for i, n in enumerate(["L0_ffn_att_src", "L0_ffn_att_dst", "L0_ffn_b_gat", "L0_ffn_ln_gamma", "L0_ffn_ln_beta"]):
                sp.dma_start(small[:, i, :], t[n].partition_broadcast(P)).then_inc(cst, 16)
            sp.dma_start(wpair[:, 0, :, :], t["L0_gnn_W1"].rearrange("(k p) n -> p k n", p=P)).then_inc(cst, 16)
            sp.dma_start(wpair[:, 1, :, :], t["L0_gnn_W2"].rearrange("(k p) n -> p k n", p=P)).then_inc(cst, 16)
            sp.dma_start(wgat[:, :, :], t["L0_ffn_W_gat"].rearrange("(k p) n -> p k n", p=P)).then_inc(cst, 16)
            sp.dma_start(b2rows[:, :, :], t["L0_ffn_b2"].rearrange("(o e) n -> o e n", o=1)).then_inc(cst, 16)
            with nc.allow_non_contiguous_dma(reason="a bias column per hidden chunk, 8 KB in all"):
                sp.dma_start(b1cols[:, :], t["L0_ffn_b1"].rearrange("e (f p) -> p (e f)", p=P)).then_inc(cst, 16)
            sp.wait_ge(S("consts"), 1)
            sp.dma_start(table["ffn"][DUMMY:DUMMY + 1, :], dummy_row_f[:, :]).then_inc(S("dummies_out"), 16)

            def lists_in(g):
                ng = GROUPS[g]
                if g == "ffn":
                    sp.wait_ge(S("list_scattered"), list_base("gnn", "scattered") + 1)
                sp.dma_start(dst_i[:, 0:ng * CHUNKS].rearrange("p (g j) -> p g j", j=CHUNKS),
                             t[g + "_dst"].rearrange("(g p j) -> p g j", p=P, j=CHUNKS)).then_inc(S("list_dst_in"), 16)
                sp.dma_start(src_i[:, 0:ng * CHUNKS].rearrange("p (g j) -> p g j", j=CHUNKS),
                             t[g + "_src"].rearrange("(g p j) -> p g j", p=P, j=CHUNKS)).then_inc(S("list_src_in"), 16)

            def lows_out(g):
                ng = GROUPS[g]
                sp.wait_ge(S("list_lo_ready"), list_base(g, "lo_ready") + 1)
                sp.dma_start(lo_dram[g].rearrange("(g p j) -> p g j", p=P, j=CHUNKS),
                             lo_b[:, 0:ng * CHUNKS].rearrange("p (g j) -> p g j", j=CHUNKS)).then_inc(S("list_lo_out"), 16)
                sp.wait_ge(S("list_lo_out"), list_base(g, "lo_out") + 16)

            def keys(g):
                sp.wait_ge(S("list_keyT_ready"), list_base(g, "keyT_ready") + 1)
                sp.dma_start(key_dram[g].rearrange("(t p) -> t p", p=P), keyT[0:TILES, :]).then_inc(S("list_key_out"), 16)
                sp.wait_ge(S("list_key_out"), list_base(g, "key_out") + 16)
                sp.dma_start(keyB, key_dram[g].partition_broadcast(P)).then_inc(S("list_keyB_in"), 16)

            def before_placing(g):
                sp.wait_ge(S("list_counts_ready"), list_base(g, "counts_ready") + 1)
                fills = sp.value_load(counts[g][0:1, 1:2], min_val=2, max_val=MAX_STEPS // FILL)
                view = slot_dram[g].rearrange("(k p f) o -> k p (f o)", p=P, f=FILL * ROUNDS)
                with sp.Fori(0, fills) as k:
                    sp.dma_start(view[bass.ds(k, 1), :, :].rearrange("k p f -> (k p) f"), dummy[:, :]).then_inc(S(g + "_filled"), 16)
                lows = lo_dram[g].rearrange("(g n) -> g n", n=GROUP)
                for i in range(2):
                    sp.dma_start(lo_row[i], lows[i:i + 1, :].to_broadcast([P, GROUP])).then_inc(S(f"list_row_in{i}"), 16)
                sp.wait_ge(S("list_order_out"), list_base(g, "order_out") + 16 * (TILES - 2))
                for i in range(2):
                    sp.wait_ge(S(f"list_slot_out{i}"), list_base(g, "slot_out") + 16)
                with nc.allow_non_contiguous_dma(reason="6400 numbers"):
                    sp.dma_start(order[g][:, 0:TILES], order_dram[g].rearrange("(t p) c -> p (t c)", p=P)).then_inc(S("list_order_in"), 16)

            def placing(g):
                ng = GROUPS[g]
                lows = lo_dram[g].rearrange("(g n) -> g n", n=GROUP)
                with sp.Fori(0, ng // 2 - 1) as k:
                    for i in range(2):
                        hold(sp, S(f"list_row_used{i}"), list_base(g, "row_used") + k + 1)
                        sp.dma_start(lo_row[i], lows[bass.ds(2 * k + (2 + i), 1), :].to_broadcast([P, GROUP])).then_inc(S(f"list_row_in{i}"), 16)
                sp.wait_ge(S("list_step_tiles"), list_base(g, "step_tiles") + 1)
                sp.dma_start(step_dram[g].rearrange("(p f) -> p f", p=P), step_i).then_inc(S("list_steps_out"), 16)

            def walk(L):
                c = layers[L]
                g = c["g"]
                sp.wait_ge(S("list_slots_done"), list_base(g, "slots_done") + 1)
                slots = slot_dram[g].rearrange("(s p r) o -> s p (r o)", p=P, r=2 * ROUNDS)
                tiles = step_dram[g].rearrange("(s c) -> s c", c=2)

                def load_sources(h, s):
                    sp.dma_start(idx[h][:, :], slots[s, :, :].rearrange("s p r -> (s p) r")).then_inc(S(f"walk_idx_in{h}"), 16)

                def load_tiles(h, s):
                    sp.dma_start(tid[h][:, :], tiles[s, :]).then_inc(S(f"walk_tid_in{h}"), 16)
                if L == "gnn2":
                    sp.wait_ge(S("gnn1_walked"), 1)
                for h in range(2):
                    load_sources(h, slice(h, h + 1))
                    load_tiles(h, slice(h, h + 1))
                done, n = bodies(sp, L)
                with sp.Fori(0, n) as k:
                    for h in range(2):
                        for s in (2 * h, 2 * h + 1):
                            hold(sp, S(f"walk_rows_in{s}"), (done + k) * (16 * ROUNDS) + 16 * ROUNDS)
                        load_sources(h, bass.ds(2 * k + (2 + h), 1))
                        hold(sp, S(f"walk_tid_read{h}"), done + k + 1)
                        load_tiles(h, bass.ds(2 * k + (2 + h), 1))
                for h in range(2):
                    hold(sp, S(f"walk_idx_in{h}"), (done + n) * 16 + 16 * (phase_of[L] + 1))
                    hold(sp, S(f"walk_tid_in{h}"), (done + n) * 16 + 16 * (phase_of[L] + 1))
            lists_in("gnn")
            lows_out("gnn")
            keys("gnn")
            before_placing("gnn")
            placing("gnn")
            lists_in("ffn")
            lows_out("ffn")
            walk("gnn1")
            before_placing("ffn")
            walk("gnn2")
            placing("ffn")
            sp.wait_ge(S("list_scattered"), list_base("ffn", "scattered") + 1)
            sp.dma_start(w1_sb, t["L0_ffn_W1"].rearrange("e (k p) f -> p e k f", p=P)).then_inc(S("experts_in"), 16)
            sp.dma_start(w2_sb, t["L0_ffn_W2"].rearrange("e (f p) n -> p e f n", p=P)).then_inc(S("experts_in"), 16)
            walk("ffn")
            sp.wait_ge(S("experts_done"), 1)
            def outputs_in(j, tile):
                sp.dma_start(y_back[j], y_dram[tile, :, :].rearrange("t p n -> (t p) n")).then_inc(S(f"y_in{j}"), 16)
            for j in range(4):
                outputs_in(j, slice(j, j + 1))
            with sp.Fori(0, TILES // 4 - 1) as k:
                for j in range(4):
                    hold(sp, S(f"y_used{j}"), k + 1)
                    outputs_in(j, bass.ds(4 * k + (4 + j), 1))
            for j in range(2):
                sp.wait_ge(S(f"y_used{j}"), TILES // 4)
                outputs_in(j, slice(TILES - 2 + j, TILES - 1 + j))

        @block.gpsimd
        def _(pool):
            eng_name[id(pool)] = "pool"
            line = Line(pool, S("pool_line"), S("spare_pool"))
            line(pool.iota(iota_i[:, :], [[1, P]], base=0, channel_multiplier=0))
            line(pool.iota(part_i[:, :], [[0, 1]], base=0, channel_multiplier=1))
            line(pool.iota(nkey_i[:, :], [[-P, TILES]], base=BIG_KEY, channel_multiplier=-1))
            line(pool.memset(dummy[:, :], DUMMY))
            pool.sem_inc(S("iotas"), 1)
            line(pool.memset(big1[:, :], 0.0))
            pool.sem_inc(S("sums_clear"), 1)
            pool.wait_ge(S("consts"), 1)
            for i, n in enumerate(["gnn1", "gnn2"]):
                pool.dma_start(table[n][DUMMY:DUMMY + 1, :], dummy_row[:, :]).then_inc(tile_sem("out", i), 16)

            def gather(tile, tab, index, sem):
                pool.indirect_dma_start(tile, None, tab, bass.IndirectOffsetOnAxis(ap=index.bitcast(U32), axis=0)).then_inc(sem, 16)

            def scatter(tab, index, tile, sem, bound=None):
                kw = {} if bound is None else dict(bounds_check=bound, oob_is_err=False)
                pool.indirect_dma_start(tab, bass.IndirectOffsetOnAxis(ap=index.bitcast(U32), axis=0), tile, None, **kw).then_inc(sem, 16)

            def ordering(g):
                pool.wait_ge(S("list_ranked"), list_base(g, "ranked") + 1)
                for n in range(TILES):
                    scatter(order_dram[g], rank_i[:, n:n + 1], node_no[:, n:n + 1], S(f"list_slot_out{n}" if n < 2 else "list_order_out"))

            def placing(g):
                pool.wait_ge(S("list_counts_ready"), list_base(g, "counts_ready") + 1)
                fills = pool.value_load(counts[g][0:1, 1:2], min_val=2, max_val=MAX_STEPS // FILL)
                hold(pool, S(g + "_filled"), fills * 16)
                with pool.Fori(0, GROUPS[g] // 2) as k:
                    for i in range(2):
                        hold(pool, S(f"list_placed{i}"), list_base(g, "placed") + k + 1)
                        for j in range(CHUNKS):
                            scatter(slot_dram[g], slot_st[i][:, j:j + 1], src_st[i][:, j:j + 1], S(f"list_slot_out{i}"),
                                    MAX_STEPS * ROUNDS * P - 1)
                for i in range(2):
                    pool.wait_ge(S(f"list_slot_out{i}"), list_base(g, "slot_out") + 16 + 16 * CHUNKS * GROUPS[g] // 2)
                pool.sem_inc(S("list_scattered"), 1)
                pool.wait_ge(S("list_steps_out"), list_base(g, "steps_out") + 16)
                pool.sem_inc(S("list_slots_done"), 1)

            def walk(L):
                c = layers[L]
                g = c["g"]
                done, n = bodies(pool, L)
                with pool.Fori(0, n) as k:
                    for s in range(STEPS):
                        if s % 2 == 0:
                            hold(pool, S(f"walk_idx_in{s // 2}"), (done + k) * 16 + 16 * (phase_of[L] + 1))
                        hold(pool, S(f"walk_rows_free{s}"), done + k + (phase_of[L] + 1))
                        for r in range(ROUNDS):
                            gather(c["ring"][s][:, r, :], table[L], idx[s // 2][:, (s % 2) * ROUNDS + r:(s % 2) * ROUNDS + r + 1],
                                   S(f"walk_rows_in{s}"))

            def tiles_loop(name, source, target, tiles_out, bound=None, ahead=2):
                def read(k):
                    for i in range(2):
                        hold(pool, tile_sem("index_in", i), tile_base(name, "index_in") + (k + 1))
                        if not isinstance(k, int) or k:
                            hold(pool, tile_sem("x_free", i), tile_base(name, "x_free") + k)
                        gather(xt[i], source, gi_in[i][:, :], tile_sem("x_in", i))

                def write(k):
                    for i in range(2):
                        hold(pool, tile_sem("index", i), tile_base(name, "index") + (k + 1))
                        hold(pool, tile_sem("out_ready", i), tile_base(name, "out_ready") + (k + 1))
                        scatter(target, gi[i][:, :], tiles_out[i] if isinstance(tiles_out[i], bass.AP) else tiles_out[i][:, :],
                                tile_sem("out", i), bound)
                if source is None:
                    with pool.Fori(0, PAIRS) as k:
                        write(k)
                else:
                    for k in range(ahead):
                        read(k)
                    with pool.Fori(0, PAIRS + 1 - ahead) as k:
                        read(k + ahead)
                        write(k)
                    if ahead == 2:
                        write(PAIRS - 1)
                for i in range(2):
                    pool.wait_ge(tile_sem("out", i), tile_base(name, "out") + 16 * PAIRS)

            ordering("gnn")
            placing("gnn")
            pool.wait_ge(S("dummies_out"), 16)
            tiles_loop("proj1", t["x"], table["gnn1"], row)
            walk("gnn1")
            ordering("ffn")
            tiles_loop("proj2", None, table["gnn2"], row)
            walk("gnn2")
            tiles_loop("fin2", t["x"], x2_dram, tmp, ahead=1)
            placing("ffn")
            tiles_loop("projf", x2_dram, table["ffn"], row_f)
            walk("ffn")
            tiles_loop("mix", None, out, yout, NODES - 1)

        @block.scalar
        def _(act):
            eng_name[id(act)] = "act"
            act_line = Line(act, S("act_line"), S("spare_act"))

            def rank_tile(n, keys=slice(0, SLOTS), to=rank):
                return act.activation(junk_act[:, keys], keyB[:, keys], ACT.Sign, bias=neg_key[:, n], accum_out=to[:, n])

            def ranking(g):
                act.wait_ge(S("list_keyB_in"), list_base(g, "keyB_in") + 16)
                act.wait_ge(S("list_key_ready"), list_base(g, "key_ready") + 1)
                for n in range(ACT_RANKS[g]):
                    act_line(rank_tile(slice(n, n + 1)))
                act.sem_inc(S("list_act_ranked"), 1)

            def placing(g):
                with act.Fori(0, GROUPS[g] // 2) as k:
                    for i in range(2):
                        for j in range(CHUNKS):
                            act.wait_ge(S("list_counted"), list_base(g, "counted") + (k * 2 + i) * CHUNKS + (j + 1))
                            act.activation(count_sb[j], run_ps, ACT.Copy).then_inc(S("list_copied"), 1)

            def probabilities(b, s):
                act.wait_ge(S(f"walk_scores{s}"), b + 1)
                act.activation(eprob[s][:, :, :], escore[s][:, :, :], ACT.Exp).then_inc(S(f"walk_probs{s}"), 1)

            def first_walk():
                _, n = bodies(act, "gnn1")
                g = "ffn"
                with act.Fori(0, HIST_BODIES) as k:
                    for s in range(STEPS):
                        probabilities(k, s)
                act.wait_ge(S("list_keyT_ready"), list_base(g, "keyT_ready") + 1)
                act.dma_start(key_dram[g].rearrange("(t p) -> t p", p=P), keyT[0:TILES, :]).then_inc(S("list_key_out"), 16)
                act.wait_ge(S("list_key_out"), list_base(g, "key_out") + 16)
                act.dma_start(keyB, key_dram[g].partition_broadcast(P)).then_inc(S("list_keyB_in"), 16)
                at = HIST_BODIES
                with act.Fori(0, KEY_BODIES) as k:
                    for s in range(STEPS):
                        probabilities(k + at, s)
                at += KEY_BODIES
                act.wait_ge(S("list_keyB_in"), list_base(g, "keyB_in") + 16)
                act.wait_ge(S("list_key_ready"), list_base(g, "key_ready") + 1)
                with act.Fori(0, ACT_RANK_BODIES) as k:
                    act_line.enter(k, STEPS)
                    for s in range(STEPS):
                        probabilities(k + at, s)
                        act_line.hold(rank_tile(bass.ds(2 * k + s // 2, 1), slice((s % 2) * SLOTS // 2, (s % 2 + 1) * SLOTS // 2), rank_parts[:, s % 2, :]))
                    act_line.leave(ACT_RANK_BODIES)
                act_line.settle()
                act.sem_inc(S("list_act_ranked"), 1)
                at += ACT_RANK_BODIES
                with act.Fori(0, n - at) as k:
                    for s in range(STEPS):
                        probabilities(k + at, s)

            def walk(L):
                done, n = bodies(act, L)
                with act.Fori(0, n) as k:
                    for s in range(STEPS):
                        probabilities(done + k, s)

            def roots(name, k):
                for i in range(2):
                    act.wait_ge(tile_sem("var", i), tile_base(name, "var") + (k + 1))
                    act.activation(rstd[i][:, 0:1], mv[i][:, 1:2], ACT.Sqrt, bias=eps_col[:, :]).then_inc(tile_sem("std", i), 1)

            def exponentials(name, k):
                for i in range(2):
                    act.wait_ge(tile_sem("neg", i), tile_base(name, "neg") + (k + 1))
                    act.activation(tmp2[i][:, :], tmp2[i][:, :], ACT.Exp).then_inc(tile_sem("exp", i), 1)

            def copies(name, k):
                for i in range(2):
                    hold(act, tile_sem("T", i), tile_base(name, "T") + (k + 1))
                    act.activation(xnT[i][:, :, :], bank[i][:, 0:DIM].rearrange("p (k n) -> p k n", k=2), ACT.Copy).then_inc(tile_sem("T_copied", i), 1)
                    if name == "projf":
                        act.activation(big2[:, bass.ds(k * 512 + i * DIM, DIM)], bank[i][:, 0:DIM], ACT.Copy).then_inc(S("expert_in_kept"), 1)

            def projection(name, front):
                front(name, 0)
                with act.Fori(0, PAIRS - 1) as k:
                    copies(name, k)
                    front(name, k + 1)
                copies(name, PAIRS - 1)

            ranking("gnn")
            placing("gnn")
            projection("proj1", roots)
            first_walk()
            projection("proj2", exponentials)
            walk("gnn2")
            with act.Fori(0, PAIRS) as k:
                exponentials("fin2", k)
            placing("ffn")
            projection("projf", roots)
            done, n = bodies(act, "ffn")
            act.sem_inc(S("gelued"), EXPERTS)
            act.sem_inc(S("y_kept"), EXPERTS)

            def hidden(k, e):
                act.wait_ge(S("hidden"), k * EXPERTS + (e + 1))
                act.wait_ge(S("expert_out"), k * EXPERTS + (e + 1))
                for f in range(FCH):
                    a = act.activation(hT[e][:, f, :], bank[e][:, f * P:(f + 1) * P], ACT.Gelu,
                                       bias=b1cols[:, e * FCH + f:e * FCH + f + 1])
                a.then_inc(S("gelued"), 1)

            def keep(k, e):
                act.wait_ge(S("expert_out"), k * EXPERTS + (e + 1 + EXPERTS))
                act.activation(y_keep[e // 2][:, (e % 2) * DIM:(e % 2 + 1) * DIM], bank[4 + e][:, 0:DIM], ACT.Copy).then_inc(S("y_kept"), 1)

            def store(k, h):
                act.wait_ge(S("y_kept"), k * EXPERTS + (2 * h + 2 + EXPERTS))
                act.dma_start(y_dram[bass.ds(k, 1), :, 2 * h * DIM:(2 * h + 2) * DIM].rearrange("t p n -> (t p) n"), y_keep[h]).then_inc(S(f"y_out{h}"), 16)

            def late_half(k):
                keep(k, 2)
                keep(k, 3)
                store(k, 1)

            def tile(k, first=False):
                for e in range(EXPERTS):
                    hidden(k, e)
                probabilities(done + k, 0)
                if not first:
                    late_half(k + (-1))
                    hold(act, S("y_out0"), k * 16)
                probabilities(done + k, 1)
                keep(k, 0)
                probabilities(done + k, 2)
                keep(k, 1)
                store(k, 0)
                probabilities(done + k, 3)
                hold(act, S("y_out1"), k * 16) if not first else None
            tile(0, True)
            with act.Fori(0, TILES - 1) as k:
                tile(k + 1)
            late_half(TILES - 1)
            for h in range(2):
                act.wait_ge(S(f"y_out{h}"), 16 * TILES)
            act.sem_inc(S("experts_done"), 1)
            with act.Fori(0, n - TILES) as k:
                for s in range(STEPS):
                    probabilities(done + (k + TILES), s)
            act.wait_ge(S("gat_var"), 1)
            act.activation(tile_cols(), tile_cols(), ACT.Sqrt, bias=eps_col[:, :]).then_inc(S("gat_std"), 1)
            act.wait_ge(S("gat_top"), 1)
            act.activation(gates[:, :], gates[:, :], ACT.Exp).then_inc(S("gat_exp"), 1)

        @block.tensor
        def _(pe):
            eng_name[id(pe)] = "pe"
            pe.wait_ge(S("consts"), 1)

            def hist_edge(first):
                return pe.matmul(hist_ps, zero_b[:, :], zero_b[:, 0:TILES], start=first, stop=not first, skip_group_check=True)

            def hist_group(g, k, i):
                pe.wait_ge(S(f"list_hot_ready{i}"), list_base(g, "hot_ready") + k * 2 + 2)
                for j in range(CHUNKS):
                    m = pe.matmul(hist_ps, one_lo[i][:, j, :], one_hi[i][:, j, :], start=False, stop=False, skip_group_check=True)
                m.then_inc(S(f"list_hot_used{i}"), 1)

            def keys(g):
                pe.wait_ge(S("list_key_ready"), list_base(g, "key_ready") + 1)
                pe.transpose(bank[5][0:TILES, 0:P], key, ident[:, :]).then_inc(S("list_keyT"), 1)

            def before_placing(g):
                pe.wait_ge(S("list_maxT"), list_base(g, "maxT") + 1)
                pe.transpose(bank[5][0:TILES, 0:P], base, ident[:, :]).then_inc(S("list_maxT_ps"), 1)
                pe.wait_ge(S("list_steps_ready"), list_base(g, "steps_ready") + 1)
                pe.matmul(bank[6][:, 0:TILES + 1], steps_b[0:TILES, :], before[0:TILES, 0:TILES + 1], start=True, stop=True).then_inc(S("list_tb"), 1)

            def placing(g):
                ng = GROUPS[g]
                if g == "ffn":
                    pe.wait_ge(S("fin2_done"), 1)
                pe.wait_ge(S("list_base_ready"), list_base(g, "base_ready") + 1)
                pe.matmul(run_ps, ident[:, :], base, start=True, stop=False, skip_group_check=True).then_inc(S("list_counted"), 1)

                def pairs(k, i):
                    chunk = lo_Tb[i].rearrange("p (q j) -> p j q", j=CHUNKS)
                    pe.wait_ge(S(f"list_loT{i}"), list_base(g, "loT") + (k * 2 + 2))
                    for j in range(CHUNKS):
                        m = pe.matmul(bank[3 + 2 * i + j // 4][:, (j % 4) * P:(j % 4 + 1) * P], chunk[:, j, :], chunk[:, j, :], start=True, stop=True)
                    m.then_inc(S(f"list_same_ps{i}"), 1)

                def count(k, i):
                    lows = lo_T[i].rearrange("p (q j) -> p j q", j=CHUNKS)
                    pe.wait_ge(S(f"list_hot2_ready{i}"), list_base(g, "hot2_ready") + (k * 4 + 4))
                    for j in range(CHUNKS):
                        c = (k * 2 + i) * CHUNKS + (j + 1)
                        pe.wait_ge(S("list_copied"), list_base(g, "copied") + c)
                        pe.matmul(run_ps, one_lo[i][:, j, :], one_hi[i][:, j, :], start=False, stop=False, skip_group_check=True).then_inc(S("list_counted"), 1)
                        look = bank[1 + i][:, j * TILES:(j + 1) * TILES]
                        pe.matmul(look, lows[:, j, :], count_sb[j], start=True, stop=False, skip_group_check=True)
                        m = pe.matmul(look, same[i][:, j, :], one_hi[i][:, j, :], start=False, stop=True, skip_group_check=True)
                    m.then_inc(S(f"list_looked{i}"), 1)

                pairs(0, 0)
                with pe.Fori(0, ng // 2 - 1) as k:
                    for i in range(2):
                        count(k, i)
                        pairs(k + i, 1 - i)
                last_pair = ng // 2 - 1
                count(last_pair, 0)
                pairs(last_pair, 1)
                count(last_pair, 1)

            def walk(L):
                done, n = bodies(pe, L)
                w = width(64)

                def step(b, s):
                    pe.wait_ge(S(f"walk_rows_free{s}"), b + (phase_of[L] + 2))
                    pe.wait_ge(S("walk_added"), b * STEPS + (s + 1 + 2 * phase_of[L]))
                    for r in range(ROUNDS):
                        m = pe.matmul(bank[s % 2][:, 0:w], ident[:, :], prod[s % 2][:, r, :], start=(r == 0), stop=(r == ROUNDS - 1))
                    m.then_inc(S("walk_summed"), 1)
                if L == "gnn1":
                    hist_edge(True)
                    with pe.Fori(0, HIST_BODIES) as k:
                        for s in range(STEPS):
                            step(k, s)
                            hist_group("ffn", k * 2 + s // 2, s % 2)
                    hist_edge(False).then_inc(S("list_hist_done"), 1)
                    keys("ffn")
                    with pe.Fori(0, n - HIST_BODIES) as k:
                        for s in range(STEPS):
                            step(k + HIST_BODIES, s)
                else:
                    with pe.Fori(0, n) as k:
                        for s in range(STEPS):
                            step(done + k, s)

            def project(name, w, cols):
                def transposes(k):
                    for i in range(2):
                        pe.wait_ge(tile_sem("xn", i), tile_base(name, "xn") + (k + 1))
                        for h in range(2):
                            m = pe.transpose(bank[i][:, h * P:(h + 1) * P], xn[i][:, h * P:(h + 1) * P], ident[:, :])
                        m.then_inc(tile_sem("T", i), 1)

                def products(k):
                    for i in range(2):
                        pe.wait_ge(tile_sem("T_copied", i), tile_base(name, "T_copied") + (k + 1))
                        for h in range(2):
                            m = pe.matmul(bank[2 + i][:, 0:cols], xnT[i][:, h, :], w(h), start=(h == 0), stop=(h == 1))
                        m.then_inc(tile_sem("feat", i), 1)
                transposes(0)
                with pe.Fori(0, PAIRS - 1) as k:
                    products(k)
                    transposes(k + 1)
                    for i in range(2):
                        hold(pe, tile_sem("out_ready", i), tile_base(name, "out_ready") + (k + 1))
                products(PAIRS - 1)
                for i in range(2):
                    pe.wait_ge(tile_sem("out_ready", i), tile_base(name, "out_ready") + PAIRS)

            hist_edge(True)
            with pe.Fori(0, GROUPS["gnn"] // 2) as k:
                for i in range(2):
                    hist_group("gnn", k, i)
            hist_edge(False).then_inc(S("list_hist_done"), 1)
            keys("gnn")
            before_placing("gnn")
            placing("gnn")
            pe.wait_ge(S("constants_loaded"), 16 * 16)
            project("proj1", lambda h: wpair[:, 0, h, :], DIM)
            walk("gnn1")
            before_placing("ffn")
            project("proj2", lambda h: wpair[:, 1, h, :], DIM)
            walk("gnn2")
            placing("ffn")
            project("projf", lambda h: wgat[:, h, :], 16)
            pe.wait_ge(S("experts_in"), 32)
            pe.wait_ge(S("expert_in_kept"), TILES)
            pe.sem_inc(S("expert_out"), EXPERTS)

            def up(k, e):
                pe.wait_ge(S("gelued"), k * EXPERTS + (e + 1))
                for f in range(FCH):
                    for h in range(2):
                        m = pe.matmul(bank[e][:, f * P:(f + 1) * P], w1_sb[:, e, h, f * P:(f + 1) * P],
                                      big2[:, bass.ds(k * DIM + h * P, P)], start=(h == 0), stop=(h == 1))
                m.then_inc(S("hidden"), 1)

            def down(k, e):
                pe.wait_ge(S("gelued"), k * EXPERTS + (e + 1 + EXPERTS))
                pe.wait_ge(S("y_kept"), k * EXPERTS + (e + 1))
                y = bank[4 + e][:, 0:DIM]
                for f in range(FCH):
                    pe.matmul(y, hT[e][:, f, :], w2_sb[:, e, f, :], start=(f == 0), stop=False)
                pe.matmul(y, ones_row[:, :], b2rows[:, e, :], start=False, stop=True).then_inc(S("expert_out"), 1)

            def tile(k, first=False):
                for e in range(EXPERTS):
                    up(k, e)
                if not first:
                    for e in (2, 3):
                        down(k + (-1), e)
                for e in (0, 1):
                    down(k, e)
            tile(0, True)
            with pe.Fori(0, TILES - 1) as k:
                tile(k + 1)
            for e in (2, 3):
                down(TILES - 1, e)

        @block.vector
        def _(dve):
            eng_name[id(dve)] = "dve"
            line = Line(dve, S("dve_line"), S("spare_dve"))
            V = nc.vector
            dve.wait_ge(S("iotas"), 1)
            line(V.tensor_copy(iota_f[:, :], iota_i[:, :]))
            line(V.tensor_copy(iota_b[:, :], iota_i[:, :]))
            line(V.tensor_copy(part_f[:, :], part_i[:, :]))
            line(V.tensor_copy(nkey[:, :], nkey_i[:, :]))
            line(V.tensor_scalar(before[:, :], iota_f[:, :], part_f[:, :], None, ALU.is_gt))
            line(V.tensor_scalar(ident[:, :], iota_f[:, :], part_f[:, :], None, ALU.is_equal))
            line(V.memset(zero_b[:, :], 0.0))
            line(V.memset(eps_col[:, :], EPS))
            line(V.memset(ones_row[:, :], 1.0))
            for r, w in ((dummy_row, width(64)), (dummy_row_f, width(4))):
                line(V.memset(r[:, 0:w], 0.0))
                line(V.memset(r[:, w:w + 4], NONE))
            for g in G:
                line(V.memset(order[g][:, TILES:TILES + 2], 0))
            for i in range(2):
                line(V.memset(row[i][:, :], 1.0))
                line(V.memset(row_f[i][:, :], 1.0))
            dve.sem_inc(S("consts"), 1)

            def one_hots(g, i, k, dst_lo, dst_hi, sem):
                c = bass.ds((2 * k + i) * CHUNKS, CHUNKS)
                V.tensor_tensor(dst_lo[i], iota_b[:, :].unsqueeze(1).to_broadcast([P, CHUNKS, P]),
                                lo_b[:, c].unsqueeze(2).to_broadcast([P, CHUNKS, P]), ALU.is_equal).then_inc(sem, 1)
                V.tensor_tensor(dst_hi[i], iota_b[:, 0:TILES].unsqueeze(1).to_broadcast([P, CHUNKS, TILES]),
                                hi_b[:, c].unsqueeze(2).to_broadcast([P, CHUNKS, TILES]), ALU.is_equal).then_inc(sem, 1)

            def lists(g):
                ng = GROUPS[g]
                n = ng * CHUNKS
                last = NODES - 1
                dve.wait_ge(S("list_dst_in"), list_base(g, "dst_in") + 16)
                dve.wait_ge(S("list_src_in"), list_base(g, "src_in") + 16)
                line(V.tensor_scalar(src_i[:, 0:n], src_i[:, 0:n], float(last), None, ALU.min))
                line(V.tensor_scalar(tmp_i[:, 0:n], dst_i[:, 0:n], 127, None, ALU.bitwise_and))
                line(V.tensor_copy(lo_b[:, 0:n], tmp_i[:, 0:n]))
                dve.sem_inc(S("list_lo_ready"), 1)
                line(V.tensor_scalar(off_f[:, 0:n], dst_i[:, 0:n], float(NODES), None, ALU.is_ge))
                line(V.tensor_scalar(tmp_i[:, 0:n], dst_i[:, 0:n], 7, None, ALU.logical_shift_right))
                line(V.scalar_tensor_tensor(hi_b[:, 0:n], off_f[:, 0:n], 64.0, tmp_i[:, 0:n], ALU.mult, ALU.add))
                line(V.tensor_scalar(off_f[:, 0:n], off_f[:, 0:n], float(2 ** 18), 8192.0, ALU.mult, ALU.add))
                for i in range(2):
                    dve.sem_inc(S(f"list_hot_used{i}"), 1)

            def hist_group(g, k, i):
                dve.wait_ge(S(f"list_hot_used{i}"), list_base(g, "hot_used") + k + 1)
                one_hots(g, i, k, one_lo, one_hi, S(f"list_hot_ready{i}"))

            def keys(g):
                dve.wait_ge(S("list_hist_done"), list_base(g, "hist_done") + 1)
                line(V.tensor_copy(deg, hist_ps))
                line(V.tensor_scalar(key, deg, 2047.0, 8192.0, ALU.min, ALU.mult))
                line(V.tensor_tensor(key, key, nkey[:, :], ALU.add))
                line(V.tensor_scalar(neg_key, key, -1.0, None, ALU.mult))
                dve.sem_inc(S("list_key_ready"), 1)
                dve.wait_ge(S("list_keyT"), list_base(g, "keyT") + 1)
                line(V.tensor_copy(keyT[0:TILES, :], bank[5][0:TILES, 0:P]))
                dve.sem_inc(S("list_keyT_ready"), 1)

            def rank_tile(n, keys=slice(0, SLOTS), to=rank):
                return V.tensor_scalar(junk[:, keys], keyB[:, keys], key[:, n], None, ALU.is_gt, ALU.add, accum_out=to[:, n])

            def before_placing(g):
                dve.wait_ge(S("list_act_ranked"), list_base(g, "act_ranked") + 1)
                if g == "ffn":
                    line(V.tensor_reduce(rank[:, :], rank_parts.rearrange("p q t -> p t q"), X, ALU.add))
                signs = rank[:, 0:ACT_RANKS[g]]
                line(V.tensor_scalar(signs, signs, float(SLOTS - 1), 0.5, ALU.add, ALU.mult))
                line(V.tensor_copy(rank_i, rank[:, :]))
                line(V.tensor_scalar(tmp_i[:, 0:TILES], nkey[:, :], -1.0, float(BIG_KEY), ALU.mult, ALU.add))
                line(V.tensor_copy(node_no, tmp_i[:, 0:TILES]))
                dve.sem_inc(S("list_ranked"), 1)
                line(V.tensor_scalar(tmp_i[:, 0:TILES], rank_i, 7, None, ALU.logical_shift_right))
                line(V.tensor_copy(tile_f, tmp_i[:, 0:TILES]))
                line(V.tensor_scalar(tmp_i[:, 0:TILES], rank_i, 127, None, ALU.bitwise_and))
                line(V.tensor_copy(place_f, tmp_i[:, 0:TILES]))
                line(V.tensor_tensor(in_tile, tile_f.unsqueeze(2).to_broadcast([P, TILES, TILES]),
                                     iota_f[:, 0:TILES].unsqueeze(1).to_broadcast([P, TILES, TILES]), ALU.is_equal))
                line(V.tensor_tensor(spread, in_tile, deg.unsqueeze(2).to_broadcast([P, TILES, TILES]), ALU.mult))
                line(V.tensor_reduce(base, spread.rearrange("p n t -> p t n"), X, ALU.max))
                dve.sem_inc(S("list_maxT"), 1)
                dve.wait_ge(S("list_maxT_ps"), list_base(g, "maxT_ps") + 1)
                line(V.tensor_reduce(maxdeg[0:TILES, :], bank[5][0:TILES, 0:P], X, ALU.max))
                line(V.tensor_scalar(steps_f[0:TILES, :], maxdeg[0:TILES, :], float(ROUNDS - 1), None, ALU.add))
                line(V.tensor_copy(steps_i[0:TILES, :], steps_f[0:TILES, :]))
                line(V.tensor_scalar(steps_i[0:TILES, :], steps_i[0:TILES, :], 2, None, ALU.logical_shift_right))
                line(V.tensor_copy(steps_f[0:TILES, :], steps_i[0:TILES, :]))
                line(V.tensor_copy(steps_b[0:TILES, :], steps_f[0:TILES, :].to_broadcast([TILES, P])))
                dve.sem_inc(S("list_steps_ready"), 1)
                dve.wait_ge(S("list_tb"), list_base(g, "tb") + 1)
                line(V.tensor_copy(tb, bank[6][:, 0:TILES + 1]))
                line(V.tensor_copy(total_i, tb[:, TILES:TILES + 1]))
                line(V.tensor_scalar(tmp_i[:, 0:1], total_i, 2, None, ALU.logical_shift_right))
                least = least_bodies[g]
                line(V.tensor_scalar(counts[g][:, 0:1], tmp_i[:, 0:1], 1.0, float(least), ALU.add, ALU.max))
                line(V.tensor_scalar(tmp_i[:, 0:1], total_i, 6, None, ALU.logical_shift_right))
                line(V.tensor_scalar(counts[g][:, 1:2], tmp_i[:, 0:1], 2.0, float(least * STEPS // FILL + 2), ALU.add, ALU.max))
                dve.sem_inc(S("list_counts_ready"), 1)
                line(V.tensor_tensor(spread, in_tile, tb[:, 0:TILES].unsqueeze(1).to_broadcast([P, TILES, TILES]), ALU.mult))
                line(V.tensor_reduce(base, spread, X, ALU.add))
                line(V.tensor_scalar(base, base, float(ROUNDS), -65536.0, ALU.mult, ALU.add))
                line(V.scalar_tensor_tensor(base, place_f, 1.0 / P, base, ALU.mult, ALU.add))
                dve.sem_inc(S("list_base_ready"), 1)

            def placing(g):
                ng = GROUPS[g]
                for i in range(2):
                    dve.sem_inc(S(f"list_looked{i}"), 1)

                def first(k, i):
                    dve.wait_ge(S(f"list_looked{i}"), list_base(g, "looked") + k + 1)
                    dve.wait_ge(S(f"list_row_in{i}"), list_base(g, "row_in") + k * 16 + 16)
                    V.tensor_scalar(lo_Tb[i], lo_row[i], part_f[:, :], None, ALU.is_equal).then_inc(S(f"list_loT{i}"), 1)
                    V.tensor_scalar(lo_T[i], lo_row[i], part_f[:, :], None, ALU.is_equal).then_inc(S(f"list_loT{i}"), 1)
                    one_hots(g, i, k, one_lo, one_hi, S(f"list_hot2_ready{i}"))
                    dve.wait_ge(S(f"list_loT{i}"), list_base(g, "loT") + k * 2 + 2)
                    dve.sem_inc(S(f"list_row_used{i}"), 1)

                def second(k, i):
                    dve.wait_ge(S(f"list_same_ps{i}"), list_base(g, "same_ps") + k + 1)
                    for h in range(2):
                        V.tensor_tensor(same[i][:, 4 * h:4 * h + 4, :], bank[3 + 2 * i + h][:, :].rearrange("p (j c) -> p j c", c=P),
                                        before[:, :].unsqueeze(1).to_broadcast([P, 4, P]), ALU.mult).then_inc(S(f"list_hot2_ready{i}"), 1)

                def chosen(k, i):
                    dve.wait_ge(S(f"list_looked{i}"), list_base(g, "looked") + k + 2)
                    return line.put(V.tensor_tensor(pick.rearrange("p (j c) -> p j c", j=CHUNKS), bank[1 + i][:, 0:CHUNKS * TILES].rearrange("p (j c) -> p j c", j=CHUNKS),
                                         one_hi[i], ALU.mult))

                def place(k, i):
                    c = bass.ds((2 * k + i) * CHUNKS, CHUNKS)
                    line(V.tensor_reduce(found, pick.rearrange("p (j c) -> p j c", j=CHUNKS), X, ALU.add))
                    a = line.put(V.tensor_scalar(ints[0], found, float(P), None, ALU.mult))
                    line.need(a)
                    b = line.put(V.tensor_scalar(ints[3], ints[0], 10, None, ALU.arith_shift_right))
                    c1 = line.put(V.tensor_scalar(ints[1], ints[0], 127, 3, ALU.bitwise_and, ALU.logical_shift_left))
                    c2 = line.put(V.tensor_scalar(ints[2], ints[0], 7, 7, ALU.arith_shift_right, ALU.bitwise_and))
                    line.need(b)
                    b = line.put(V.tensor_tensor(ints[4], ints[3], off_f[:, c], ALU.add))
                    line.need(c2)
                    c1 = line.put(V.tensor_tensor(ints[1], ints[1], ints[2], ALU.bitwise_or))
                    line.need(b)
                    b = line.put(V.tensor_scalar(ints[3], ints[4], 10, None, ALU.logical_shift_left))
                    dve.wait_ge(S(f"list_slot_out{i}"), list_base(g, "slot_out") + 16 + k * (16 * CHUNKS))
                    line.put(V.tensor_tensor(src_st[i], src_i[:, c], src_i[:, c], ALU.max))
                    line.need(b)
                    line(V.tensor_tensor(slot_st[i], ints[3], ints[1], ALU.bitwise_or))
                    dve.sem_inc(S(f"list_placed{i}"), 1)

                def turn(k, i):
                    second(k + i, 1 - i)
                    picked = chosen(k, i)
                    line.need(picked)
                    dve.sem_inc(S("spare_dve"), 1)
                    first(k + 1, i)
                    place(k, i)

                for i in range(2):
                    first(0, i)
                second(0, 0)
                with dve.Fori(0, ng // 2 - 1) as k:
                    line.enter(k, 2 * 11)
                    for i in range(2):
                        turn(k, i)
                    line.leave(ng // 2 - 1)
                line.settle()
                last_pair = ng // 2 - 1
                second(last_pair, 1)
                for i in range(2):
                    line.need(chosen(last_pair, i))
                    place(last_pair, i)
                line(V.memset(step_acc, 0.0))
                line(V.tensor_scalar(step_f, iota_f[:, 0:1].to_broadcast([P, STEP_COLS]), 0.0, None, ALU.mult))
                line(V.tensor_scalar(step_f[:, 0:P], iota_f[:, :], 0.0, None, ALU.add))
                line(V.tensor_scalar(step_f[:, P:2 * P], iota_f[:, :], float(P), None, ALU.add))
                line(V.tensor_scalar(step_f[:, 2 * P:STEP_COLS], iota_f[:, 0:STEP_COLS - 2 * P], float(2 * P), None, ALU.add))
                line(V.tensor_scalar(steps_f, part_f[:, :], float(STEP_COLS), None, ALU.mult))
                line(V.tensor_scalar(step_f, step_f, steps_f, None, ALU.add))
                for n_ in range(1, TILES):
                    line(V.scalar_tensor_tensor(step_acc, step_f, tb[:, n_:n_ + 1], step_acc, ALU.is_ge, ALU.add))
                line(V.tensor_copy(step_i, step_acc))
                dve.sem_inc(S("list_step_tiles"), 1)

            def walk(L):
                nonlocal line
                c = layers[L]
                g, d, sums, rg = c["g"], c["d"], c["sums"], c["ring"]
                w = width(d)
                for s in range(STEPS):
                    dve.sem_inc(S(f"walk_rows_free{s}"), 1)
                done, n = bodies(dve, L)
                mine = Line(dve, S(L + "_line"), S("spare_dve"))
                on_pe = L != "ffn"
                if on_pe:
                    dve.sem_inc(S("walk_added"), 2)

                def body(bodies_here, beside=None):
                    tiles = {}
                    steps = len(bodies_here) * STEPS

                    def place_of(t):
                        return bodies_here[t // STEPS], t % STEPS

                    def score(t):
                        k, s = place_of(t)
                        if s % 2 == 0:
                            hold(dve, S(f"walk_tid_in{s // 2}"), (done + k) * 16 + 16 * (phase_of[L] + 1))
                            for q in range(2):
                                tiles[t + q] = dve.value_load(tid[s // 2][0:1, q:q + 1], min_val=0, max_val=TILES - 1)
                            dve.sem_inc(S(f"walk_tid_read{s // 2}"), 1)
                        hc = bass.ds(tiles[t] * HEADS, HEADS)
                        dve.wait_ge(S(f"walk_rows_in{s}"), (done + k) * (16 * ROUNDS) + 16 * ROUNDS)
                        m = mine.put(V.tensor_tensor(zbuf[:, :, :], rg[s][:, :, w:w + 4], er[:, hc].unsqueeze(1).to_broadcast([P, ROUNDS, HEADS]), ALU.add))
                        yield
                        mine.need(m)
                        m = mine.put(V.scalar_tensor_tensor(zbuf[:, :, :], zbuf[:, :, :], 0.2, zbuf[:, :, :], ALU.mult, ALU.max))
                        yield
                        mine.need(m)
                        m = mine.put(V.tensor_reduce(tmax[:, :], zbuf[:, :, :].rearrange("p r h -> p h r"), X, ALU.max))
                        yield
                        mine.need(m)
                        m = mine.put(V.tensor_tensor(tmax[:, :], tmax[:, :], top[:, hc], ALU.max))
                        yield
                        mine.need(m)
                        mine.put(V.tensor_tensor(escore[s][:, 0:ROUNDS, :], zbuf[:, :, :], tmax[:, :].unsqueeze(1).to_broadcast([P, ROUNDS, HEADS]), ALU.subtract))
                        V.tensor_tensor(escore[s][:, ROUNDS, :], top[:, hc], tmax[:, :], ALU.subtract).then_inc(S(f"walk_scores{s}"), 1)
                        yield
                        dve.wait_ge(S(f"walk_scores{s}"), done + k + 1)
                        mine.put(V.tensor_tensor(top[:, hc], tmax[:, :], tmax[:, :], ALU.max))

                    def weigh(t):
                        k, s = place_of(t)
                        dve.wait_ge(S(f"walk_probs{s}"), done + k + 1)
                        pr = prod[s % 2][:, :, 0:w].rearrange("p r (h d) -> p r h d", h=HEADS)
                        V.tensor_tensor(pr, rg[s][:, :, 0:w].rearrange("p r (h d) -> p r h d", h=HEADS),
                                        eprob[s][:, 0:ROUNDS, :].unsqueeze(3).to_broadcast([P, ROUNDS, HEADS, d + 1]), ALU.mult).then_inc(S(f"walk_rows_free{s}"), 1)

                    def total(t):
                        return sums[:, bass.ds(tiles[t] * w, w)]

                    def rescale(t):
                        tot = total(t).rearrange("p (h d) -> p h d", h=HEADS)
                        return mine.put(V.tensor_tensor(tot, tot, eprob[t % STEPS][:, ROUNDS, :].unsqueeze(2).to_broadcast([P, HEADS, d + 1]), ALU.mult))

                    def add(t):
                        k, s = place_of(t)
                        if on_pe:
                            dve.wait_ge(S("walk_summed"), (done + k) * STEPS + (s + 1))
                            part = bank[s % 2][:, 0:w]
                            V.tensor_tensor(total(t), total(t), part, ALU.add).then_inc(S("walk_added"), 1)
                            return (S("walk_added"), (done + k) * STEPS + (s + 1 + 2 * (phase_of[L] + 1)))
                        dve.wait_ge(S(f"walk_rows_free{s}"), done + k + (phase_of[L] + 2))
                        m = mine.put(V.tensor_reduce(part_sum[:, 0:w], prod[s % 2][:, :, 0:w].rearrange("p r w -> p w r"), X, ALU.add))
                        mine.need(m)
                        m = mine.put(V.tensor_tensor(total(t), total(t), part_sum[:, 0:w], ALU.add))
                        mine.need(m)
                        return None

                    for _ in score(0):
                        pass
                    scaled = None
                    for t in range(steps):
                        nxt = score(t + 1) if t + 1 < steps else iter(())
                        if beside is not None and t:
                            beside(*place_of(t - 1))
                        next(nxt, None)
                        weigh(t)
                        next(nxt, None)
                        if t and on_pe:
                            mine.need(scaled)
                            sem, value = add(t - 1)
                            next(nxt, None)
                            dve.wait_ge(sem, value)
                        else:
                            next(nxt, None)
                        scaled = rescale(t)
                        for _ in nxt:
                            pass
                        if not on_pe:
                            mine.need(scaled)
                            add(t)
                    if beside is not None:
                        beside(*place_of(steps - 1))
                    if on_pe:
                        mine.need(scaled)
                        sem, value = add(steps - 1)
                        hold(dve, sem, value)

                per = (7 if on_pe else 9) * STEPS
                at = 0
                if L == "gnn1":
                    with dve.Fori(0, HIST_BODIES // TURN) as k:
                        mine.enter(k, TURN * per)
                        body([TURN * k + b for b in range(TURN)], lambda b, s: hist_group("ffn", b * 2 + s // 2, s % 2))
                        mine.leave(HIST_BODIES // TURN)
                    keys("ffn")
                    at = HIST_BODIES
                    with dve.Fori(0, KEY_BODIES) as k:
                        mine.enter(k, per)
                        body([k + at])
                        mine.leave(KEY_BODIES)
                    at += KEY_BODIES
                    dve.wait_ge(S("list_keyB_in"), list_base("ffn", "keyB_in") + 16)
                    with dve.Fori(0, DVE_RANK_BODIES // TURN) as k:
                        mine.enter(k, TURN * (per + STEPS))
                        body([TURN * k + (at + b) for b in range(TURN)],
                             lambda b, s: mine.put(rank_tile(bass.ds(b + (ACT_RANKS["ffn"] - at), 1), slice(s * SLOTS // STEPS, (s + 1) * SLOTS // STEPS),
                                                             rank_parts[:, s, :])))
                        mine.leave(DVE_RANK_BODIES // TURN)
                    at += DVE_RANK_BODIES
                with dve.Fori(0, n - at if at else n) as k:
                    mine.enter(k, per)
                    body([k + at if at else k])
                    mine.leave(None)

            def index(name, g, k, i):
                hold(dve, tile_sem("out", i), tile_base(name, "out") + k * 16)
                line.hold(V.tensor_copy(gi[i][:, :], order[g][:, bass.ds(2 * k + i, 1)]))
                dve.sem_inc(tile_sem("index", i), 1)

            def by_turns(parts):
                while parts:
                    parts = [p for p in parts if next(p, StopIteration) is not StopIteration]

            def index_in(name, g, k, i, first=False):
                c = slice(i, i + 1) if first else bass.ds(2 * k + (2 + i), 1)
                V.tensor_copy(gi_in[i][:, :], order[g][:, c]).then_inc(tile_sem("index_in", i), 1)

            def norm(name, g, k, i):
                dve.wait_ge(tile_sem("x_in", i), tile_base(name, "x_in") + k * 16 + 16)
                m = line.put(V.bn_stats(stats[i][:, :], xt[i]))
                yield True
                line.need(m)
                dve.sem_inc(S("spare_dve"), 1)
                V.bn_aggr(mv[i][:, :], stats[i][:, :]).then_inc(tile_sem("var", i), 1)
                index_in(name, g, k, i)
                if name == "projf":
                    line.put(V.tensor_tensor(big1[:, bass.ds((2 * k + i) * DIM, DIM)], xt[i], xt[i], ALU.max))
                yield True
                dve.wait_ge(tile_sem("std", i), tile_base(name, "std") + k + 1)
                m = line.put(V.reciprocal(rstd[i][:, 1:2], rstd[i][:, 0:1]))
                yield True
                if not isinstance(k, int):
                    dve.wait_ge(tile_sem("T", i), tile_base(name, "T") + k)
                line.need(m)
                V.tensor_scalar(xn[i], xt[i], mv[i][:, 0:1], rstd[i][:, 1:2], ALU.subtract, ALU.mult).then_inc(tile_sem("xn", i), 1)
                yield True
                dve.wait_ge(tile_sem("xn", i), tile_base(name, "xn") + k + 1)
                dve.sem_inc(tile_sem("x_free", i), 1)

            def rows(name, L, k, i):
                c = layers[L]
                d = c["d"]
                w = width(d)
                n = HEADS * d
                r = c["row"][i]
                hc = bass.ds((2 * k + i) * HEADS, HEADS)
                f = bank[2 + i][:, 0:n]
                dve.wait_ge(tile_sem("feat", i), tile_base(name, "feat") + k + 1)
                a = line.put(V.tensor_tensor(tmp[i][:, 0:n], f, c["al"], ALU.mult))
                b = line.put(V.tensor_tensor(rtmp[i][:, 0:n], f, c["ar"], ALU.mult))
                yield True
                index(name, c["g"], k, i)
                line.need(a)
                line.put(V.tensor_reduce(r[:, w:w + 4], tmp[i][:, 0:n].rearrange("p (h d) -> p h d", h=HEADS), X, ALU.add))
                yield True
                line.need(b)
                e = line.put(V.tensor_reduce(er_new[i][:, :], rtmp[i][:, 0:n].rearrange("p (h d) -> p h d", h=HEADS), X, ALU.add))
                V.tensor_copy(r[:, 0:w].rearrange("p (h d) -> p h d", h=HEADS)[:, :, 0:d], f.rearrange("p (h d) -> p h d", h=HEADS)).then_inc(tile_sem("out_ready", i), 1)
                yield True
                line.need(e)
                line.put(V.tensor_tensor(er[:, hc], er_new[i][:, :], er_new[i][:, :], ALU.max))
                if name == "projf":
                    m = line.put(V.tensor_tensor(zbuf[:, i, :], r[:, w:w + 4], er_new[i][:, :], ALU.add))
                    yield True
                    line.need(m)
                    line.put(V.scalar_tensor_tensor(top[:, hc], zbuf[:, i, :], 0.2, zbuf[:, i, :], ALU.mult, ALU.max))
                    dve.wait_ge(tile_sem("out_ready", i), tile_base(name, "out_ready") + k + 1)
                    line.put(V.tensor_tensor(sums_f[:, bass.ds((2 * k + i) * w, w)], r[:, 0:w], r[:, 0:w], ALU.max))

            def later(turns, part):
                for _ in range(turns):
                    yield True
                yield from part

            def projection(name, L, front, per, turns):
                by_turns([front(0, i) for i in range(2)])
                with dve.Fori(0, PAIRS - 1) as k:
                    line.enter(k, per)
                    by_turns([later(turns, rows(name, L, k, i)) for i in range(2)] + [front(k + 1, i) for i in range(2)])
                    line.leave(PAIRS - 1)
                line.settle()
                by_turns([rows(name, L, PAIRS - 1, i) for i in range(2)])
                line.settle()

            def aggregate(name, k, i, bias, residual):
                w = width(64)
                sv = big1[:, bass.ds((2 * k + i) * w, w)].rearrange("p (h d) -> p h d", h=HEADS)
                hd = xn[i].rearrange("p (h d) -> p h d", h=HEADS)
                m = line.put(V.scalar_tensor_tensor(rstd[i][:, :].unsqueeze(2), sv[:, :, 64:65], 0.0, sv[:, :, 64:65], ALU.is_le, ALU.add))
                yield True
                line.need(m)
                m = line.put(V.reciprocal(rstd[i][:, :], rstd[i][:, :]))
                yield True
                line.need(m)
                if not residual and not isinstance(k, int):
                    dve.wait_ge(tile_sem("T", i), tile_base(name, "T") + k)
                m = line.put(V.tensor_tensor(hd, sv[:, :, 0:64], rstd[i][:, :].unsqueeze(2).to_broadcast([P, HEADS, 64]), ALU.mult))
                yield True
                if residual:
                    line.need(m)
                    m = line.put(V.tensor_tensor(xn[i], xn[i], big2[:, bass.ds((2 * k + i) * DIM, DIM)], ALU.add))
                    yield True
                line.need(m)
                m = line.put(V.tensor_tensor(xn[i], xn[i], bias, ALU.add))
                yield True
                line.need(m)
                V.tensor_scalar(tmp2[i], xn[i], 0.0, None, ALU.min).then_inc(tile_sem("neg", i), 1)
                yield True
                dve.wait_ge(tile_sem("neg", i), tile_base(name, "neg") + k + 1)
                m = line.put(V.tensor_scalar(xn[i], xn[i], 0.0, None, ALU.max))
                yield True
                line.need(m)
                dve.wait_ge(tile_sem("exp", i), tile_base(name, "exp") + k + 1)
                a = V.scalar_tensor_tensor(xn[i], tmp2[i], -1.0, xn[i], ALU.add, ALU.add)
                if not residual:
                    a.then_inc(tile_sem("xn", i), 1)
                    yield True
                    dve.wait_ge(tile_sem("xn", i), tile_base(name, "xn") + k + 1)
                    line.put(V.tensor_tensor(big2[:, bass.ds((2 * k + i) * DIM, DIM)], xn[i], xn[i], ALU.max))
                else:
                    m = line.put(a)
                    yield True
                    line.need(m)
                    index(name, "gnn", k, i)
                    yield True
                    dve.wait_ge(tile_sem("x_in", i), tile_base(name, "x_in") + k * 16 + 16)
                    V.tensor_tensor(tmp[i], xt[i], xn[i], ALU.add).then_inc(tile_sem("out_ready", i), 1)

            def first_gather(name, g):
                for i in range(2):
                    index_in(name, g, None, i, True)

            def last_gather(name):
                for i in range(2):
                    dve.wait_ge(tile_sem("x_in", i), tile_base(name, "x_in") + 16 * PAIRS + 16)

            lists("gnn")
            with dve.Fori(0, GROUPS["gnn"] // 2) as k:
                for i in range(2):
                    hist_group("gnn", k, i)
            keys("gnn")
            dve.wait_ge(S("list_keyB_in"), list_base("gnn", "keyB_in") + 16)
            for n in range(ACT_RANKS["gnn"], TILES):
                line(rank_tile(slice(n, n + 1)))
            before_placing("gnn")
            placing("gnn")
            dve.wait_ge(S("constants_loaded"), 16 * 16)
            dve.wait_ge(S("sums_clear"), 1)
            dve.wait_ge(S("list_order_in"), list_base("gnn", "order_in") + 16)
            first_gather("proj1", "gnn")
            projection("proj1", "gnn1", lambda k, i: norm("proj1", "gnn", k, i), 2 * 8, 2)
            last_gather("proj1")
            line(V.memset(top[:, :], NONE))
            lists("ffn")
            line(V.memset(rank_parts, 0.0))
            walk("gnn1")
            dve.sem_inc(S("gnn1_walked"), 1)
            before_placing("ffn")
            projection("proj2", "gnn2", lambda k, i: aggregate("proj2", k, i, vecs[:, 2, :], False), 2 * 12, 6)
            line(V.memset(big1[:, :], 0.0))
            line(V.memset(top[:, :], NONE))
            walk("gnn2")
            first_gather("fin2", "gnn")
            with dve.Fori(0, PAIRS) as k:
                line.enter(k, 2 * 8)
                by_turns([aggregate("fin2", k, i, vecs[:, 5, :], True) for i in range(2)])
                for i in range(2):
                    dve.wait_ge(tile_sem("out_ready", i), tile_base("fin2", "out_ready") + k + 1)
                    dve.sem_inc(tile_sem("x_free", i), 1)
                    index_in("fin2", "gnn", k, i)
                line.leave(PAIRS)
            line.settle()
            last_gather("fin2")
            for i in range(2):
                dve.wait_ge(tile_sem("out", i), tile_base("fin2", "out") + 16 * PAIRS)
            dve.sem_inc(S("fin2_done"), 1)
            placing("ffn")
            dve.wait_ge(S("list_order_in"), list_base("ffn", "order_in") + 16)
            first_gather("projf", "ffn")
            projection("projf", "ffn", lambda k, i: norm("projf", "ffn", k, i), 2 * 12, 2)
            last_gather("projf")
            walk("ffn")
            sf = sums_f[:, :].rearrange("p (t h d) -> p t h d", t=TILES, h=HEADS)
            n16 = TILES * 16
            reg = ring_all[:, 0:SLOTS // 2]
            agg = reg[:, 0:n16]
            agg4 = agg.rearrange("p (t h e) -> p t h e", t=TILES, h=HEADS)
            agg3 = agg.rearrange("p (t c) -> p t c", t=TILES)
            sq = reg[:, n16:2 * n16]
            sq3 = sq.rearrange("p (t c) -> p t c", t=TILES)
            den = reg[:, 2 * n16:2 * n16 + TILES * HEADS].rearrange("p (t h) -> p t h", t=TILES)
            mean = reg[:, 2 * n16 + 200:2 * n16 + 250]
            std = tile_cols()
            sc = reg[:, 2 * n16 + 256:2 * n16 + 456]
            sc3 = sc.rearrange("p (t e) -> p t e", t=TILES)
            cmp_ = reg[:, n16:2 * n16].rearrange("p (t e j) -> p t e j", t=TILES, e=EXPERTS)
            g3 = gates[:, :].rearrange("p (t e) -> p t e", t=TILES)

            def cols(v):
                return v.unsqueeze(2).to_broadcast([P, TILES, 16])
            line(V.tensor_scalar(den.unsqueeze(3), sf[:, :, :, 4:5], 1e-16, None, ALU.add))
            line(V.reciprocal(den, den))
            for h in range(HEADS):
                line(V.tensor_tensor(agg4[:, :, h, :], sf[:, :, h, 0:4], den[:, :, h:h + 1].to_broadcast([P, TILES, 4]), ALU.mult))
            line(V.tensor_tensor(agg3, agg3, small[:, 2, :].unsqueeze(1).to_broadcast([P, TILES, 16]), ALU.add))
            line(V.tensor_reduce(mean, agg3, X, ALU.add))
            line(V.tensor_scalar(mean, mean, 1.0 / 16, None, ALU.mult))
            line(V.tensor_tensor(agg3, agg3, cols(mean), ALU.subtract))
            line(V.tensor_tensor(sq, agg, agg, ALU.mult))
            line(V.tensor_reduce(std, sq3, X, ALU.add))
            line(V.tensor_scalar(std, std, 1.0 / 16, None, ALU.mult))
            dve.sem_inc(S("gat_var"), 1)
            dve.wait_ge(S("gat_std"), 1)
            line(V.reciprocal(std, std))
            line(V.tensor_tensor(agg3, agg3, cols(std), ALU.mult))
            line(V.tensor_tensor(agg3, agg3, small[:, 3, :].unsqueeze(1).to_broadcast([P, TILES, 16]), ALU.mult))
            line(V.tensor_tensor(agg3, agg3, small[:, 4, :].unsqueeze(1).to_broadcast([P, TILES, 16]), ALU.add))
            line(V.tensor_reduce(sc3, agg4.rearrange("p t h e -> p t e h"), X, ALU.add))
            line(V.tensor_scalar(sc, sc, 0.25, None, ALU.mult))
            take = reg[:, 2 * n16 + 456:2 * n16 + 656].rearrange("p (t e) -> p t e", t=TILES)
            eq = reg[:, 0:n16].rearrange("p (t e j) -> p t e j", t=TILES, e=EXPERTS)
            for e in range(EXPERTS):
                line(V.tensor_tensor(cmp_[:, :, e, :], sc3, sc3[:, :, e:e + 1].to_broadcast([P, TILES, EXPERTS]), ALU.is_gt))
                if e:
                    line(V.tensor_tensor(eq[:, :, e, 0:e], sc3[:, :, 0:e], sc3[:, :, e:e + 1].to_broadcast([P, TILES, e]), ALU.is_equal))
                    line(V.tensor_tensor(cmp_[:, :, e, 0:e], cmp_[:, :, e, 0:e], eq[:, :, e, 0:e], ALU.add))
            line(V.tensor_reduce(take, cmp_, X, ALU.add))
            line(V.tensor_scalar(take, take, 2.0, None, ALU.is_lt))
            line(V.tensor_reduce(mean, sc3, X, ALU.max))
            line(V.tensor_tensor(g3, sc3, mean.unsqueeze(2).to_broadcast([P, TILES, EXPERTS]), ALU.subtract))
            dve.sem_inc(S("gat_top"), 1)
            dve.wait_ge(S("gat_exp"), 1)
            line(V.tensor_tensor(g3, g3, take, ALU.mult))
            line(V.tensor_reduce(mean, g3, X, ALU.add))
            line(V.reciprocal(mean, mean))
            line(V.tensor_tensor(g3, g3, mean.unsqueeze(2).to_broadcast([P, TILES, EXPERTS]), ALU.mult))
            def mixed(k, q, pair, i):
                j = 2 * q + i
                dve.wait_ge(S(f"y_in{j}"), k * 16 + 16)
                for e in range(EXPERTS):
                    gate = gates[:, bass.ds((2 * pair + i) * EXPERTS + e, 1)]
                    prev = big1[:, bass.ds((2 * pair + i) * DIM, DIM)] if e == 0 else yacc[i]
                    part = y_back[j][:, e * DIM:(e + 1) * DIM]
                    if e < EXPERTS - 1:
                        m = line.put(V.scalar_tensor_tensor(yacc[i], part, gate, prev, ALU.mult, ALU.add))
                        yield
                        line.need(m)
                    else:
                        index("mix", "ffn", pair, i)
                        yield
                        V.scalar_tensor_tensor(yout[i], part, gate, prev, ALU.mult, ALU.add).then_inc(tile_sem("out_ready", i), 1)
                dve.wait_ge(tile_sem("out_ready", i), tile_base("mix", "out_ready") + pair + 1)
                dve.sem_inc(S(f"y_used{j}"), 1)
            with dve.Fori(0, TILES // 4) as k:
                line.enter(k, 2 * 2 * EXPERTS)
                for q in range(2):
                    by_turns([mixed(k, q, 2 * k + q, i) for i in range(2)])
                line.leave(TILES // 4)
            line.settle()
            by_turns([mixed(TILES // 4, 0, PAIRS - 1, i) for i in range(2)])


NAMES = ["x", "gnn_src", "gnn_dst", "ffn_src", "ffn_dst", "L0_gnn_W1", "L0_gnn_al1", "L0_gnn_ar1", "L0_gnn_b1",
         "L0_gnn_W2", "L0_gnn_al2", "L0_gnn_ar2", "L0_gnn_b2", "L0_ffn_W_gat", "L0_ffn_att_src", "L0_ffn_att_dst",
         "L0_ffn_b_gat", "L0_ffn_ln_gamma", "L0_ffn_ln_beta", "L0_ffn_W1", "L0_ffn_b1", "L0_ffn_W2", "L0_ffn_b2"]


def kernel(**inputs):
    import numpy as np
    import concourse.bacc as bacc
    from concourse import mybir as mb
    from concourse.bass_utils import run_bass_kernel_spmd

    def padded(a, n, fill):
        a = np.asarray(a)
        return np.concatenate([a, np.full((n - a.shape[0],) + a.shape[1:], fill, a.dtype)])

    a = {k: np.asarray(v) for k, v in inputs.items()}
    edges = a.pop("L0_ffn_edge_index")
    a["x"] = padded(a["x"], SLOTS, 0)
    a["gnn_src"] = padded(a.pop("src"), GROUPS["gnn"] * GROUP, 0)
    a["gnn_dst"] = padded(a.pop("dst"), GROUPS["gnn"] * GROUP, BIG_KEY)
    a["ffn_src"], a["ffn_dst"] = edges[0], edges[1]
    for n in ("L0_gnn_al1", "L0_gnn_ar1", "L0_gnn_al2", "L0_gnn_ar2", "L0_ffn_att_src", "L0_ffn_att_dst"):
        a[n] = a[n].reshape(-1)

    nc = bacc.Bacc("TRN2", target_bir_lowering=False, num_devices=1)
    arrays, aps = {}, {}
    for n in NAMES:
        v = np.ascontiguousarray(a[n])
        arrays[f"in_{n}"] = v
        aps[n] = nc.dram_tensor(f"in_{n}", v.shape, mb.dt.from_np(v.dtype), kind="ExternalInput").ap()
    out = nc.dram_tensor("result", (NODES, DIM), mb.dt.float32, kind="ExternalOutput").ap()
    build(nc, aps, out)
    r = run_bass_kernel_spmd(nc, [arrays], core_ids=[0])
    return r.results[0]["result"]
```
